# Optimizing a Trainium2 kernel written in Bass

```python
import numpy as np
import jax
import jax.numpy as jnp

def _softmax(x, axis=-1):
    return jax.nn.softmax(x, axis=axis)

def _gelu(x):
    return jax.nn.gelu(x, approximate=True)

def _silu(x):
    return jax.nn.silu(x)

def _sigmoid(x):
    return jax.nn.sigmoid(x)

def _layernorm(x, axis=-1, eps=1e-05):
    m = jnp.mean(x, axis=axis, keepdims=True)
    v = jnp.var(x, axis=axis, keepdims=True)
    return (x - m) / jnp.sqrt(v + eps)

def _scatter_add(tgt, idx, src, axis=0):
    return tgt.at[idx].add(src)

def _segment_sum(src, seg, n):
    return jax.ops.segment_sum(src, seg, n)
kernel_name = 'mk_hybrid_d1_jaxref_r8_c690c8'

def setup_inputs(seed: int=0):
    np.random.seed(seed)
    _w = jnp.asarray

    def _L0_attn_a_setup():
        import jax, jax.numpy as jnp
        import numpy as np
        D = 256
        H = 16
        HD = D // H
        key = jax.random.key(seed)
        k1, k2, k3 = jax.random.split(key, 3)
        x = jax.random.normal(k1, (2, 256, D), dtype=jnp.float32)
        Wqkv = jax.random.normal(k2, (D, 3 * D), dtype=jnp.float32) * D ** (-0.5)
        Wo = jax.random.normal(k3, (D, D), dtype=jnp.float32) * D ** (-0.5)
        return {'x': x, 'Wqkv': Wqkv, 'Wo': Wo}
    _L0_attn_a_in = _L0_attn_a_setup()

    def _L0_attn_b_setup():
        import jax, jax.numpy as jnp
        import numpy as np
        B, S, H = (2, 256, 256)
        NH = 16
        Q_LORA, KV_LORA = (192, 64)
        D_K, D_R, D_V = (128, 64, 128)
        IH, ID, TOPK = (8, 128, 8)

        def _rope_tables(dim, end, base=10000.0):
            inv = 1.0 / base ** (np.arange(0, dim, 2)[:dim // 2].astype(np.float32) / dim)
            freqs = np.outer(np.arange(end, dtype=np.float32), inv)
            return (jnp.asarray(np.cos(freqs)), jnp.asarray(np.sin(freqs)))

        def _apply_rope(x, cos, sin):
            xr, xi = (x[..., 0::2], x[..., 1::2])
            c, s_ = (cos[None, None], sin[None, None])
            out_r = xr * c - xi * s_
            out_i = xr * s_ + xi * c
            return jnp.stack([out_r, out_i], axis=-1).reshape(x.shape)
        key = jax.random.key(seed)
        ks = jax.random.split(key, 16)
        std = 0.02

        def w(k, shape):
            return jax.random.normal(k, shape, dtype=jnp.float32) * std
        return {'x': jax.random.normal(ks[0], (B, S, H), dtype=jnp.float32), 'W_c': w(ks[1], (H, KV_LORA)), 'W_cp': w(ks[2], (H, Q_LORA)), 'W_qc': w(ks[3], (Q_LORA, NH * D_K)), 'W_qr': w(ks[4], (Q_LORA, NH * D_R)), 'W_kc': w(ks[5], (KV_LORA, NH * D_K)), 'W_kr': w(ks[6], (H, D_R)), 'W_v': w(ks[7], (KV_LORA, NH * D_V)), 'W_o': w(ks[8], (NH * D_V, H)), 'W_idx': w(ks[9], (H, IH * ID)), 'W_gate': w(ks[10], (H, IH)), 'W_sq': w(ks[11], (ID, ID)), 'W_sk': w(ks[12], (ID, ID)), 'W_sv': w(ks[13], (ID, ID)), 'W_iout': w(ks[14], (ID, H))}
    _L0_attn_b_in = _L0_attn_b_setup()

    def _L0_ffn_setup():
        import jax, jax.numpy as jnp
        import numpy as np
        EPS = 1e-06
        Q_B = 128.0

        def layer_norm(x):
            mean = jnp.mean(x, axis=-1, keepdims=True)
            var = jnp.var(x, axis=-1, keepdims=True)
            return (x - mean) / jnp.sqrt(var + EPS)

        def absmax_quant(x):
            gamma = jnp.max(jnp.abs(x), axis=-1, keepdims=True)
            x_hat = jnp.clip(x * Q_B / gamma, -Q_B + EPS, Q_B - EPS)
            return x_hat * gamma / Q_B

        def ternarize_weights(w):
            gamma = jnp.mean(jnp.abs(w))
            return jnp.sign(jnp.round(w / (gamma + EPS))) * gamma

        def bitlinear(x, w):
            xn = layer_norm(x)
            x_hat = xn + jax.lax.stop_gradient(absmax_quant(xn) - xn)
            w_hat = w + jax.lax.stop_gradient(ternarize_weights(w) - w)
            return jnp.einsum('bsd,od->bso', x_hat, w_hat)
        key = jax.random.key(seed)
        k1, k2, k3 = jax.random.split(key, 3)
        B, S, D = (4, 256, 256)
        x = jax.random.normal(k1, (B, S, D), dtype=jnp.float32)
        w_fc = jax.random.normal(k2, (4 * D, D), dtype=jnp.float32) / np.sqrt(D)
        w_proj = jax.random.normal(k3, (D, 4 * D), dtype=jnp.float32) / np.sqrt(4 * D)
        return {'x': x, 'w_fc': w_fc, 'w_proj': w_proj}
    _L0_ffn_in = _L0_ffn_setup()
    _d = {'L0_attn_a_x': _L0_attn_a_in['x'], 'L0_attn_a_Wqkv': _L0_attn_a_in['Wqkv'], 'L0_attn_a_Wo': _L0_attn_a_in['Wo'], 'L0_attn_b_W_c': _L0_attn_b_in['W_c'], 'L0_attn_b_W_cp': _L0_attn_b_in['W_cp'], 'L0_attn_b_W_qc': _L0_attn_b_in['W_qc'], 'L0_attn_b_W_qr': _L0_attn_b_in['W_qr'], 'L0_attn_b_W_kc': _L0_attn_b_in['W_kc'], 'L0_attn_b_W_kr': _L0_attn_b_in['W_kr'], 'L0_attn_b_W_v': _L0_attn_b_in['W_v'], 'L0_attn_b_W_o': _L0_attn_b_in['W_o'], 'L0_attn_b_W_idx': _L0_attn_b_in['W_idx'], 'L0_attn_b_W_gate': _L0_attn_b_in['W_gate'], 'L0_attn_b_W_sq': _L0_attn_b_in['W_sq'], 'L0_attn_b_W_sk': _L0_attn_b_in['W_sk'], 'L0_attn_b_W_sv': _L0_attn_b_in['W_sv'], 'L0_attn_b_W_iout': _L0_attn_b_in['W_iout'], 'L0_ffn_w_fc': _L0_ffn_in['w_fc'], 'L0_ffn_w_proj': _L0_ffn_in['w_proj']}
    _x0 = _d['L0_attn_a_x']
    _d['L0_attn_a_x'] = jax.random.normal(jax.random.fold_in(jax.random.key(seed), 1), (1, 1024, 256), dtype=_x0.dtype)
    del _x0
    return _d

def reference(L0_attn_a_x, L0_attn_a_Wqkv, L0_attn_a_Wo, L0_attn_b_W_c, L0_attn_b_W_cp, L0_attn_b_W_qc, L0_attn_b_W_qr, L0_attn_b_W_kc, L0_attn_b_W_kr, L0_attn_b_W_v, L0_attn_b_W_o, L0_attn_b_W_idx, L0_attn_b_W_gate, L0_attn_b_W_sq, L0_attn_b_W_sk, L0_attn_b_W_sv, L0_attn_b_W_iout, L0_ffn_w_fc, L0_ffn_w_proj):

    def _L0_attn_a_ref(x, Wqkv, Wo):
        import jax, jax.numpy as jnp
        import numpy as np
        D = 256
        H = 16
        HD = D // H
        B, S, _ = x.shape
        qkv = (x @ Wqkv).reshape(B, S, 3, H, HD)
        q = qkv[:, :, 0].transpose(0, 2, 1, 3)
        k = qkv[:, :, 1].transpose(0, 2, 1, 3)
        v = qkv[:, :, 2].transpose(0, 2, 1, 3)
        scores = jnp.einsum('bhqd,bhkd->bhqk', q, k) * HD ** (-0.5)
        causal = jnp.tril(jnp.ones((S, S), dtype=bool))
        scores = jnp.where(causal, scores, jnp.float32(-1000000000.0))
        a = jax.nn.softmax(scores, axis=-1)
        o = jnp.einsum('bhqk,bhkd->bhqd', a, v)
        o = o.transpose(0, 2, 1, 3).reshape(B, S, H * HD)
        return o @ Wo

    def _L0_attn_b_ref(x, W_c, W_cp, W_qc, W_qr, W_kc, W_kr, W_v, W_o, W_idx, W_gate, W_sq, W_sk, W_sv, W_iout):
        import jax, jax.numpy as jnp
        import numpy as np
        B, S, H = (2, 256, 256)
        NH = 16
        Q_LORA, KV_LORA = (192, 64)
        D_K, D_R, D_V = (128, 64, 128)
        IH, ID, TOPK = (8, 128, 8)

        def _rope_tables(dim, end, base=10000.0):
            inv = 1.0 / base ** (np.arange(0, dim, 2)[:dim // 2].astype(np.float32) / dim)
            freqs = np.outer(np.arange(end, dtype=np.float32), inv)
            return (jnp.asarray(np.cos(freqs)), jnp.asarray(np.sin(freqs)))

        def _apply_rope(x, cos, sin):
            xr, xi = (x[..., 0::2], x[..., 1::2])
            c, s_ = (cos[None, None], sin[None, None])
            out_r = xr * c - xi * s_
            out_i = xr * s_ + xi * c
            return jnp.stack([out_r, out_i], axis=-1).reshape(x.shape)
        b, s, _ = x.shape
        cos, sin = _rope_tables(D_R, s)
        c = x @ W_c
        cp = x @ W_cp
        q_c = (cp @ W_qc).reshape(b, s, NH, D_K).transpose(0, 2, 1, 3)
        k_c = (c @ W_kc).reshape(b, s, NH, D_K).transpose(0, 2, 1, 3)
        q_r = (cp @ W_qr).reshape(b, s, NH, D_R).transpose(0, 2, 1, 3)
        k_r = jnp.broadcast_to((x @ W_kr)[:, None], (b, NH, s, D_R))
        v = (c @ W_v).reshape(b, s, NH, D_V).transpose(0, 2, 1, 3)
        q_r = _apply_rope(q_r, cos, sin)
        k_r = _apply_rope(k_r, cos, sin)
        q = jnp.concatenate([q_c, q_r], axis=-1)
        k = jnp.concatenate([k_c, k_r], axis=-1)
        scale = 1.0 / np.sqrt(D_K + D_R)
        scores = jnp.einsum('bhqd,bhkd->bhqk', q, k) * scale
        causal = jnp.triu(jnp.ones((s, s), dtype=bool), 1)
        scores = jnp.where(causal[None, None], -jnp.inf, scores)
        probs = jax.nn.softmax(scores.astype(jnp.float32), axis=-1).astype(q.dtype)
        attn = jnp.einsum('bhqk,bhkd->bhqd', probs, v)
        idx_states = (x @ W_idx).reshape(b, s, IH, ID)
        gate = x @ W_gate
        _, top_idx = jax.lax.top_k(gate.transpose(0, 2, 1), TOPK)
        ish = idx_states.transpose(0, 2, 1, 3)
        sel = jnp.take_along_axis(ish, top_idx[..., None], axis=2)
        sq, sk, sv = (sel @ W_sq, sel @ W_sk, sel @ W_sv)
        sprobs = jax.nn.softmax(jnp.einsum('bhqd,bhkd->bhqk', sq, sk) / np.sqrt(ID), axis=-1)
        sout = jnp.einsum('bhqk,bhkd->bhqd', sprobs, sv)
        sparse_out = sout.reshape(b, IH * TOPK, ID) @ W_iout
        io = sparse_out.reshape(b, IH, TOPK, H).mean(axis=2)
        io = jnp.broadcast_to(io[:, :, None, :D_V], (b, IH, s, D_V))
        io = jnp.repeat(io, NH // IH, axis=1)
        attn = attn + io
        out = attn.transpose(0, 2, 1, 3).reshape(b, s, NH * D_V) @ W_o
        return out

    def _L0_ffn_ref(x, w_fc, w_proj):
        import jax, jax.numpy as jnp
        import numpy as np
        EPS = 1e-06
        Q_B = 128.0

        def layer_norm(x):
            mean = jnp.mean(x, axis=-1, keepdims=True)
            var = jnp.var(x, axis=-1, keepdims=True)
            return (x - mean) / jnp.sqrt(var + EPS)

        def absmax_quant(x):
            gamma = jnp.max(jnp.abs(x), axis=-1, keepdims=True)
            x_hat = jnp.clip(x * Q_B / gamma, -Q_B + EPS, Q_B - EPS)
            return x_hat * gamma / Q_B

        def ternarize_weights(w):
            gamma = jnp.mean(jnp.abs(w))
            return jnp.sign(jnp.round(w / (gamma + EPS))) * gamma

        def bitlinear(x, w):
            xn = layer_norm(x)
            x_hat = xn + jax.lax.stop_gradient(absmax_quant(xn) - xn)
            w_hat = w + jax.lax.stop_gradient(ternarize_weights(w) - w)
            return jnp.einsum('bsd,od->bso', x_hat, w_hat)
        h = bitlinear(x, w_fc)
        h = jax.nn.gelu(h, approximate=False)
        return bitlinear(h, w_proj)
    x = L0_attn_a_x
    x = x + _L0_attn_a_ref(_layernorm(x, axis=-1), L0_attn_a_Wqkv, L0_attn_a_Wo)
    x = x + _L0_ffn_ref(_layernorm(x, axis=-1), L0_ffn_w_fc, L0_ffn_w_proj)
    x = x + _L0_attn_b_ref(_layernorm(x, axis=-1), L0_attn_b_W_c, L0_attn_b_W_cp, L0_attn_b_W_qc, L0_attn_b_W_qr, L0_attn_b_W_kc, L0_attn_b_W_kr, L0_attn_b_W_v, L0_attn_b_W_o, L0_attn_b_W_idx, L0_attn_b_W_gate, L0_attn_b_W_sq, L0_attn_b_W_sk, L0_attn_b_W_sv, L0_attn_b_W_iout)
    x = x + _L0_ffn_ref(_layernorm(x, axis=-1), L0_ffn_w_fc, L0_ffn_w_proj)
    return x

_drawn_inputs = setup_inputs


def setup_inputs(seed=0):
    import zlib

    import numpy as np

    out = dict(_drawn_inputs(seed))
    spreads = {}
    factors = {'L0_attn_b_W_c': 8.0,
     'L0_attn_b_W_cp': 8.0,
     'L0_attn_b_W_qc': 8.0,
     'L0_attn_b_W_qr': 8.0,
     'L0_attn_b_W_kc': 8.0,
     'L0_attn_b_W_kr': 8.0,
     'L0_attn_b_W_v': 8.0,
     'L0_attn_b_W_o': 8.0,
     'L0_attn_b_W_idx': 8.0,
     'L0_attn_b_W_gate': 8.0,
     'L0_attn_b_W_sq': 8.0,
     'L0_attn_b_W_sk': 8.0,
     'L0_attn_b_W_sv': 8.0,
     'L0_attn_b_W_iout': 8.0}
    for name, (base, spread) in spreads.items():
        noise = np.random.default_rng([zlib.crc32(name.encode()), seed]).standard_normal(out[name].shape)
        drawn = base * np.exp(spread * noise) if base else spread * noise
        out[name] = jnp.asarray(drawn.astype(out[name].dtype))
    for name, factor in factors.items():
        out[name] = (out[name] * factor).astype(out[name].dtype)
    return out
```

```python
from contextlib import ExitStack

import concourse.bass as bass
from concourse import mybir
from concourse.alu_op_type import AluOpType as ALU
import numpy as np

ACT = mybir.ActivationFunctionType
AX = mybir.AxisListType
F32 = mybir.dt.float32
F32R = mybir.dt.float32r
BF16 = mybir.dt.bfloat16
I32 = mybir.dt.int32

P = 128
S = 1024
D = 256
NT = S // P
KO = D // P
NH = 16
HD = 16
FF = 4 * D
FO = FF // P
BANK = 512
QL, KVL = 192, 64
QL2 = QL - P
DK, DR, DV = 128, 64, 128
IH, TOPK = 8, 8
RSQRT_SEED = float(0x5F3759DF)


class Tensors:
    pass


class Stage:

    def __init__(self, ctx, nc, name):
        self.ctx, self.nc, self.name, self.made = ctx, nc, name, {}

    def __call__(self, what):
        if what not in self.made:
            self.made[what] = self.ctx.enter_context(self.nc.semaphore(f"{self.name}_{what}"))
        return self.made[what]


class Chain:

    def __init__(self, eng, sem):
        self.eng, self.sem, self.n = eng, sem, 0

    def step(self, ins):
        self.n += 1
        ins.then_inc(self.sem, 1)
        self.eng.wait_ge(self.sem, self.n)


def rsqrt(dve, chain, y, t, v):
    chain.step(dve.tensor_scalar(y.bitcast(I32), v.bitcast(I32), -0.5, RSQRT_SEED, ALU.mult, ALU.add))
    for _ in range(4):
        chain.step(dve.tensor_tensor(t, y, y, ALU.mult))
        chain.step(dve.scalar_tensor_tensor(out=t, in0=t, scalar=-0.5, in1=v, op0=ALU.mult, op1=ALU.mult))
        chain.step(dve.scalar_tensor_tensor(out=y, in0=t, scalar=1.5, in1=y, op0=ALU.add, op1=ALU.mult))


def layer_stats(dve, chain, k, x):
    for t in range(NT):
        chain.step(dve.bn_stats(k.stats[:, t, 0:6], x[:, t, :]))
        chain.step(dve.bn_aggr(k.mv[:, t, :], k.stats[:, t, 0:6]))


def prepare(nc, ctx, k, io):
    s = Stage(ctx, nc, "prep")
    with nc.Block() as block:

        @block.sync
        def _(sp):
            sp.dma_start(k.x[:, :, :], io["L0_attn_a_x"].rearrange("a (t p) d -> p (a t) d", p=P)).then_inc(s("x"), 16)
            sp.dma_start(k.ident[:, :], io["ident"]).then_inc(s("const"), 16)
            sp.dma_start(k.mask[:, :], io["mask"]).then_inc(s("const"), 16)
            sp.dma_start(k.cols[:, :], io["cols"]).then_inc(s("const"), 16)
            sp.dma_start(k.w_qkv[:, :, :], io["L0_attn_a_Wqkv"].rearrange("(a p) n -> p a n", p=P)).then_inc(s("const"), 16)
            sp.wait_ge(s("wo_zero"), 1)
            for j in range(4):
                src = io["L0_attn_a_Wo"].rearrange("(g j d) n -> j d g n", j=4, d=HD)[j]
                sp.dma_start(k.w_o[32 * j:32 * j + HD, :, :], src).then_inc(s("const"), 16)

        @block.scalar
        def _(act):
            act.dma_start(k.w_fc[:, :, :], io["L0_ffn_w_fc"].rearrange("(t p) n -> p t n", p=P)).then_inc(s("w_fc"), 16)
            act.dma_start(k.w_pr[:, :, :], io["L0_ffn_w_proj"].rearrange("(t p) n -> p t n", p=P)).then_inc(s("w_pr"), 16)
            for n in range(8):
                act.wait_ge(s("w_turned"), n + 1)
                act.activation(k.tern_out(n), k.ps[:, n % 4, :], ACT.Copy).then_inc(s("w_out"), 1)

        @block.gpsimd
        def _(pool):
            pool.memset(k.w_o[:, :, :], 0.0).then_inc(s("wo_zero"), 1)
            pool.memset(k.v_a[:, :, :, :], 0.0).then_inc(s("v_zero"), 1)
            pool.memset(k.ones[:, :], 1.0).then_inc(s("ones"), 1)
            pool.wait_ge(s("const"), 16 * 8)
            for n, w in enumerate((k.wq2, k.wk2)):
                for dup in range(2):
                    for a in range(KO):
                        pool.tensor_copy(w[:, a, :, dup, :],
                                         k.w_qkv[:, a, n * D:(n + 1) * D].rearrange("p (h d) -> p h d", d=HD)).then_inc(s("w_dup"), 1)

        @block.vector
        def _(dve):
            c = Chain(dve, s("dve"))
            dve.wait_ge(s("const"), 16 * 8)
            c.step(dve.tensor_copy(k.ident_bf[:, :], k.ident[:, :]))
            c.step(dve.tensor_copy(k.mask_bf[:, :], k.mask[:, :]))
            dve.wait_ge(s("x"), 16)
            layer_stats(dve, c, k, k.x)
            dve.wait_ge(s("w_fc"), 16)
            dve.wait_ge(s("w_pr"), 16)
            for n, w in enumerate((k.w_fc, k.w_pr)):
                dve.tensor_reduce(k.wsum[:, n:n + 1], w[:, :, :].rearrange("p a b -> p (a b)"), AX.X, ALU.add,
                                  apply_absolute_value=True).then_inc(s("wsum"), 1)
            dve.wait_ge(s("gamma"), 1)
            c.step(dve.tensor_scalar(k.gamma[:, :], k.ps[:, 7, 0:2], 1.0 / (FF * D), None, ALU.mult))
            c.step(dve.tensor_scalar(k.thr[:, :], k.gamma[:, :], 1e-6, 0.5, ALU.add, ALU.mult))
            c.step(dve.tensor_scalar(k.nthr[:, :], k.thr[:, :], -1.0, None, ALU.mult))
            for n, w in enumerate((k.w_fc, k.w_pr)):
                flat = w[:, :, :].rearrange("p a b -> p (a b)")
                c.step(dve.tensor_scalar(k.tmp2k[:, :], flat, k.nthr[:, n:n + 1], None, ALU.is_lt))
                dve.scalar_tensor_tensor(out=flat, in0=flat, scalar=k.thr[:, n:n + 1], in1=k.tmp2k[:, :],
                                         op0=ALU.is_gt, op1=ALU.subtract).then_inc(s("tern"), 1)
                dve.wait_ge(s("tern"), n + 1)
            c.step(dve.tensor_scalar(k.var[:, :], k.mv[:, :, 1], 1e-5, None, ALU.add))
            rsqrt(dve, c, k.rstd[:, :], k.tmp8[:, :], k.var[:, :])
            for t in range(NT):
                c.step(dve.tensor_scalar(k.xn[:, t, :], k.x[:, t, :], k.mv[:, t, 0:1], k.rstd[:, t:t + 1],
                                         ALU.subtract, ALU.mult))

        @block.tensor
        def _(pe):
            pe.wait_ge(s("wsum"), 2)
            pe.wait_ge(s("ones"), 1)
            pe.matmul(k.ps[:, 7, 0:2], k.ones[:, :], k.wsum[:, :], start=True, stop=True).then_inc(s("gamma"), 1)
            pe.wait_ge(s("const"), 16 * 8)
            for n in range(8):
                pe.wait_ge(s("tern"), 1 if n < 4 else 2)
                if n >= 4:
                    pe.wait_ge(s("w_out"), n - 3)
                for b in range(4):
                    ins = pe.transpose(k.ps[:, n % 4, b * P:(b + 1) * P], k.tern_in(n, b), k.ident[:, :])
                ins.then_inc(s("w_turned"), 1)


def turn_x(pe, k, s, t):
    for a in range(KO):
        ins = pe.transpose(k.ps[:, t % 4, a * P:(a + 1) * P], k.xn[:, t, a * P:(a + 1) * P], k.ident[:, :])
    ins.then_inc(s("turned"), 1)


def project_a(nc, ctx, k):
    s = Stage(ctx, nc, "pa")
    jobs = [("k", g, h) for g in range(4) for h in range(2)] + [("q", g, h) for g in range(4) for h in range(2)]
    with nc.Block() as block:

        @block.tensor
        def _(pe):
            for t in range(NT):
                if t >= 4:
                    pe.wait_ge(s("xT"), t - 3)
                turn_x(pe, k, s, t)
            pe.wait_ge(s("xT"), NT)
            for n, (what, g, half) in enumerate(jobs):
                w = k.wk2 if what == "k" else k.wq2
                if n >= 4:
                    pe.wait_ge(s("hi"), n - 3)
                    pe.wait_ge(s("lo"), n - 3)
                for a in range(KO):
                    ins = pe.matmul(k.ps[:, n % 4, :], w[:, a, 4 * g:4 * g + 4, :, :].rearrange("p h u d -> p (h u d)"),
                                    k.xT[:, a, half * BANK:(half + 1) * BANK], start=(a == 0), stop=(a == KO - 1))
                ins.then_inc(s("proj"), 1)
            for t in range(NT):
                if t >= 4:
                    pe.wait_ge(s("v"), t - 3)
                for a in range(KO):
                    ins = pe.matmul(k.ps[:, 4 + t % 4, 0:D], k.xT[:, a, t * P:(t + 1) * P], k.w_qkv[:, a, 2 * D:3 * D],
                                    start=(a == 0), stop=(a == KO - 1))
                ins.then_inc(s("vproj"), 1)

        @block.scalar
        def _(act):
            for t in range(NT):
                act.wait_ge(s("turned"), t + 1)
                act.activation(k.xT[:, :, t * P:(t + 1) * P], k.ps[:, t % 4, 0:D].rearrange("p (a n) -> p a n", a=KO),
                               ACT.Copy).then_inc(s("xT"), 1)
            for n, (what, g, half) in enumerate(jobs):
                act.wait_ge(s("proj"), n + 1)
                sl = slice(half * BANK, (half + 1) * BANK)
                if what == "k":
                    if n >= 2:
                        act.wait_ge(s("lo"), n - 1)
                    act.activation(k.khi[:, n % 2, :], k.ps[:, n % 4, :], ACT.Copy).then_inc(s("hi"), 1)
                else:
                    act.activation(k.qhi[:, g, sl], k.ps[:, n % 4, :], ACT.Copy, scale=float(HD) ** -0.5).then_inc(s("hi"), 1)
            for t in range(NT):
                act.wait_ge(s("vproj"), t + 1)
                act.activation(k.v_a[:, t, :, 0:HD], k.ps[:, 4 + t % 4, 0:D].rearrange("p (h d) -> p h d", d=HD),
                               ACT.Copy).then_inc(s("v"), 1)

        @block.vector
        def _(dve):
            c = Chain(dve, s("dve"))
            for n, (what, g, half) in enumerate(jobs):
                dve.wait_ge(s("proj"), n + 1)
                dve.wait_ge(s("hi"), n + 1)
                sl = slice(half * BANK, (half + 1) * BANK)
                if what == "k":
                    hi = k.khi[:, n % 2, :].bitcast(F32)
                    c.step(dve.tensor_scalar(k.tmp512[:, :], hi, k.cols[:, 1:2], None, ALU.mult))
                    dve.scalar_tensor_tensor(out=k.khl[:, g, sl], in0=k.ps[:, n % 4, :], scalar=k.cols[:, 0:1],
                                             in1=k.tmp512[:, :], op0=ALU.mult, op1=ALU.add).then_inc(s("lo"), 1)
                    dve.wait_ge(s("lo"), n + 1)
                else:
                    dve.scalar_tensor_tensor(out=k.qlo[:, g, sl], in0=k.ps[:, n % 4, :], scalar=float(HD) ** -0.5,
                                             in1=k.qhi[:, g, sl].bitcast(F32), op0=ALU.mult, op1=ALU.subtract).then_inc(s("lo"), 1)


def attention(nc, ctx, k, name, hu, passes, value, width, pool_unit=None, extra=None):
    s = Stage(ctx, nc, name)
    units = [(g, qt) for g in range(NH // hu) for qt in range(NT)]
    steps = [(u, j) for u in range(len(units)) for j in range(hu)]
    qt_of = [units[u][1] for u, _ in steps]
    n_ch = [1 if q < 4 else 2 for q in qt_of]
    first_ch = [sum(n_ch[:i]) for i in range(len(steps) + 1)]
    LT, LV = 2, 4
    NS = len(steps)
    if extra is not None:
        extra.bind(s, steps, units)

    def even(n):
        return (n + 1) // 2

    def odd(n):
        return n // 2

    with nc.Block() as block:

        @block.tensor
        def _(pe):
            if extra is not None:
                extra.pe_first(pe)
            for i in range(NS + LV + 1):
                if i < NS:
                    u, j = steps[i]
                    qt = qt_of[i]
                    if extra is not None:
                        extra.pe(pe, i)
                    if pool_unit is not None:
                        pe.wait_ge(s("q_masked"), 2 * (u + 1))
                    if i >= 2:
                        pe.wait_ge(s("exp"), i - 1)
                    nk = (qt + 1) * P
                    for c0 in range(0, nk, BANK):
                        n = min(BANK, nk - c0)
                        out = k.ps[:, 2 * (i % 2) + c0 // BANK, 0:n]
                        last = c0 + n == nk
                        ps = passes(i, u, j, qt)
                        for m, (q, kk) in enumerate(ps):
                            ins = pe.matmul(out, q, kk[:, c0:c0 + n], start=(m == 0), stop=(m == len(ps) - 1 and not last))
                        if last:
                            ins = pe.matmul(out[:, n - P:n], k.ident_bf[:, :], k.mask_bf[:, :], start=False, stop=True)
                    ins.then_inc(s("scores"), 1)
                if LT <= i < NS + LT:
                    i2 = i - LT
                    pe.wait_ge(s("exp"), i2 + 1)
                    for ch in range(n_ch[i2]):
                        n = first_ch[i2] + ch
                        if n >= 2:
                            pe.wait_ge(s("out_even" if n % 2 == 0 else "out_odd"), n // 2)
                        for b in range(4 * ch, min(4 * ch + 4, qt_of[i2] + 1)):
                            ins = pe.transpose(k.ps[:, 4 + n % 2, (b % 4) * P:(b % 4 + 1) * P],
                                               k.prob[:, i2 % 3, b * P:(b + 1) * P], k.ident[:, :])
                        ins.then_inc(s("turned"), 1)
                if i >= LV and steps[min(i - LV, NS - 1)][1] == hu - 1 and i - LV < NS:
                    u = steps[i - LV][0]
                    g, qt = units[u]
                    n = first_ch[i - LV + 1]
                    pe.wait_ge(s("out_even"), even(n))
                    pe.wait_ge(s("out_odd"), odd(n))
                    if u >= 1:
                        pe.wait_ge(s("o_out"), u)
                    for b in range(qt + 1):
                        for jj in range(hu):
                            ins = pe.matmul(k.ps[width * jj:width * (jj + 1), 6, 0:P], value(b, g * hu + jj),
                                            k.pT[:, u % 2, jj, b * P:(b + 1) * P], start=(b == 0), stop=(b == qt))
                    ins.then_inc(s("pv"), 1)

        def take_out(eng, i2, parity, copy):
            u, j = steps[i2]
            for ch in range(n_ch[i2]):
                n = first_ch[i2] + ch
                if n % 2 != parity:
                    continue
                eng.wait_ge(s("turned"), n + 1)
                if u >= 2:
                    eng.wait_ge(s("pv"), u - 1)
                w = (min(4 * ch + 4, qt_of[i2] + 1) - 4 * ch) * P
                copy(k.pT[:, u % 2, j, ch * BANK:ch * BANK + w], k.ps[:, 4 + parity, 0:w])

        @block.vector
        def _(dve):
            if extra is not None:
                extra.dve_first(dve)
            for i in range(NS + LV + 2):
                if i < NS:
                    nk = (qt_of[i] + 1) * P
                    dve.wait_ge(s("scores"), i + 1)
                    u, j = steps[i]
                    col = k.nmax[:, qt_of[i], units[u][0] * hu + j]
                    ap = k.ps[:, 2 * (i % 2):2 * (i % 2) + 2, :].rearrange("p a b -> p (a b)")[:, 0:nk]
                    dve.tensor_reduce(k.nmax[:, qt_of[i], units[u][0] * hu + j:units[u][0] * hu + j + 1], ap, AX.X, ALU.max,
                                      negate=True).then_inc(s("max"), 1)
                if LT <= i < NS + LT:
                    take_out(dve, i - LT, 1, lambda o, a: dve.tensor_copy(o, a).then_inc(s("out_odd"), 1))
                if i >= LV + 1 and i - LV - 1 < NS and steps[i - LV - 1][1] == hu - 1:
                    u = steps[i - LV - 1][0]
                    g, qt = units[u]
                    dve.wait_ge(s("pv"), u + 1)
                    dve.tensor_copy(k.oT[:, g, qt * P:(qt + 1) * P], k.ps[:, 6, 0:P]).then_inc(s("o_out"), 1)
                if extra is not None and i < NS:
                    extra.dve(dve, i)

        @block.scalar
        def _(act):
            if extra is not None:
                extra.act_first(act)
            for i in range(NS + LT):
                if i >= LT:
                    take_out(act, i - LT, 0, lambda o, a: act.activation(o, a, ACT.Copy).then_inc(s("out_even"), 1))
                if i < NS:
                    nk = (qt_of[i] + 1) * P
                    u, j = steps[i]
                    h = units[u][0] * hu + j
                    act.wait_ge(s("max"), i + 1)
                    if i >= 3:
                        act.wait_ge(s("turned"), first_ch[i - 2])
                    ap = k.ps[:, 2 * (i % 2):2 * (i % 2) + 2, :].rearrange("p a b -> p (a b)")[:, 0:nk]
                    act.activation(k.prob[:, i % 3, 0:nk], ap, ACT.Exp, bias=k.nmax[:, qt_of[i], h:h + 1],
                                   accum_out=k.den[:, qt_of[i], h:h + 1]).then_inc(s("exp"), 1)
                if extra is not None and i < NS:
                    extra.act(act, i)

        if pool_unit is not None:
            @block.gpsimd
            def _(pool):
                for u, (g, qt) in enumerate(units):
                    if u >= 2:
                        pool.wait_ge(s("scores"), hu * (u - 1))
                    pool_unit(pool, s, u, g, qt)
        if extra is not None:
            @block.gpsimd
            def _(pool):
                extra.pool(pool)

            @block.sync
            def _(sp):
                extra.sync(sp)


def attend_a(nc, ctx, k):
    def masked(pool, s, u, g, qt):
        for part, q in enumerate((k.qhi, k.qlo)):
            src = q[:, g, qt * P:(qt + 1) * P].bitcast(F32).unsqueeze(1).broadcast_to([P, 4, P])
            row = k.cols[:, 4:8].unsqueeze(2).broadcast_to([P, 4, P])
            pool.tensor_tensor(k.qm[:, u % 2, part, :, :], src, row, ALU.mult).then_inc(s("q_masked"), 1)

    def passes(i, u, j, qt):
        g = u // NT
        return [(k.qm[:, u % 2, part, j, :], k.khl[:, g, :]) for part in range(2)]

    attention(nc, ctx, k, "aa", 4, passes, lambda b, h: k.v_a[:, b, h, :], 32, pool_unit=masked)


def finish_attention(nc, ctx, k, name, n_groups, sel, w_out, norm, row=None):
    s = Stage(ctx, nc, name)
    with nc.Block() as block:

        @block.tensor
        def _(pe):
            pe.wait_ge(s("rden"), 1)
            for t in range(NT):
                ins = pe.transpose(k.ps[0:NH, 6 + t // 4, (t % 4) * P:(t % 4 + 1) * P], k.rden[:, t, :], k.ident[:, :])
            ins.then_inc(s("rT"), 1)
            pe.wait_ge(s("rT_out"), 1)
            for n in range(2 * n_groups):
                g, half = divmod(n, 2)
                if n >= 4:
                    pe.wait_ge(s("o_norm"), n - 3)
                pe.matmul(k.ps[:, n % 4, :], sel[:, g, :], k.rT[:, half * BANK:(half + 1) * BANK],
                          start=True, stop=True).then_inc(s("bc"), 1)
            pe.wait_ge(s("o_norm"), 2 * n_groups)
            for t in range(NT):
                if t >= 2:
                    pe.wait_ge(s("x_new"), t - 1)
                for g in range(n_groups):
                    last = g == n_groups - 1 and row is None
                    ins = pe.matmul(k.ps[:, 4 + t % 2, 0:D], k.oT[:, g, t * P:(t + 1) * P], w_out[:, g, :],
                                    start=(g == 0), stop=last)
                if row is not None:
                    ins = pe.matmul(k.ps[:, 4 + t % 2, 0:D], k.ones[0:1, :], row, start=False, stop=True)
                ins.then_inc(s("proj"), 1)

        @block.scalar
        def _(act):
            act.wait_ge(s("rT"), 1)
            act.activation(k.rT[:, :], k.ps[0:NH, 6:8, :].rearrange("p a b -> p (a b)"), ACT.Copy).then_inc(s("rT_out"), 1)

        @block.vector
        def _(dve):
            c = Chain(dve, s("dve"))
            dve.reciprocal(k.rden[:, :, :], k.den[:, :, :]).then_inc(s("rden"), 1)
            for n in range(2 * n_groups):
                g, half = divmod(n, 2)
                o = k.oT[:, g, half * BANK:(half + 1) * BANK]
                dve.wait_ge(s("bc"), n + 1)
                dve.tensor_tensor(o, k.ps[:, n % 4, :], o, ALU.mult).then_inc(s("o_norm"), 1)
            for t in range(NT):
                dve.wait_ge(s("proj"), t + 1)
                dve.tensor_tensor(k.x[:, t, :], k.ps[:, 4 + t % 2, 0:D], k.x[:, t, :], ALU.add).then_inc(s("x_new"), 1)
                dve.wait_ge(s("x_new"), t + 1)
                c.step(dve.bn_stats(k.stats[:, t, 0:6], k.x[:, t, :]))
                c.step(dve.bn_aggr(k.mv[:, t, :], k.stats[:, t, 0:6]))
            norm(dve, c)


def ffn_norm(dve, c, k):
    e1, e2 = 1e-5, 1e-6
    c.step(dve.tensor_scalar(k.var[:, :], k.mv[:, :, 1], 1.0 + e2, e1 * e2, ALU.mult, ALU.add))
    rsqrt(dve, c, k.rstd[:, :], k.tmp8[:, :], k.var[:, :])
    c.step(dve.tensor_scalar(k.sc_fc[:, :], k.rstd[:, :], k.gamma[:, 0:1], None, ALU.mult))


def ffn(nc, ctx, k, name, out=None):
    s = Stage(ctx, nc, name)
    def x_turn(t):
        return t + 2 * max(0, t - 3)

    def hidden_turn(t):
        return min(t + 4, NT) + 2 * t

    def turned_parts(t):
        if t < NT:
            yield x_turn(t), k.xqT[:, t % 2], KO, 0, None
        if t >= 2:
            for c in range(2):
                yield hidden_turn(t - 2) + c, k.hT[:, (t - 2) % 2], 4, 4 * c, t - 2

    def dst(buf, part, w, b0):
        return buf[:, part, b0:b0 + w, :].rearrange("p a b -> p (a b)")

    def free_to_write(eng, t, hid):
        if hid is None:
            if t >= 2:
                eng.wait_ge(s("fc"), t - 1)
        elif hid >= 2:
            eng.wait_ge(s("proj"), hid - 1)

    def dst(buf, part, w, b0):
        return buf[:, part, b0:b0 + w, :].rearrange("p a b -> p (a b)")

    def chunks(t):
        return [(hidden_turn(t) + c, k.hT[:, t % 2], 4 * c) for c in range(2)]

    with nc.Block() as block:

        @block.tensor
        def _(pe):
            def turn(n, src, w):
                if n >= 3:
                    pe.wait_ge(s("hi"), n - 2)
                    pe.wait_ge(s("lo"), n - 2)
                for b in range(w):
                    ins = pe.transpose(k.ps[:, 4 + n % 3, b * P:(b + 1) * P], src[:, b * P:(b + 1) * P], k.ident[:, :])
                ins.then_inc(s("turned"), 1)

            def fc(t):
                pe.wait_ge(s("hi"), x_turn(t) + 1)
                pe.wait_ge(s("lo"), x_turn(t) + 1)
                if t >= 2:
                    pe.wait_ge(s("gelu"), t - 1)
                for n in range(2):
                    for m, (part, a) in enumerate([(part, a) for part in range(2) for a in range(KO)]):
                        ins = pe.matmul(k.ps[:, 2 * (t % 2) + n, :], k.xqT[:, t % 3, part, a, :],
                                        k.t_fc[:, a, n * BANK:(n + 1) * BANK], start=(m == 0), stop=(m == 2 * KO - 1))
                ins.then_inc(s("fc"), 1)

            def proj(t):
                pe.wait_ge(s("hi"), hidden_turn(t) + 2)
                pe.wait_ge(s("lo"), hidden_turn(t) + 2)
                if t >= 1:
                    pe.wait_ge(s("o_raw"), t)
                for f in range(FO):
                    for part in range(2):
                        ins = pe.matmul(k.ps[:, 7, 0:D], k.hT[:, t % 2, part, f, :], k.t_pr[:, f, :],
                                        start=(f == 0 and part == 0), stop=(f == FO - 1 and part == 1))
                ins.then_inc(s("proj"), 1)

            for t in range(NT + 4):
                if t < NT:
                    pe.wait_ge(s("x_clip"), t + 1)
                    turn(x_turn(t), k.xn[:, t, :], KO)
                if 2 <= t < NT + 2:
                    fc(t - 2)
                if 3 <= t < NT + 3:
                    pe.wait_ge(s("h_clip"), t - 2)
                    for c in range(2):
                        turn(hidden_turn(t - 3) + c, k.hc[:, (t - 3) % 2, c * BANK:(c + 1) * BANK], 4)
                if t >= 4:
                    proj(t - 4)

        @block.scalar
        def _(act):
            def hi(n, buf, w, b0):
                act.wait_ge(s("turned"), n + 1)
                act.activation(dst(buf, 0, w, b0), k.ps[:, 4 + n % 3, 0:w * P], ACT.Copy).then_inc(s("hi"), 1)

            for t in range(NT + 5):
                if t >= 5:
                    act.wait_ge(s("proj"), t - 4)
                    act.activation(k.o_raw[:, t - 5, :], k.ps[:, 7, 0:D], ACT.Copy).then_inc(s("o_raw"), 1)
                if t < NT:
                    if t >= 3:
                        act.wait_ge(s("fc"), t - 2)
                    hi(x_turn(t), k.xqT[:, t % 3], KO, 0)
                if 2 <= t < NT + 2:
                    h = t - 2
                    act.wait_ge(s("fc"), h + 1)
                    if h >= 2:
                        act.wait_ge(s("mean"), h - 1)
                        act.wait_ge(s("centred"), h - 1)
                    act.activation(k.h[:, h % 2, :], k.ps[:, 2 * (h % 2):2 * (h % 2) + 2, :].rearrange("p a b -> p (a b)"),
                                   ACT.Gelu, scale=k.sc_fc[:, h:h + 1]).then_inc(s("gelu"), 1)
                if 3 <= t < NT + 3:
                    if t >= 5:
                        act.wait_ge(s("proj"), t - 4)
                    for n, buf, b0 in chunks(t - 3):
                        hi(n, buf, 4, b0)
                if 2 <= t < NT + 2:
                    h = t - 2
                    act.wait_ge(s("mean"), h + 1)
                    act.wait_ge(s("gelu"), h + 1)
                    if h >= 2:
                        act.wait_ge(s("turned"), hidden_turn(h - 2) + 2)
                    act.activation(k.hc[:, h % 2, :], k.h[:, h % 2, :], ACT.Identity,
                                   bias=k.nmean[:, h:h + 1]).then_inc(s("centred"), 1)

        @block.vector
        def _(dve):
            c = Chain(dve, s("dve"))

            def centre_x(t):
                xc = k.xn[:, t, :]
                c.step(dve.tensor_scalar(xc, k.x[:, t, :], k.mv[:, t, 0:1], None, ALU.subtract))
                c.step(dve.tensor_reduce(k.big[:, 0:1], xc, AX.X, ALU.max, apply_absolute_value=True))
                c.step(dve.tensor_scalar(k.big[:, 1:2], k.big[:, 0:1], -1.0, None, ALU.mult))
                dve.tensor_scalar(xc, xc, k.big[:, 0:1], k.big[:, 1:2], ALU.min, ALU.max).then_inc(s("x_clip"), 1)
                dve.wait_ge(s("x_clip"), t + 1)

            def hidden_mean(t):
                h = k.h[:, t % 2, :]
                dve.wait_ge(s("gelu"), t + 1)
                for n in range(2):
                    c.step(dve.bn_stats(k.stats[:, t, 6 * n:6 * n + 6], h[:, n * BANK:(n + 1) * BANK]))
                c.step(dve.bn_aggr(k.mvh[:, t, :], k.stats[:, t, 0:12]))
                dve.tensor_scalar(k.nmean[:, t:t + 1], k.mvh[:, t, 0:1], -1.0, None, ALU.mult).then_inc(s("mean"), 1)

            def hidden_clip(t):
                hc = k.hc[:, t % 2, :]
                dve.wait_ge(s("centred"), t + 1)
                c.step(dve.tensor_reduce(k.big[:, 2:3], hc, AX.X, ALU.max, apply_absolute_value=True))
                c.step(dve.tensor_scalar(k.big[:, 3:4], k.big[:, 2:3], -1.0, None, ALU.mult))
                dve.tensor_scalar(hc, hc, k.big[:, 2:3], k.big[:, 3:4], ALU.min, ALU.max).then_inc(s("h_clip"), 1)
                dve.wait_ge(s("h_clip"), t + 1)

            def lo(n, buf, w, b0):
                dve.wait_ge(s("hi"), n + 1)
                dve.tensor_tensor(dst(buf, 1, w, b0), k.ps[:, 4 + n % 3, 0:w * P], dst(buf, 0, w, b0).bitcast(F32),
                                  ALU.subtract).then_inc(s("lo"), 1)

            centre_x(0)
            centre_x(1)
            for t in range(NT + 3):
                if t < NT:
                    lo(x_turn(t), k.xqT[:, t % 3], KO, 0)
                if t + 2 < NT:
                    centre_x(t + 2)
                if 2 <= t < NT + 2:
                    hidden_mean(t - 2)
                if t >= 3:
                    for n, buf, b0 in chunks(t - 3):
                        lo(n, buf, 4, b0)
                if 2 <= t < NT + 2:
                    hidden_clip(t - 2)
            c.step(dve.tensor_scalar(k.var[:, :], k.mvh[:, :, 1], 1e-6, None, ALU.add))
            rsqrt(dve, c, k.rstd[:, :], k.tmp8[:, :], k.var[:, :])
            c.step(dve.tensor_scalar(k.sc_pr[:, :], k.rstd[:, :], k.gamma[:, 1:2], None, ALU.mult))
            for t in range(NT):
                dve.wait_ge(s("o_raw"), t + 1)
                dve.scalar_tensor_tensor(out=k.x[:, t, :], in0=k.o_raw[:, t, :], scalar=k.sc_pr[:, t:t + 1],
                                         in1=k.x[:, t, :], op0=ALU.mult, op1=ALU.add).then_inc(s("x_new"), 1)
            if out is None:
                dve.wait_ge(s("x_new"), NT)
                layer_stats(dve, c, k, k.x)
                c.step(dve.tensor_scalar(k.var[:, :], k.mv[:, :, 1], 1e-5, None, ALU.add))
                rsqrt(dve, c, k.rstd[:, :], k.tmp8[:, :], k.var[:, :])
                for t in range(NT):
                    c.step(dve.tensor_scalar(k.xn[:, t, :], k.x[:, t, :], k.mv[:, t, 0:1], k.rstd[:, t:t + 1],
                                             ALU.subtract, ALU.mult))

        if out is not None:
            @block.sync
            def _(sp):
                for t in range(NT):
                    sp.wait_ge(s("x_new"), t + 1)
                    sp.dma_start(out[0, t * P:(t + 1) * P, :], k.x[:, t, :]).then_inc(s("stored"), 16)
                sp.wait_ge(s("stored"), 16 * NT)


def load_b(nc, ctx, k, io):
    s = Stage(ctx, nc, "lb")
    with nc.Block() as block:

        @block.sync
        def _(sp):
            for dst, src in ((k.w_qc[:, 0, :], io["L0_attn_b_W_qc"][0:P]), (k.w_qc[0:QL2, 1, :], io["L0_attn_b_W_qc"][P:QL]),
                             (k.w_qr[:, 0, :], io["L0_attn_b_W_qr"][0:P]), (k.w_qr[0:QL2, 1, :], io["L0_attn_b_W_qr"][P:QL]),
                             (k.w_kc[:, :], io["L0_attn_b_W_kc"]), (k.w_v[:, :], io["L0_attn_b_W_v"]),
                             (k.w_ob[:, :, :], io["L0_attn_b_W_o"].rearrange("(h p) n -> p h n", p=P)),
                             (k.w_cp[:, :, :], io["L0_attn_b_W_cp"].rearrange("(a p) n -> p a n", p=P)),
                             (k.w_ck[:, :, 0:KVL], io["L0_attn_b_W_c"].rearrange("(a p) n -> p a n", p=P)),
                             (k.w_kr[:, :, :], io["L0_attn_b_W_kr"].rearrange("(a p) n -> p a n", p=P)),
                             (k.cos[:, :], io["cos"]), (k.sin[:, :], io["sin"]), (k.sel_b[:, :, :], io["sel_b"])):
                sp.dma_start(dst, src).then_inc(s("loaded"), 16)
            sp.wait_ge(s("loaded"), 16 * 13)

        @block.gpsimd
        def _(pool):
            pool.wait_ge(s("loaded"), 16 * 13)
            for half in range(2):
                for a, rows in ((0, P), (1, QL2)):
                    pool.tensor_copy(k.aw[0:rows, a, :, KVL + 32 * half:KVL + 32 * half + 32],
                                     k.w_qr[0:rows, a, :].rearrange("p (h f two) -> p h f two", two=2, f=32)[:, :, :, half])\
                        .then_inc(s("rope_cols"), 1)
                pool.tensor_copy(k.w_ck[:, :, KVL + 32 * half:KVL + 32 * half + 32],
                                 k.w_kr[:, :, :].rearrange("p a (f two) -> p a f two", two=2)[:, :, :, half])\
                    .then_inc(s("rope_cols"), 1)


def prepare_b(nc, ctx, k):
    s = Stage(ctx, nc, "pb")
    jobs = ([("x", t) for t in range(NT)] + [("w", h) for h in range(NH)] + [("k", n) for n in range(2)]
            + [("cp", n) for n in range(4)] + [("a", n) for n in range(4)] + [("vo", n) for n in range(NH // 2)] + [("c", 0)])
    at = {j: n for n, j in enumerate(jobs)}

    def outs(eng_is_act):
        for n, (what, i) in enumerate(jobs):
            b = k.ps[:, n % 8, :]
            parts = {
                "x": lambda: [(k.xT[:, :, i * P:(i + 1) * P], b[:, 0:D].rearrange("p (a n) -> p a n", a=KO))],
                "w": lambda: [(k.wT[:, i, :], b[:, 0:QL + 2 * KVL])],
                "k": lambda: [(k.kraw[:, i * BANK:(i + 1) * BANK], b)],
                "cp": lambda: [(k.cpT[:, 0, (i % 2) * BANK:(i % 2 + 1) * BANK], b)] if i < 2 else
                              [(k.cpT[0:QL2, 1, (i % 2) * BANK:(i % 2 + 1) * BANK], b[0:QL2, :])],
                "a": lambda: [(k.aw[:, 0, 4 * i:4 * i + 4, 0:KVL], b[:, 0:D].rearrange("p (h n) -> p h n", h=4)),
                              (k.aw[0:QL2, 1, 4 * i:4 * i + 4, 0:KVL], b[0:QL2, D:2 * D].rearrange("p (h n) -> p h n", h=4))],
                "vo": lambda: [(k.w_vo[:, i, :], b[:, 0:D])],
                "c": lambda: [(k.c_tok[:, :, :].rearrange("p t n -> p (t n)"), b)],
            }[what]()
            if (n % 2 == 0) == eng_is_act:
                yield n, parts

    with nc.Block() as block:

        @block.tensor
        def _(pe):
            def done(*names):
                n = max(at[x] for x in names)
                pe.wait_ge(s("act_out"), n // 2 + 1)
                pe.wait_ge(s("dve_out"), (n + 1) // 2)

            for n, (what, i) in enumerate(jobs):
                b = k.ps[:, n % 8, :]
                if n >= 8:
                    done(jobs[n - 8])
                if what == "x":
                    for a in range(KO):
                        ins = pe.transpose(b[:, a * P:(a + 1) * P], k.xn[:, i, a * P:(a + 1) * P], k.ident[:, :])
                elif what == "w":
                    cols = slice(i * P, (i + 1) * P)
                    pe.transpose(b[:, 0:P], k.w_qc[:, 0, cols], k.ident[:, :])
                    pe.transpose(b[:, P:QL], k.w_qc[0:QL2, 1, cols], k.ident[0:QL2, 0:QL2])
                    pe.transpose(b[:, QL:QL + KVL], k.w_kc[:, cols], k.ident[0:KVL, 0:KVL])
                    ins = pe.transpose(b[:, QL + KVL:QL + 2 * KVL], k.w_v[:, cols], k.ident[0:KVL, 0:KVL])
                elif what == "k":
                    done(("x", NT - 1))
                    for a in range(KO):
                        ins = pe.matmul(b, k.w_ck[:, a, :], k.xT[:, a, i * BANK:(i + 1) * BANK], start=(a == 0), stop=(a == KO - 1))
                elif what == "cp":
                    for a in range(KO):
                        w = k.w_cp[:, a, 0:P] if i < 2 else k.w_cp[:, a, P:QL]
                        ins = pe.matmul(b if i < 2 else b[0:QL2, :], w, k.xT[:, a, (i % 2) * BANK:(i % 2 + 1) * BANK],
                                        start=(a == 0), stop=(a == KO - 1))
                elif what == "a":
                    done(("w", 4 * i + 3))
                    for h in range(4):
                        for part, rows in ((0, P), (1, QL2)):
                            ins = pe.matmul(b[0:rows, part * D + h * KVL:part * D + (h + 1) * KVL],
                                            k.wT[:, 4 * i + h, part * P:part * P + rows], k.wT[:, 4 * i + h, QL:QL + KVL],
                                            start=True, stop=True)
                elif what == "vo":
                    for j in range(2):
                        ins = pe.matmul(b[KVL * j:KVL * (j + 1), 0:D], k.wT[:, 2 * i + j, QL + KVL:QL + 2 * KVL],
                                        k.w_ob[:, 2 * i + j, :], start=True, stop=True)
                else:
                    done(("k", 1))
                    for t in range(NT):
                        ins = pe.transpose(b[:, t * KVL:(t + 1) * KVL], k.kraw[0:KVL, t * P:(t + 1) * P], k.ident[0:KVL, 0:KVL])
                ins.then_inc(s("job"), 1)

        @block.scalar
        def _(act):
            for n, parts in outs(True):
                act.wait_ge(s("job"), n + 1)
                for m, (o, a) in enumerate(parts):
                    ins = act.activation(o, a, ACT.Copy)
                ins.then_inc(s("act_out"), 1)
            act.wait_ge(s("key"), 2)
            act.activation(k.k_hi[:, :], k.key[:, :], ACT.Copy).then_inc(s("khi"), 1)

        @block.vector
        def _(dve):
            c = Chain(dve, s("dve"))
            for n, parts in outs(False):
                dve.wait_ge(s("job"), n + 1)
                for o, a in parts:
                    ins = dve.tensor_copy(o, a)
                ins.then_inc(s("dve_out"), 1)
            dve.wait_ge(s("act_out"), (len(jobs) + 1) // 2)
            dve.wait_ge(s("dve_out"), len(jobs) // 2)
            dve.tensor_tensor(k.key[:, :], k.kraw[:, :], k.cos[:, :], ALU.mult).then_inc(s("key"), 1)
            dve.wait_ge(s("swapped"), 32)
            c.step(dve.tensor_tensor(k.swp[KVL:P, 0, :], k.swp[KVL:P, 0, :], k.sin[KVL:P, :], ALU.mult))
            dve.wait_ge(s("key"), 1)
            dve.tensor_tensor(k.key[KVL:P, :], k.key[KVL:P, :], k.swp[KVL:P, 0, :], ALU.add).then_inc(s("key"), 1)
            dve.wait_ge(s("khi"), 1)
            c.step(dve.tensor_tensor(k.k_lo[:, :], k.key[:, :], k.k_hi[:, :].bitcast(F32), ALU.subtract))

        @block.sync
        def _(sp):
            sp.wait_ge(s("act_out"), at[("k", 1)] // 2 + 1)
            sp.wait_ge(s("dve_out"), (at[("k", 1)] + 1) // 2)
            sp.dma_start(k.swp[KVL:KVL + 32, 0, :], k.kraw[KVL + 32:P, :]).then_inc(s("swapped"), 16)
            sp.dma_start(k.swp[KVL + 32:P, 0, :], k.kraw[KVL:KVL + 32, :]).then_inc(s("swapped"), 16)
            sp.wait_ge(s("swapped"), 32)


def sparse_b(nc, ctx, k, io):
    s = Stage(ctx, nc, "sp")
    J = IH * TOPK
    with nc.Block() as block:

        @block.sync
        def _(sp):
            for dst, src in ((k.w_gate[:, :, :], io["L0_attn_b_W_gate"].rearrange("(a p) n -> p a n", p=P)),
                             (k.w_idx[:, :, :], io["L0_attn_b_W_idx"].rearrange("(a p) n -> p a n", p=P)),
                             (k.w_s[:, 0, :], io["L0_attn_b_W_sq"]), (k.w_s[:, 1, :], io["L0_attn_b_W_sk"]),
                             (k.w_s[:, 2, :], io["L0_attn_b_W_sv"]), (k.w_s[:, 3, :], io["L0_attn_b_W_iout"][:, 0:DV]),
                             (k.small[:, :], io["small"])):
                sp.dma_start(dst, src).then_inc(s("loaded"), 16)

        eye8, mean8, tokens, block_mask = k.small[0:IH, 0:IH], k.small[0:J, 8:16], k.small[:, 16:24], k.small[0:J, 24:24 + J]

        @block.tensor
        def _(pe):
            pe.wait_ge(s("loaded"), 16 * 7)
            for half in range(2):
                for a in range(KO):
                    ins = pe.matmul(k.ps[0:IH, half, :], k.w_gate[:, a, :], k.xT[:, a, half * BANK:(half + 1) * BANK],
                                    start=(a == 0), stop=(a == KO - 1))
            ins.then_inc(s("pe"), 1)
            pe.wait_ge(s("v_index"), 1)
            pe.matmul(k.ps[:, 2, 0:J], k.ones[0:IH, :], k.bd[:, :, :].rearrange("p a b -> p (a b)"),
                      start=True, stop=True).then_inc(s("pe"), 1)
            pe.wait_ge(s("v_onehot"), NT)
            for a in range(KO):
                for t in range(NT):
                    ins = pe.matmul(k.ps[:, 3, a * J:(a + 1) * J], k.xn[:, t, a * P:(a + 1) * P], k.onehot[:, t, :],
                                    start=(t == 0), stop=(t == NT - 1))
            ins.then_inc(s("pe"), 1)
            pe.wait_ge(s("v_xsel"), 1)
            for h in range(IH):
                for a in range(KO):
                    ins = pe.matmul(k.ps[:, 4, h * TOPK:(h + 1) * TOPK], k.w_idx[:, a, h * P:(h + 1) * P],
                                    k.xsel[:, a, h * TOPK:(h + 1) * TOPK], start=(a == 0), stop=(a == KO - 1))
            ins.then_inc(s("pe"), 1)
            pe.wait_ge(s("v_sel"), 1)
            pe.matmul(k.ps[:, 5, 0:J], k.w_s[:, 0, :], k.sel[:, :], start=True, stop=True)
            pe.matmul(k.ps[:, 5, J:2 * J], k.w_s[:, 1, :], k.sel[:, :], start=True, stop=True)
            pe.matmul(k.ps[0:J, 5, 2 * J:2 * J + P], k.sel[:, :], k.w_s[:, 2, :], start=True, stop=True).then_inc(s("pe"), 1)
            pe.wait_ge(s("v_qkv"), 2)
            pe.matmul(k.ps[0:J, 6, 0:J], k.sqk[:, 0:J], k.sqk[:, J:2 * J], start=True, stop=True).then_inc(s("pe"), 1)
            pe.wait_ge(s("v_prob"), 1)
            pe.matmul(k.ps[0:J, 7, 0:IH], k.sprob[:, :], mean8, start=True, stop=True).then_inc(s("pe"), 1)
            pe.wait_ge(s("v_pm"), 1)
            pe.matmul(k.ps[:, 0, 0:IH], k.sv[:, :], k.chain[0:J, 0:IH], start=True, stop=True).then_inc(s("pe"), 1)
            pe.wait_ge(s("v_m"), 1)
            pe.matmul(k.ps[:, 1, 0:IH], k.w_s[:, 3, :], k.chain[:, 8:8 + IH], start=True, stop=True).then_inc(s("pe"), 1)
            pe.wait_ge(s("v_io"), 1)
            for h in range(NH):
                ins = pe.matmul(k.ps[0:1, 2, 0:D], k.chain[:, 16 + h // 2:17 + h // 2], k.w_ob[:, h, :],
                                start=(h == 0), stop=(h == NH - 1))
            ins.then_inc(s("pe"), 1)

        @block.scalar
        def _(act):
            act.wait_ge(s("v_smax"), 1)
            act.activation(k.sprob[:, :], k.sprob[:, :], ACT.Exp, bias=k.scol[0:J, 0:1], accum_out=k.scol[0:J, 1:2])\
                .then_inc(s("exp"), 1)

        @block.vector
        def _(dve):
            c = Chain(dve, s("dve"))

            def pe_done(n):
                dve.wait_ge(s("pe"), n)

            pe_done(1)
            c.step(dve.tensor_copy(k.gT[:, :], k.ps[0:IH, 0:2, :].rearrange("p a b -> p (a b)")))
            c.step(dve.max(k.top[:, :], k.gT[:, :]))
            c.step(dve.max_index(k.top_at[:, :], k.top[:, :], k.gT[:, :]))
            c.step(dve.tensor_copy(k.top[:, :], k.top_at[:, :]))
            dve.tensor_tensor(k.bd[:, :, :], k.top[:, :].unsqueeze(1).broadcast_to([IH, IH, TOPK]),
                              eye8.unsqueeze(2).broadcast_to([IH, IH, TOPK]), ALU.mult).then_inc(s("v_index"), 1)
            pe_done(2)
            for t in range(NT):
                dve.tensor_scalar(k.onehot[:, t, :], k.ps[:, 2, 0:J], tokens[:, t:t + 1], None, ALU.is_equal).then_inc(s("v_onehot"), 1)
            pe_done(3)
            dve.tensor_copy(k.xsel[:, :, :].rearrange("p a b -> p (a b)"), k.ps[:, 3, 0:KO * J]).then_inc(s("v_xsel"), 1)
            pe_done(4)
            dve.tensor_copy(k.sel[:, :], k.ps[:, 4, 0:J]).then_inc(s("v_sel"), 1)
            pe_done(5)
            dve.tensor_copy(k.sqk[:, :], k.ps[:, 5, 0:2 * J]).then_inc(s("v_qkv"), 1)
            dve.tensor_copy(k.sv[:, :], k.ps[0:J, 5, 2 * J:2 * J + P]).then_inc(s("v_qkv"), 1)
            pe_done(6)
            c.step(dve.scalar_tensor_tensor(out=k.sprob[:, :], in0=k.ps[0:J, 6, 0:J], scalar=float(P) ** -0.5, in1=block_mask,
                                            op0=ALU.mult, op1=ALU.add))
            dve.tensor_reduce(k.scol[0:J, 0:1], k.sprob[:, :], AX.X, ALU.max, negate=True).then_inc(s("v_smax"), 1)
            dve.wait_ge(s("exp"), 1)
            c.step(dve.reciprocal(k.scol[0:J, 2:3], k.scol[0:J, 1:2]))
            dve.tensor_scalar(k.sprob[:, :], k.sprob[:, :], k.scol[0:J, 2:3], None, ALU.mult).then_inc(s("v_prob"), 1)
            pe_done(7)
            dve.tensor_copy(k.chain[0:J, 0:IH], k.ps[0:J, 7, 0:IH]).then_inc(s("v_pm"), 1)
            pe_done(8)
            dve.tensor_copy(k.chain[:, 8:8 + IH], k.ps[:, 0, 0:IH]).then_inc(s("v_m"), 1)
            pe_done(9)
            dve.tensor_copy(k.chain[:, 16:16 + IH], k.ps[:, 1, 0:IH]).then_inc(s("v_io"), 1)
            pe_done(10)
            c.step(dve.tensor_copy(k.row[:, :], k.ps[0:1, 2, 0:D]))


class QueriesB:

    HALF_AT = (1, 3, 5, 7)
    SPLIT_AT = (11, 14)
    PER = 2 * NT

    def __init__(self, k):
        self.k = k

    def bind(self, s, steps, units):
        self.s, self.pairs = s, NH // 2

    def work(self, i):
        p, at = divmod(i, self.PER)
        if p + 1 >= self.pairs:
            return [], []
        return ([4 * (p + 1) + m for m, x in enumerate(self.HALF_AT) if x == at],
                [2 * (p + 1) + m for m, x in enumerate(self.SPLIT_AT) if x == at])

    def product(self, pe, m):
        k, s, (h, half) = self.k, self.s, divmod(m, 2)
        if m >= 1:
            pe.wait_ge(s("q_raw"), m)
            pe.wait_ge(s("q_cos"), m)
        sl = slice(half * BANK, (half + 1) * BANK)
        pe.matmul(k.ps[:, 7, :], k.aw[:, 0, h, :], k.cpT[:, 0, sl], start=True, stop=False)
        pe.matmul(k.ps[:, 7, :], k.aw[0:QL2, 1, h, :], k.cpT[0:QL2, 1, sl], start=False, stop=True).then_inc(s("q_prod"), 1)

    def cosine(self, dve, m):
        k, s, (h, half) = self.k, self.s, divmod(m, 2)
        sl = slice(half * BANK, (half + 1) * BANK)
        dve.wait_ge(s("q_prod"), m + 1)
        if h >= 2:
            dve.wait_ge(s("q_hi"), h - 1)
            dve.wait_ge(s("q_lo"), h - 1)
        dve.wait_ge(s("q_raw"), m + 1)
        dve.tensor_tensor(k.q1[:, h % 2, sl], k.ps[:, 7, :], k.cos[:, sl], ALU.mult).then_inc(s("q_cos"), 1)

    def raw(self, act, m):
        k, s, (h, half) = self.k, self.s, divmod(m, 2)
        act.wait_ge(s("q_prod"), m + 1)
        if h >= 2:
            act.wait_ge(s("q_swap0" if h % 2 == 0 else "q_swap1"), 32 * (h // 2))
        act.activation(k.qraw[KVL:P, h % 2, half * BANK:(half + 1) * BANK], k.ps[KVL:P, 7, :], ACT.Copy).then_inc(s("q_raw"), 1)

    def hi(self, act, h):
        k, s = self.k, self.s
        act.wait_ge(s("q_rope"), h + 1)
        act.wait_ge(s("q_cos"), 2 * h + 2)
        if h >= 4:
            act.wait_ge(s("scores"), self.PER * (h // 2 - 1))
        act.activation(k.q_hl[:, (h // 2) % 2, h % 2, 0, :], k.q1[:, h % 2, :], ACT.Copy).then_inc(s("q_hi"), 1)

    def lo(self, dve, h):
        k, s = self.k, self.s
        dve.wait_ge(s("q_hi"), h + 1)
        dve.wait_ge(s("q_rope"), h + 1)
        if h >= 4:
            dve.wait_ge(s("scores"), self.PER * (h // 2 - 1))
        dve.tensor_tensor(k.q_hl[:, (h // 2) % 2, h % 2, 1, :], k.q1[:, h % 2, :],
                          k.q_hl[:, (h // 2) % 2, h % 2, 0, :].bitcast(F32), ALU.subtract).then_inc(s("q_lo"), 1)

    def pe_first(self, pe):
        for m in range(4):
            self.product(pe, m)

    def dve_first(self, dve):
        for m in range(4):
            self.cosine(dve, m)
        for h in range(2):
            self.lo(dve, h)

    def act_first(self, act):
        for m in range(4):
            self.raw(act, m)
        for h in range(2):
            self.hi(act, h)

    def pe(self, pe, i):
        for m in self.work(i)[0]:
            self.product(pe, m)
        if i % self.PER == 0:
            pe.wait_ge(self.s("q_hi"), 2 * (i // self.PER) + 2)
            pe.wait_ge(self.s("q_lo"), 2 * (i // self.PER) + 2)

    def dve(self, dve, i):
        for m in self.work(i)[0]:
            self.cosine(dve, m)
        for h in self.work(i)[1]:
            self.lo(dve, h)

    def act(self, act, i):
        for m in self.work(i)[0]:
            self.raw(act, m)
        for h in self.work(i)[1]:
            self.hi(act, h)

    def pool(self, pool):
        k, s = self.k, self.s
        for h in range(NH):
            pool.wait_ge(s("q_swap0" if h % 2 == 0 else "q_swap1"), 32 * (h // 2 + 1))
            w = k.swp[KVL:P, h % 2, :]
            pool.tensor_tensor(w, w, k.sin[KVL:P, :], ALU.mult).then_inc(s("q_sin"), 1)
            pool.wait_ge(s("q_sin"), h + 1)
            pool.wait_ge(s("q_cos"), 2 * h + 2)
            q = k.q1[KVL:P, h % 2, :]
            pool.tensor_tensor(q, q, w, ALU.add).then_inc(s("q_rope"), 1)

    def sync(self, sp):
        k, s = self.k, self.s
        for h in range(NH):
            sp.wait_ge(s("q_raw"), 2 * h + 2)
            if h >= 2:
                sp.wait_ge(s("q_rope"), h - 1)
            sem = s("q_swap0" if h % 2 == 0 else "q_swap1")
            sp.dma_start(k.swp[KVL:KVL + 32, h % 2, :], k.qraw[KVL + 32:P, h % 2, :]).then_inc(sem, 16)
            sp.dma_start(k.swp[KVL + 32:P, h % 2, :], k.qraw[KVL:KVL + 32, h % 2, :]).then_inc(sem, 16)


def attend_b(nc, ctx, k):
    def passes(i, u, j, qt):
        q = [k.q_hl[:, (u // NT) % 2, j, part, qt * P:(qt + 1) * P] for part in range(2)]
        return [(q[0], k.k_hi), (q[0], k.k_lo), (q[1], k.k_hi)]

    attention(nc, ctx, k, "ab", 2, passes, lambda b, h: k.c_tok[:, b, :], KVL, extra=QueriesB(k))


def build(nc, io, out):
    with ExitStack() as ctx:
        k = Tensors()

        def sb(name, shape, dt=F32, c=ctx):
            t = c.enter_context(nc.sbuf_tensor(name, shape, dt))
            return t

        k.ps = ctx.enter_context(nc.psum_tensor("banks", [P, 8, BANK], F32))
        k.x = sb("x", [P, NT, D])
        k.xn = sb("xn", [P, NT, D])
        k.t_fc = sb("t_fc", [P, KO, FF], F32R)
        k.t_pr = sb("t_pr", [P, FO, D], F32R)
        k.ident = sb("ident", [P, P])
        k.ident_bf = sb("ident_bf", [P, P], BF16)
        k.mask_bf = sb("mask_bf", [P, P], BF16)
        k.cols = sb("cols", [P, 8])
        k.ones = sb("ones", [P, P])
        k.stats = sb("stats", [P, NT, 12])
        k.mv = sb("mv", [P, NT, 2])
        k.mvh = sb("mvh", [P, NT, 2])
        k.var, k.rstd, k.tmp8, k.sc_fc, k.sc_pr = (sb(n, [P, NT]) for n in ("var", "rstd", "tmp8", "sc_fc", "sc_pr"))
        k.gamma, k.thr, k.nthr, k.wsum = (sb(n, [P, 2]) for n in ("gamma", "thr", "nthr", "wsum"))
        k.big = sb("big", [P, 4])
        k.nmax = sb("nmax", [P, NT, NH])
        k.den = sb("den", [P, NT, NH])
        k.rden = sb("rden", [P, NT, NH])
        k.rT = sb("rT", [NH, S])

        with ExitStack() as a:
            k.w_o = sb("w_o_a", [P, 4, D], F32, a)
            k.v_a = sb("v_a", [P, NT, NH, 32], F32, a)
            k.qhi = sb("qhi", [P, 4, S], F32R, a)
            k.qlo = sb("qlo", [P, 4, S], F32R, a)
            k.khl = sb("khl", [P, 4, S], F32R, a)
            k.sel = sb("sel_a", [NH, 4, P], F32, a)
            with ExitStack() as w:
                k.mask = sb("mask", [P, P], F32, w)
                k.w_qkv = sb("w_qkv", [P, KO, 3 * D], F32, w)
                k.wq2 = sb("wq2", [P, KO, NH, 2, HD], F32, w)
                k.wk2 = sb("wk2", [P, KO, NH, 2, HD], F32, w)
                k.w_fc = sb("w_fc", [P, FO, D], F32, w)
                k.w_pr = sb("w_pr", [P, KO, FF], F32, w)
                k.tmp2k = sb("tmp2k", [P, 2 * S], F32, w)
                k.tern_in = lambda n, b: (k.w_fc[:, 4 * (n % 2) + b, (n // 2) * P:(n // 2 + 1) * P] if n < 4 else
                                          k.w_pr[:, b % 2, (2 * (n - 4) + b // 2) * P:(2 * (n - 4) + b // 2 + 1) * P])
                k.tern_out = lambda n: (k.t_fc[:, n // 2, BANK * (n % 2):BANK * (n % 2 + 1)] if n < 4 else
                                        k.t_pr[:, 2 * (n - 4):2 * (n - 4) + 2, :].rearrange("p a b -> p (a b)"))
                prepare(nc, ctx, k, io)
                k.xT = k.w_fc[:, :, :].rearrange("p a b -> p (a b)").rearrange("p (a b) -> p a b", a=KO)
                k.khi = sb("khi", [P, 2, BANK], F32R, w)
                k.tmp512 = k.tmp2k[:, 0:BANK]
                project_a(nc, ctx, k)
            k.qm = sb("qm", [P, 2, 2, 4, P], F32R, a)
            k.prob = sb("prob_a", [P, 3, S], F32, a)
            k.pT = sb("pT_a", [P, 2, 4, S], F32, a)
            k.oT = sb("oT_a", [P, 4, S], F32, a)
            attend_a(nc, ctx, k)
            s = Stage(ctx, nc, "sel")
            with nc.Block() as block:
                @block.sync
                def _(sp):
                    sp.dma_start(k.sel[:, :, :], io["sel_a"]).then_inc(s("sel"), 16)
                    sp.wait_ge(s("sel"), 16)
            finish_attention(nc, ctx, k, "fa", 4, k.sel, k.w_o, lambda dve, c: ffn_norm(dve, c, k))

        with ExitStack() as f:
            alloc_ffn(k, lambda n, sh, dt=F32: sb(n + "_1", sh, dt, f))
            ffn(nc, ctx, k, "f1", out if io.get("stop") == 1 else None)
        if io.get("stop") == 1:
            return

        with ExitStack() as b:
            k.aw = sb("aw", [P, 2, NH, P], F32, b)
            k.w_vo = sb("w_vo", [P, NH // 2, D], F32, b)
            k.cpT = sb("cpT", [P, 2, S], F32, b)
            k.k_hi, k.k_lo = sb("k_hi", [P, S], F32R, b), sb("k_lo", [P, S], F32R, b)
            k.c_tok = sb("c_tok", [P, NT, KVL], F32, b)
            k.cos, k.sin = sb("cos", [P, S], F32, b), sb("sin", [P, S], F32, b)
            k.sel_b = sb("sel_b", [NH, NH // 2, P], F32, b)
            k.row = sb("row", [1, D], F32, b)
            k.swp = sb("swp", [P, 2, S], F32, b)
            with ExitStack() as w:
                k.xT = sb("xT_b", [P, KO, S], F32, w)
                k.w_ob = sb("w_ob", [P, NH, D], F32, w)
                with ExitStack() as v:
                    k.w_qc = sb("w_qc", [P, 2, NH * DK], F32, v)
                    k.w_qr = sb("w_qr", [P, 2, NH * DR], F32, v)
                    k.w_kc, k.w_v = sb("w_kc", [KVL, NH * DK], F32, v), sb("w_v", [KVL, NH * DV], F32, v)
                    k.w_cp = sb("w_cp", [P, KO, QL], F32, v)
                    k.w_ck = sb("w_ck", [P, KO, P], F32, v)
                    k.w_kr = sb("w_kr", [P, KO, DR], F32, v)
                    load_b(nc, ctx, k, io)
                    k.wT = sb("wT", [P, NH, QL + 2 * KVL], F32, v)
                    k.kraw, k.key = sb("kraw", [P, S], F32, v), sb("key", [P, S], F32, v)
                    prepare_b(nc, ctx, k)
                J = IH * TOPK
                k.w_gate, k.w_idx, k.w_s = (sb("w_gate", [P, KO, IH], F32, w), sb("w_idx", [P, KO, IH * P], F32, w),
                                            sb("w_s", [P, 4, P], F32, w))
                k.small = sb("small", [P, 24 + J], F32, w)
                k.gT, k.top, k.top_at = sb("gT", [IH, S], F32, w), sb("top", [IH, 8], F32, w), sb("top_at", [IH, 8], mybir.dt.uint32, w)
                k.bd, k.onehot, k.xsel = sb("bd", [IH, IH, TOPK], F32, w), sb("onehot", [P, NT, J], F32, w), sb("xsel", [P, KO, J], F32, w)
                k.sel, k.sqk, k.sv = sb("sel", [P, J], F32, w), sb("sqk", [P, 2 * J], F32, w), sb("sv", [J, P], F32, w)
                k.sprob, k.scol, k.chain = sb("sprob", [J, J], F32, w), sb("scol", [P, 4], F32, w), sb("chain", [P, 24], F32, w)
                sparse_b(nc, ctx, k, io)
            k.qraw = k.xn[:, :, :].rearrange("p a b -> p (a b)").rearrange("p (a b) -> p a b", a=2)
            k.q1 = sb("q1", [P, 2, S], F32, b)
            k.q_hl = sb("q_hl", [P, 2, 2, 2, S], F32R, b)
            k.prob = sb("prob_b", [P, 3, S], F32, b)
            k.pT = sb("pT_b", [P, 2, 2, S], F32, b)
            k.oT = sb("oT_b", [P, NH // 2, S], F32, b)
            attend_b(nc, ctx, k)
            finish_attention(nc, ctx, k, "fb", NH // 2, k.sel_b, k.w_vo, lambda dve, c: ffn_norm(dve, c, k), row=k.row[:, :])

        with ExitStack() as f:
            alloc_ffn(k, lambda n, sh, dt=F32: sb(n + "_2", sh, dt, f))
            ffn(nc, ctx, k, "f2", out)


def alloc_ffn(k, sb):
    k.xqT = sb("xqT", [P, 3, 2, KO, P], F32R)
    k.h = sb("h", [P, 2, FF])
    k.hc = sb("hc", [P, 2, FF])
    k.hT = sb("hT", [P, 2, 2, FO, P], F32R)
    k.o_raw = sb("o_raw", [P, NT, D])
    k.nmean = sb("nmean", [P, NT])


def constants():
    c = {"ident": np.eye(P, dtype=np.float32)}
    q, kk = np.arange(P)[:, None], np.arange(P)[None, :]
    c["mask"] = np.where(kk > q, np.float32(-1e30), np.float32(0)).astype(np.float32)
    cols = np.zeros((P, 8), np.float32)
    odd = (np.arange(P) // HD) % 2
    cols[:, 0], cols[:, 1] = odd, 1 - 2 * odd
    for j in range(4):
        cols[32 * j:32 * j + 32, 4 + j] = 1
    c["cols"] = cols
    sel = np.zeros((NH, 4, P), np.float32)
    for g in range(4):
        for j in range(4):
            sel[4 * g + j, g, 32 * j:32 * j + 32] = 1
    c["sel_a"] = sel
    sel = np.zeros((NH, NH // 2, P), np.float32)
    for h in range(NH):
        sel[h, h // 2, KVL * (h % 2):KVL * (h % 2 + 1)] = 1
    c["sel_b"] = sel
    inv = 1.0 / 10000.0 ** (np.arange(0, DR, 2)[:DR // 2].astype(np.float32) / DR)
    freqs = np.outer(np.arange(S, dtype=np.float32), inv)
    root = (DK + DR) ** -0.25
    cos, sin = np.cos(freqs).T, np.sin(freqs).T
    c["cos"] = (np.concatenate([np.ones((KVL, S)), cos, cos]) * root).astype(np.float32)
    c["sin"] = (np.concatenate([np.zeros((KVL, S)), -sin, sin]) * root).astype(np.float32)
    J = IH * TOPK
    small = np.zeros((P, 24 + J), np.float32)
    small[:IH, :IH] = np.eye(IH)
    small[:J, 8:16] = np.repeat(np.eye(IH), TOPK, axis=0) / TOPK
    small[:, 16:24] = np.arange(S).reshape(NT, P).T
    head = np.arange(J) // TOPK
    small[:J, 24:] = np.where(head[:, None] == head[None, :], 0, np.float32(-1e30))
    c["small"] = small
    return c


_INS = ["L0_attn_a_x", "L0_attn_a_Wqkv", "L0_attn_a_Wo", "L0_attn_b_W_c", "L0_attn_b_W_cp", "L0_attn_b_W_qc",
        "L0_attn_b_W_qr", "L0_attn_b_W_kc", "L0_attn_b_W_kr", "L0_attn_b_W_v", "L0_attn_b_W_o", "L0_attn_b_W_idx",
        "L0_attn_b_W_gate", "L0_attn_b_W_sq", "L0_attn_b_W_sk", "L0_attn_b_W_sv", "L0_attn_b_W_iout",
        "L0_ffn_w_fc", "L0_ffn_w_proj"]


def kernel(**inputs):
    import numpy as _np
    import concourse.bacc as _bacc
    from concourse import mybir as _mybir
    from concourse.bass_utils import run_bass_kernel_spmd as _run

    nc = _bacc.Bacc("TRN2", target_bir_lowering=False, num_devices=1)
    arrays, io = {}, {}
    for name, a in [(n, _np.ascontiguousarray(inputs[n])) for n in _INS] + list(constants().items()):
        arrays[f"in_{name}"] = a
        io[name] = nc.dram_tensor(f"in_{name}", a.shape, _mybir.dt.from_np(a.dtype), kind="ExternalInput").ap()
    out = nc.dram_tensor("out", (1, S, D), F32, kind="ExternalOutput").ap()
    build(nc, io, out)
    r = _run(nc, [arrays], core_ids=[0])
    return r.results[0]["out"]
```

```python
from contextlib import ExitStack

import concourse.bass as bass
from concourse import mybir
from concourse.alu_op_type import AluOpType as ALU
import numpy as np

ACT = mybir.ActivationFunctionType
AX = mybir.AxisListType
F32 = mybir.dt.float32
F32R = mybir.dt.float32r
BF16 = mybir.dt.bfloat16
I32 = mybir.dt.int32

P = 128
S = 1024
D = 256
NT = S // P
KO = D // P
NH = 16
HD = 16
FF = 4 * D
FO = FF // P
BANK = 512
QL, KVL = 192, 64
QL2 = QL - P
DK, DR, DV = 128, 64, 128
IH, TOPK = 8, 8
RSQRT_SEED = float(0x5F3759DF)


class Tensors:
    pass


class Stage:

    def __init__(self, ctx, nc, name):
        self.ctx, self.nc, self.name, self.made = ctx, nc, name, {}

    def __call__(self, what):
        if what not in self.made:
            self.made[what] = self.ctx.enter_context(self.nc.semaphore(f"{self.name}_{what}"))
        return self.made[what]


class Chain:

    def __init__(self, eng, sem):
        self.eng, self.sem, self.n = eng, sem, 0

    def step(self, ins):
        self.n += 1
        ins.then_inc(self.sem, 1)
        self.eng.wait_ge(self.sem, self.n)


def rsqrt(dve, chain, y, t, v):
    chain.step(dve.tensor_scalar(y.bitcast(I32), v.bitcast(I32), -0.5, RSQRT_SEED, ALU.mult, ALU.add))
    for _ in range(4):
        chain.step(dve.tensor_tensor(t, y, y, ALU.mult))
        chain.step(dve.scalar_tensor_tensor(out=t, in0=t, scalar=-0.5, in1=v, op0=ALU.mult, op1=ALU.mult))
        chain.step(dve.scalar_tensor_tensor(out=y, in0=t, scalar=1.5, in1=y, op0=ALU.add, op1=ALU.mult))


def layer_stats(dve, chain, k, x):
    for t in range(NT):
        chain.step(dve.bn_stats(k.stats[:, t, 0:6], x[:, t, :]))
        chain.step(dve.bn_aggr(k.mv[:, t, :], k.stats[:, t, 0:6]))


def prepare(nc, ctx, k, io):
    s = Stage(ctx, nc, "prep")
    with nc.Block() as block:

        @block.sync
        def _(sp):
            sp.dma_start(k.x[:, :, :], io["L0_attn_a_x"].rearrange("a (t p) d -> p (a t) d", p=P)).then_inc(s("x"), 16)
            sp.dma_start(k.ident[:, :], io["ident"]).then_inc(s("const"), 16)
            sp.dma_start(k.mask[:, :], io["mask"]).then_inc(s("const"), 16)
            sp.dma_start(k.cols[:, :], io["cols"]).then_inc(s("const"), 16)
            sp.dma_start(k.w_qkv[:, :, :], io["L0_attn_a_Wqkv"].rearrange("(a p) n -> p a n", p=P)).then_inc(s("const"), 16)
            sp.dma_start(k.sel_f[:, :, :], io["sel"]).then_inc(s("sel"), 16)
            sp.wait_ge(s("wo_zero"), 1)
            for j in range(4):
                src = io["L0_attn_a_Wo"].rearrange("(g j d) n -> j d g n", j=4, d=HD)[j]
                sp.dma_start(k.w_o[32 * j:32 * j + HD, :, :], src).then_inc(s("const"), 16)

        @block.scalar
        def _(act):
            act.dma_start(k.w_fc[:, :, :], io["L0_ffn_w_fc"].rearrange("(t p) n -> p t n", p=P)).then_inc(s("w_fc"), 16)
            act.dma_start(k.w_pr[:, :, :], io["L0_ffn_w_proj"].rearrange("(t p) n -> p t n", p=P)).then_inc(s("w_pr"), 16)
            for n in range(8):
                act.wait_ge(s("w_turned"), n + 1)
                act.activation(k.tern_out(n), k.ps[:, n % 4, :], ACT.Copy).then_inc(s("w_out"), 1)

        @block.gpsimd
        def _(pool):
            pool.memset(k.w_o[:, :, :], 0.0).then_inc(s("wo_zero"), 1)
            pool.memset(k.v_a[:, :, :, :], 0.0).then_inc(s("v_zero"), 1)
            pool.memset(k.ones[:, :], 1.0).then_inc(s("ones"), 1)
            pool.wait_ge(s("const"), 16 * 8)
            pool.wait_ge(s("sel"), 16)
            pool.tensor_copy(k.sel_bf[:, :, :], k.sel_f[:, :, :]).then_inc(s("sel_out"), 1)
            for n, w in enumerate((k.wq2, k.wk2)):
                for dup in range(2):
                    for a in range(KO):
                        pool.tensor_copy(w[:, a, :, dup, :],
                                         k.w_qkv[:, a, n * D:(n + 1) * D].rearrange("p (h d) -> p h d", d=HD)).then_inc(s("w_dup"), 1)

        @block.vector
        def _(dve):
            c = Chain(dve, s("dve"))
            dve.wait_ge(s("const"), 16 * 8)
            c.step(dve.tensor_copy(k.ident_bf[:, :], k.ident[:, :]))
            c.step(dve.tensor_copy(k.mask_bf[:, :], k.mask[:, :]))
            dve.wait_ge(s("x"), 16)
            layer_stats(dve, c, k, k.x)
            dve.wait_ge(s("w_fc"), 16)
            dve.wait_ge(s("w_pr"), 16)
            for n, w in enumerate((k.w_fc, k.w_pr)):
                dve.tensor_reduce(k.wsum[:, n:n + 1], w[:, :, :].rearrange("p a b -> p (a b)"), AX.X, ALU.add,
                                  apply_absolute_value=True).then_inc(s("wsum"), 1)
            dve.wait_ge(s("gamma"), 1)
            c.step(dve.tensor_scalar(k.gamma[:, :], k.ps[:, 7, 0:2], 1.0 / (FF * D), None, ALU.mult))
            c.step(dve.tensor_scalar(k.thr[:, :], k.gamma[:, :], 1e-6, 0.5, ALU.add, ALU.mult))
            c.step(dve.tensor_scalar(k.nthr[:, :], k.thr[:, :], -1.0, None, ALU.mult))
            for n, w in enumerate((k.w_fc, k.w_pr)):
                flat = w[:, :, :].rearrange("p a b -> p (a b)")
                c.step(dve.tensor_scalar(k.tmp2k[:, :], flat, k.nthr[:, n:n + 1], None, ALU.is_lt))
                dve.scalar_tensor_tensor(out=flat, in0=flat, scalar=k.thr[:, n:n + 1], in1=k.tmp2k[:, :],
                                         op0=ALU.is_gt, op1=ALU.subtract).then_inc(s("tern"), 1)
                dve.wait_ge(s("tern"), n + 1)
            c.step(dve.tensor_scalar(k.var[:, :], k.mv[:, :, 1], 1e-5, None, ALU.add))
            rsqrt(dve, c, k.rstd[:, :], k.tmp8[:, :], k.var[:, :])
            for t in range(NT):
                c.step(dve.tensor_scalar(k.xn[:, t, :], k.x[:, t, :], k.mv[:, t, 0:1], k.rstd[:, t:t + 1],
                                         ALU.subtract, ALU.mult))

        @block.tensor
        def _(pe):
            pe.wait_ge(s("wsum"), 2)
            pe.wait_ge(s("ones"), 1)
            pe.matmul(k.ps[:, 7, 0:2], k.ones[:, :], k.wsum[:, :], start=True, stop=True).then_inc(s("gamma"), 1)
            pe.wait_ge(s("const"), 16 * 8)
            for n in range(8):
                pe.wait_ge(s("tern"), 1 if n < 4 else 2)
                if n >= 4:
                    pe.wait_ge(s("w_out"), n - 3)
                for b in range(4):
                    ins = pe.transpose(k.ps[:, n % 4, b * P:(b + 1) * P], k.tern_in(n, b), k.ident[:, :])
                ins.then_inc(s("w_turned"), 1)


def turn_x(pe, k, s, t):
    for a in range(KO):
        ins = pe.transpose(k.ps[:, t % 4, a * P:(a + 1) * P], k.xn[:, t, a * P:(a + 1) * P], k.ident[:, :])
    ins.then_inc(s("turned"), 1)


def project_a(nc, ctx, k):
    s = Stage(ctx, nc, "pa")
    jobs = [("k", g, h) for g in range(4) for h in range(2)] + [("q", g, h) for g in range(4) for h in range(2)]
    with nc.Block() as block:

        @block.tensor
        def _(pe):
            for t in range(NT):
                if t >= 4:
                    pe.wait_ge(s("xT"), t - 3)
                turn_x(pe, k, s, t)
            pe.wait_ge(s("xT"), NT)
            for n, (what, g, half) in enumerate(jobs):
                w = k.wk2 if what == "k" else k.wq2
                if n >= 4:
                    pe.wait_ge(s("hi"), n - 3)
                    pe.wait_ge(s("lo"), n - 3)
                for a in range(KO):
                    ins = pe.matmul(k.ps[:, n % 4, :], w[:, a, 4 * g:4 * g + 4, :, :].rearrange("p h u d -> p (h u d)"),
                                    k.xT[:, a, half * BANK:(half + 1) * BANK], start=(a == 0), stop=(a == KO - 1))
                ins.then_inc(s("proj"), 1)
            for t in range(NT):
                if t >= 4:
                    pe.wait_ge(s("v"), t - 3)
                for a in range(KO):
                    ins = pe.matmul(k.ps[:, 4 + t % 4, 0:D], k.xT[:, a, t * P:(t + 1) * P], k.w_qkv[:, a, 2 * D:3 * D],
                                    start=(a == 0), stop=(a == KO - 1))
                ins.then_inc(s("vproj"), 1)

        @block.scalar
        def _(act):
            for t in range(NT):
                act.wait_ge(s("turned"), t + 1)
                act.activation(k.xT[:, :, t * P:(t + 1) * P], k.ps[:, t % 4, 0:D].rearrange("p (a n) -> p a n", a=KO),
                               ACT.Copy).then_inc(s("xT"), 1)
            for n, (what, g, half) in enumerate(jobs):
                act.wait_ge(s("proj"), n + 1)
                sl = slice(half * BANK, (half + 1) * BANK)
                if what == "k":
                    if n >= 2:
                        act.wait_ge(s("lo"), n - 1)
                    act.activation(k.khi[:, n % 2, :], k.ps[:, n % 4, :], ACT.Copy).then_inc(s("hi"), 1)
                else:
                    act.activation(k.qhi[:, g, sl], k.ps[:, n % 4, :], ACT.Copy, scale=float(HD) ** -0.5).then_inc(s("hi"), 1)
            for t in range(NT):
                act.wait_ge(s("vproj"), t + 1)
                act.activation(k.v_a[:, t, :, 0:HD], k.ps[:, 4 + t % 4, 0:D].rearrange("p (h d) -> p h d", d=HD),
                               ACT.Copy).then_inc(s("v"), 1)

        @block.vector
        def _(dve):
            c = Chain(dve, s("dve"))
            for n, (what, g, half) in enumerate(jobs):
                dve.wait_ge(s("proj"), n + 1)
                dve.wait_ge(s("hi"), n + 1)
                sl = slice(half * BANK, (half + 1) * BANK)
                if what == "k":
                    hi = k.khi[:, n % 2, :].bitcast(F32)
                    c.step(dve.tensor_scalar(k.tmp512[:, :], hi, k.cols[:, 1:2], None, ALU.mult))
                    dve.scalar_tensor_tensor(out=k.khl[:, g, sl], in0=k.ps[:, n % 4, :], scalar=k.cols[:, 0:1],
                                             in1=k.tmp512[:, :], op0=ALU.mult, op1=ALU.add).then_inc(s("lo"), 1)
                    dve.wait_ge(s("lo"), n + 1)
                else:
                    dve.scalar_tensor_tensor(out=k.qlo[:, g, sl], in0=k.ps[:, n % 4, :], scalar=float(HD) ** -0.5,
                                             in1=k.qhi[:, g, sl].bitcast(F32), op0=ALU.mult, op1=ALU.subtract).then_inc(s("lo"), 1)


def attention(nc, ctx, k, name, hu, passes, value, width, lag_short, pool_unit=None, extra=None):
    s = Stage(ctx, nc, name)
    units = [(g, qt) for g in range(NH // hu) for qt in range(NT)]
    steps = [(u, j) for u in range(len(units)) for j in range(hu)]
    qt_of = [units[u][1] for u, _ in steps]
    n_ch = [1 if q < 4 else 2 for q in qt_of]
    first_ch = [sum(n_ch[:i]) for i in range(len(steps) + 1)]
    NS = len(steps)
    turn_steps, n = [], 0
    while n < NS:
        i = len(turn_steps)
        m = max(n, min(NS, i + 1 - (lag_short if i < NS and n_ch[i] == 1 else 2)))
        turn_steps.append(range(n, m))
        n = m
    turned_at = {i2: i for i, r in enumerate(turn_steps) for i2 in r}
    pv_round = [turned_at[hu * u + hu - 1] + 2 for u in range(len(units))]
    for u in reversed(range(len(units) - 2)):
        pv_round[u] = min(pv_round[u], turned_at[hu * (u + 2)] - 1, pv_round[u + 1] - 1)
    pv_at = {r: u for u, r in enumerate(pv_round)}
    rounds = max(pv_at) + 2

    def turns(i):
        return turn_steps[i] if i < len(turn_steps) else ()

    def scores_of(i):
        return k.ps[:, first_ch[i] % 4:first_ch[i] % 4 + n_ch[i], :].rearrange("p a b -> p (a b)")[:, 0:(qt_of[i] + 1) * P]

    def probs_of(i, c0, c1):
        at = (first_ch[i] % 6) * BANK
        return k.prob[:, :, :].rearrange("p a b -> p (a b)")[:, at + c0:at + c1]

    if extra is not None:
        extra.bind(s, steps, units)

    def even(n):
        return (n + 1) // 2

    def odd(n):
        return n // 2

    with nc.Block() as block:

        @block.tensor
        def _(pe):
            if extra is not None:
                extra.pe_first(pe)
            for i in range(rounds):
                if i < NS:
                    u, j = steps[i]
                    qt = qt_of[i]
                    if extra is not None:
                        extra.pe(pe, i)
                    if pool_unit is not None:
                        pe.wait_ge(s("q_masked"), 2 * (u + 1))
                    before = sum(1 for m in range(i) if first_ch[m] < first_ch[i + 1] - 4)
                    if before:
                        pe.wait_ge(s("exp"), before)
                    nk = (qt + 1) * P
                    for c0 in range(0, nk, BANK):
                        n = min(BANK, nk - c0)
                        out = k.ps[:, first_ch[i] % 4 + c0 // BANK, 0:n]
                        last = c0 + n == nk
                        ps = passes(i, u, j, qt)
                        for m, (q, kk) in enumerate(ps):
                            ins = pe.matmul(out, q, kk[:, c0:c0 + n], start=(m == 0), stop=(m == len(ps) - 1 and not last))
                        if last:
                            ins = pe.matmul(out[:, n - P:n], k.ident_bf[:, :], k.mask_bf[:, :], start=False, stop=True)
                    ins.then_inc(s("scores"), 1)
                for i2 in turns(i):
                    pe.wait_ge(s("exp"), i2 + 1)
                    for ch in range(n_ch[i2]):
                        n = first_ch[i2] + ch
                        if n >= 2:
                            pe.wait_ge(s("out_even" if n % 2 == 0 else "out_odd"), n // 2)
                        for b in range(4 * ch, min(4 * ch + 4, qt_of[i2] + 1)):
                            ins = pe.transpose(k.ps[:, 4 + n % 2, (b % 4) * P:(b % 4 + 1) * P],
                                               probs_of(i2, b * P, (b + 1) * P), k.ident[:, :])
                        ins.then_inc(s("turned"), 1)
                if i in pv_at:
                    u = pv_at[i]
                    g, qt = units[u]
                    n = first_ch[hu * u + hu]
                    pe.wait_ge(s("out_even"), even(n))
                    pe.wait_ge(s("out_odd"), odd(n))
                    if u >= 1:
                        pe.wait_ge(s("o_out"), u)
                    for b in range(qt + 1):
                        for jj in range(hu):
                            ins = pe.matmul(k.ps[width * jj:width * (jj + 1), 6, 0:P], value(b, g * hu + jj),
                                            k.pT[:, u % 2, jj, b * P:(b + 1) * P], start=(b == 0), stop=(b == qt))
                    ins.then_inc(s("pv"), 1)

        def take_out(eng, i2, parity, copy):
            u, j = steps[i2]
            for ch in range(n_ch[i2]):
                n = first_ch[i2] + ch
                if n % 2 != parity:
                    continue
                eng.wait_ge(s("turned"), n + 1)
                if u >= 2:
                    eng.wait_ge(s("pv"), u - 1)
                w = (min(4 * ch + 4, qt_of[i2] + 1) - 4 * ch) * P
                copy(k.pT[:, u % 2, j, ch * BANK:ch * BANK + w], k.ps[:, 4 + parity, 0:w])

        @block.vector
        def _(dve):
            if extra is not None:
                extra.dve_first(dve)
            for i in range(rounds):
                if i < NS:
                    dve.wait_ge(s("scores"), i + 1)
                    u, j = steps[i]
                    dve.tensor_reduce(k.nmax[:, qt_of[i], units[u][0] * hu + j:units[u][0] * hu + j + 1], scores_of(i), AX.X, ALU.max,
                                      negate=True).then_inc(s("max"), 1)
                for i2 in turns(i):
                    take_out(dve, i2, 1, lambda o, a: dve.tensor_copy(o, a).then_inc(s("out_odd"), 1))
                if i - 1 in pv_at:
                    u = pv_at[i - 1]
                    g, qt = units[u]
                    dve.wait_ge(s("pv"), u + 1)
                    dve.tensor_copy(k.oT[:, g, qt * P:(qt + 1) * P], k.ps[:, 6, 0:P]).then_inc(s("o_out"), 1)
                if extra is not None and i < NS:
                    extra.dve(dve, i)

        @block.scalar
        def _(act):
            if extra is not None:
                extra.act_first(act)
            for i in range(rounds):
                for i2 in turns(i):
                    take_out(act, i2, 0, lambda o, a: act.activation(o, a, ACT.Copy).then_inc(s("out_even"), 1))
                if i < NS:
                    nk = (qt_of[i] + 1) * P
                    u, j = steps[i]
                    h = units[u][0] * hu + j
                    act.wait_ge(s("max"), i + 1)
                    if first_ch[i + 1] > 6:
                        act.wait_ge(s("turned"), first_ch[i + 1] - 6)
                    act.activation(probs_of(i, 0, nk), scores_of(i), ACT.Exp, bias=k.nmax[:, qt_of[i], h:h + 1],
                                   accum_out=k.den[:, qt_of[i], h:h + 1]).then_inc(s("exp"), 1)
                if extra is not None and i < NS:
                    extra.act(act, i)

        if pool_unit is not None:
            @block.gpsimd
            def _(pool):
                for u, (g, qt) in enumerate(units):
                    if u >= 2:
                        pool.wait_ge(s("scores"), hu * (u - 1))
                    pool_unit(pool, s, u, g, qt)
        if extra is not None:
            @block.gpsimd
            def _(pool):
                extra.pool(pool)

            @block.sync
            def _(sp):
                extra.sync(sp)


def attend_a(nc, ctx, k):
    def masked(pool, s, u, g, qt):
        for part, q in enumerate((k.qhi, k.qlo)):
            src = q[:, g, qt * P:(qt + 1) * P].bitcast(F32).unsqueeze(1).broadcast_to([P, 4, P])
            row = k.cols[:, 4:8].unsqueeze(2).broadcast_to([P, 4, P])
            pool.tensor_tensor(k.qm[:, u % 2, part, :, :], src, row, ALU.mult).then_inc(s("q_masked"), 1)

    def passes(i, u, j, qt):
        g = u // NT
        return [(k.qm[:, u % 2, part, j, :], k.khl[:, g, :]) for part in range(2)]

    attention(nc, ctx, k, "aa", 4, passes, lambda b, h: k.v_a[:, b, h, :], 32, 3, pool_unit=masked)


def finish_attention(nc, ctx, k, name, ng, sel, norm, row=None):
    s = Stage(ctx, nc, name)
    spread = [(half, g) for half in range(2) for g in range(ng)]
    per_tile = ng // 4
    with nc.Block() as block:

        @block.tensor
        def _(pe):
            def spread_product(n):
                half, g = spread[n]
                if n >= 4:
                    pe.wait_ge(s("o_norm"), n - 3)
                pe.matmul(k.ps[:, n % 4, :], sel[:, g, :], k.rT[:, half * BANK:(half + 1) * BANK],
                          start=True, stop=True).then_inc(s("spread"), 1)

            def project(t):
                done = ng if t < 4 else 2 * ng
                pe.wait_ge(s("o_hi"), done)
                pe.wait_ge(s("o_lo"), done)
                if t >= 2:
                    pe.wait_ge(s("x_new"), t - 1)
                for g in range(ng):
                    for m, (o, w) in enumerate(((k.o_hi, k.wo_hi), (k.o_lo, k.wo_hi), (k.o_hi, k.wo_lo))):
                        ins = pe.matmul(k.ps[:, 4 + t % 2, 0:D], o[:, g, t * P:(t + 1) * P], w[:, g, :],
                                        start=(g == 0 and m == 0), stop=(g == ng - 1 and m == 2 and row is None))
                if row is not None:
                    ins = pe.matmul(k.ps[:, 4 + t % 2, 0:D], k.ones[0:1, :], row, start=False, stop=True)
                ins.then_inc(s("proj"), 1)

            pe.wait_ge(s("parts"), 1)
            turned = k.ps[0:96, 6, :].bitcast(BF16)
            for t in range(NT):
                ins = pe.transpose(turned[:, t * P:(t + 1) * P], k.r3[:, t, :], k.ident_bf[:, :])
            ins.then_inc(s("rT"), 1)
            pe.wait_ge(s("rT_out"), 1)
            for n in range(ng):
                spread_product(n)
            for n in range(ng, ng + per_tile):
                spread_product(n)
            pe.wait_ge(s("w_hi"), 1)
            pe.wait_ge(s("w_lo"), 1)
            for t in range(NT):
                project(t)
                if t < 3:
                    for n in range(ng + (t + 1) * per_tile, ng + (t + 2) * per_tile):
                        spread_product(n)

        @block.scalar
        def _(act):
            act.activation(k.wo_hi[:, :, :], k.w_out[:, :, :], ACT.Copy).then_inc(s("w_hi"), 1)
            act.wait_ge(s("rT"), 1)
            act.activation(k.rT[:, :], k.ps[0:96, 6, :].bitcast(BF16), ACT.Copy).then_inc(s("rT_out"), 1)
            for n, (half, g) in enumerate(spread):
                sl = slice(half * BANK, (half + 1) * BANK)
                act.wait_ge(s("o_norm"), n + 1)
                act.activation(k.o_hi[:, g, sl], k.oT[:, g, sl], ACT.Copy).then_inc(s("o_hi"), 1)

        @block.gpsimd
        def _(pool):
            pool.memset(k.r3[:, :, :], 0.0).then_inc(s("r3_zero"), 1)
            pool.wait_ge(s("w_hi"), 1)
            pool.tensor_tensor(k.wo_lo[:, :, :], k.w_out[:, :, :], k.wo_hi[:, :, :].bitcast(F32), ALU.subtract).then_inc(s("w_lo"), 1)
            for n, (half, g) in enumerate(spread):
                sl = slice(half * BANK, (half + 1) * BANK)
                pool.wait_ge(s("o_hi"), n + 1)
                pool.tensor_tensor(k.o_lo[:, g, sl], k.oT[:, g, sl], k.o_hi[:, g, sl].bitcast(F32), ALU.subtract).then_inc(s("o_lo"), 1)

        @block.vector
        def _(dve):
            c = Chain(dve, s("dve"))

            def normalise(n):
                half, g = spread[n]
                o = k.oT[:, g, half * BANK:(half + 1) * BANK]
                dve.wait_ge(s("spread"), n + 1)
                dve.tensor_tensor(o, k.ps[:, n % 4, :], o, ALU.mult).then_inc(s("o_norm"), 1)

            def add(t):
                dve.wait_ge(s("proj"), t + 1)
                dve.tensor_tensor(k.x[:, t, :], k.ps[:, 4 + t % 2, 0:D], k.x[:, t, :], ALU.add).then_inc(s("x_new"), 1)
                dve.wait_ge(s("x_new"), t + 1)
                c.step(dve.bn_stats(k.stats[:, t, 0:6], k.x[:, t, :]))
                c.step(dve.bn_aggr(k.mv[:, t, :], k.stats[:, t, 0:6]))

            dve.wait_ge(s("r3_zero"), 1)
            c.step(dve.reciprocal(k.den[:, :, :], k.den[:, :, :]))
            for part in range(3):
                r = k.r3[:, :, 32 * part:32 * part + NH]
                if part == 2:
                    dve.tensor_copy(r, k.den[:, :, :]).then_inc(s("parts"), 1)
                else:
                    c.step(dve.tensor_copy(r, k.den[:, :, :]))
                    c.step(dve.tensor_tensor(k.den[:, :, :], k.den[:, :, :], r, ALU.subtract))
            for n in range(ng + per_tile):
                normalise(n)
            for t in range(NT):
                if t < 3:
                    for n in range(ng + (t + 1) * per_tile, ng + (t + 2) * per_tile):
                        normalise(n)
                add(t)
            norm(dve, c)


def ffn_norm(dve, c, k):
    e1, e2 = 1e-5, 1e-6
    c.step(dve.tensor_scalar(k.var[:, :], k.mv[:, :, 1], 1.0 + e2, e1 * e2, ALU.mult, ALU.add))
    rsqrt(dve, c, k.rstd[:, :], k.tmp8[:, :], k.var[:, :])
    c.step(dve.tensor_scalar(k.sc_fc[:, :], k.rstd[:, :], k.gamma[:, 0:1], None, ALU.mult))


def ffn(nc, ctx, k, name, out=None, beside=None):
    s = Stage(ctx, nc, name)
    def x_turn(t):
        return t + 2 * max(0, t - 3)

    def hidden_turn(t):
        return min(t + 4, NT) + 2 * t

    def turned_parts(t):
        if t < NT:
            yield x_turn(t), k.xqT[:, t % 2], KO, 0, None
        if t >= 2:
            for c in range(2):
                yield hidden_turn(t - 2) + c, k.hT[:, (t - 2) % 2], 4, 4 * c, t - 2

    def dst(buf, part, w, b0):
        return buf[:, part, b0:b0 + w, :].rearrange("p a b -> p (a b)")

    def free_to_write(eng, t, hid):
        if hid is None:
            if t >= 2:
                eng.wait_ge(s("fc"), t - 1)
        elif hid >= 2:
            eng.wait_ge(s("proj"), hid - 1)

    def dst(buf, part, w, b0):
        return buf[:, part, b0:b0 + w, :].rearrange("p a b -> p (a b)")

    def chunks(t):
        return [(hidden_turn(t) + c, k.hT[:, t % 2], 4 * c) for c in range(2)]

    with nc.Block() as block:

        @block.tensor
        def _(pe):
            def turn(n, src, w):
                if n >= 3:
                    pe.wait_ge(s("hi"), n - 2)
                    pe.wait_ge(s("lo"), n - 2)
                for b in range(w):
                    ins = pe.transpose(k.ps[:, 4 + n % 3, b * P:(b + 1) * P], src[:, b * P:(b + 1) * P], k.ident[:, :])
                ins.then_inc(s("turned"), 1)

            def fc(t):
                pe.wait_ge(s("hi"), x_turn(t) + 1)
                pe.wait_ge(s("lo"), x_turn(t) + 1)
                if t >= 2:
                    pe.wait_ge(s("gelu"), t - 1)
                for n in range(2):
                    for m, (part, a) in enumerate([(part, a) for part in range(2) for a in range(KO)]):
                        ins = pe.matmul(k.ps[:, 2 * (t % 2) + n, :], k.xqT[:, t % 3, part, a, :],
                                        k.t_fc[:, a, n * BANK:(n + 1) * BANK], start=(m == 0), stop=(m == 2 * KO - 1))
                ins.then_inc(s("fc"), 1)

            def proj(t):
                pe.wait_ge(s("hi"), hidden_turn(t) + 2)
                pe.wait_ge(s("lo"), hidden_turn(t) + 2)
                if t >= 1:
                    pe.wait_ge(s("o_raw"), t)
                for f in range(FO):
                    for part in range(2):
                        ins = pe.matmul(k.ps[:, 7, 0:D], k.hT[:, t % 2, part, f, :], k.t_pr[:, f, :],
                                        start=(f == 0 and part == 0), stop=(f == FO - 1 and part == 1))
                ins.then_inc(s("proj"), 1)

            for t in range(NT + 4):
                if t < NT:
                    pe.wait_ge(s("x_clip"), t + 1)
                    turn(x_turn(t), k.xn[:, t, :], KO)
                if 2 <= t < NT + 2:
                    fc(t - 2)
                if 3 <= t < NT + 3:
                    pe.wait_ge(s("h_clip"), t - 2)
                    for c in range(2):
                        turn(hidden_turn(t - 3) + c, k.hc[:, (t - 3) % 2, c * BANK:(c + 1) * BANK], 4)
                if t >= 4:
                    proj(t - 4)

        @block.scalar
        def _(act):
            def hi(n, buf, w, b0):
                act.wait_ge(s("turned"), n + 1)
                act.activation(dst(buf, 0, w, b0), k.ps[:, 4 + n % 3, 0:w * P], ACT.Copy).then_inc(s("hi"), 1)

            for t in range(NT + 5):
                if t >= 5:
                    act.wait_ge(s("proj"), t - 4)
                    act.activation(k.o_raw[:, t - 5, :], k.ps[:, 7, 0:D], ACT.Copy).then_inc(s("o_raw"), 1)
                if t < NT:
                    if t >= 3:
                        act.wait_ge(s("fc"), t - 2)
                    hi(x_turn(t), k.xqT[:, t % 3], KO, 0)
                if 2 <= t < NT + 2:
                    h = t - 2
                    act.wait_ge(s("fc"), h + 1)
                    if h >= 2:
                        act.wait_ge(s("mean"), h - 1)
                        act.wait_ge(s("centred"), h - 1)
                    act.activation(k.h[:, h % 2, :], k.ps[:, 2 * (h % 2):2 * (h % 2) + 2, :].rearrange("p a b -> p (a b)"),
                                   ACT.Gelu, scale=k.sc_fc[:, h:h + 1]).then_inc(s("gelu"), 1)
                if 3 <= t < NT + 3:
                    if t >= 5:
                        act.wait_ge(s("proj"), t - 4)
                    for n, buf, b0 in chunks(t - 3):
                        hi(n, buf, 4, b0)
                if 2 <= t < NT + 2:
                    h = t - 2
                    act.wait_ge(s("mean"), h + 1)
                    act.wait_ge(s("gelu"), h + 1)
                    if h >= 2:
                        act.wait_ge(s("turned"), hidden_turn(h - 2) + 2)
                    act.activation(k.hc[:, h % 2, :], k.h[:, h % 2, :], ACT.Identity,
                                   bias=k.nmean[:, h:h + 1]).then_inc(s("centred"), 1)

        @block.vector
        def _(dve):
            c = Chain(dve, s("dve"))

            def centre_x(t):
                xc = k.xn[:, t, :]
                c.step(dve.tensor_scalar(xc, k.x[:, t, :], k.mv[:, t, 0:1], None, ALU.subtract))
                c.step(dve.tensor_reduce(k.big[:, 0:1], xc, AX.X, ALU.max, apply_absolute_value=True))
                c.step(dve.tensor_scalar(k.big[:, 1:2], k.big[:, 0:1], -1.0, None, ALU.mult))
                dve.tensor_scalar(xc, xc, k.big[:, 0:1], k.big[:, 1:2], ALU.min, ALU.max).then_inc(s("x_clip"), 1)
                dve.wait_ge(s("x_clip"), t + 1)

            def hidden_mean(t):
                h = k.h[:, t % 2, :]
                dve.wait_ge(s("gelu"), t + 1)
                for n in range(2):
                    c.step(dve.bn_stats(k.stats[:, t, 6 * n:6 * n + 6], h[:, n * BANK:(n + 1) * BANK]))
                c.step(dve.bn_aggr(k.mvh[:, t, :], k.stats[:, t, 0:12]))
                dve.tensor_scalar(k.nmean[:, t:t + 1], k.mvh[:, t, 0:1], -1.0, None, ALU.mult).then_inc(s("mean"), 1)

            def hidden_clip(t):
                hc = k.hc[:, t % 2, :]
                dve.wait_ge(s("centred"), t + 1)
                c.step(dve.tensor_reduce(k.big[:, 2:3], hc, AX.X, ALU.max, apply_absolute_value=True))
                c.step(dve.tensor_scalar(k.big[:, 3:4], k.big[:, 2:3], -1.0, None, ALU.mult))
                dve.tensor_scalar(hc, hc, k.big[:, 2:3], k.big[:, 3:4], ALU.min, ALU.max).then_inc(s("h_clip"), 1)
                dve.wait_ge(s("h_clip"), t + 1)

            def lo(n, buf, w, b0):
                dve.wait_ge(s("hi"), n + 1)
                dve.tensor_tensor(dst(buf, 1, w, b0), k.ps[:, 4 + n % 3, 0:w * P], dst(buf, 0, w, b0).bitcast(F32),
                                  ALU.subtract).then_inc(s("lo"), 1)

            centre_x(0)
            centre_x(1)
            for t in range(NT + 3):
                if t < NT:
                    lo(x_turn(t), k.xqT[:, t % 3], KO, 0)
                if t + 2 < NT:
                    centre_x(t + 2)
                if 2 <= t < NT + 2:
                    hidden_mean(t - 2)
                if t >= 3:
                    for n, buf, b0 in chunks(t - 3):
                        lo(n, buf, 4, b0)
                if 2 <= t < NT + 2:
                    hidden_clip(t - 2)
            c.step(dve.tensor_scalar(k.var[:, :], k.mvh[:, :, 1], 1e-6, None, ALU.add))
            rsqrt(dve, c, k.rstd[:, :], k.tmp8[:, :], k.var[:, :])
            c.step(dve.tensor_scalar(k.sc_pr[:, :], k.rstd[:, :], k.gamma[:, 1:2], None, ALU.mult))
            for t in range(NT):
                dve.wait_ge(s("o_raw"), t + 1)
                dve.scalar_tensor_tensor(out=k.x[:, t, :], in0=k.o_raw[:, t, :], scalar=k.sc_pr[:, t:t + 1],
                                         in1=k.x[:, t, :], op0=ALU.mult, op1=ALU.add).then_inc(s("x_new"), 1)
            if out is None:
                dve.wait_ge(s("x_new"), NT)
                layer_stats(dve, c, k, k.x)
                c.step(dve.tensor_scalar(k.var[:, :], k.mv[:, :, 1], 1e-5, None, ALU.add))
                rsqrt(dve, c, k.rstd[:, :], k.tmp8[:, :], k.var[:, :])
                for t in range(NT):
                    c.step(dve.tensor_scalar(k.xn[:, t, :], k.x[:, t, :], k.mv[:, t, 0:1], k.rstd[:, t:t + 1],
                                             ALU.subtract, ALU.mult))

        if beside is not None:
            @block.gpsimd
            def _(pool):
                beside.gpsimd(pool)

            @block.sync
            def _(sp):
                beside.sync(sp)

        if out is not None:
            @block.sync
            def _(sp):
                for t in range(NT):
                    sp.wait_ge(s("x_new"), t + 1)
                    sp.dma_start(out[0, t * P:(t + 1) * P, :], k.x[:, t, :]).then_inc(s("stored"), 16)
                sp.wait_ge(s("stored"), 16 * NT)


class LoadB:

    def __init__(self, ctx, nc, k, io):
        self.s, self.k, self.io = Stage(ctx, nc, "lb"), k, io

    def sync(self, sp):
        k, io = self.k, self.io
        for dst, src in ((k.w_qr[:, 0, :], io["L0_attn_b_W_qr"][0:P]), (k.w_qr[0:QL2, 1, :], io["L0_attn_b_W_qr"][P:QL]),
                         (k.w_kr[:, :, :], io["L0_attn_b_W_kr"].rearrange("(a p) n -> p a n", p=P))):
            sp.dma_start(dst, src).then_inc(self.s("rope_loaded"), 16)
        for dst, src in ((k.w_qc[:, 0, :], io["L0_attn_b_W_qc"][0:P]), (k.w_qc[0:QL2, 1, :], io["L0_attn_b_W_qc"][P:QL]),
                         (k.w_kc[:, :], io["L0_attn_b_W_kc"]), (k.w_v[:, :], io["L0_attn_b_W_v"]),
                         (k.w_ob[:, :, :], io["L0_attn_b_W_o"].rearrange("(h p) n -> p h n", p=P)),
                         (k.w_cp[:, :, :], io["L0_attn_b_W_cp"].rearrange("(a p) n -> p a n", p=P)),
                         (k.w_ck[:, :, 0:KVL], io["L0_attn_b_W_c"].rearrange("(a p) n -> p a n", p=P)),
                         (k.cos[:, :], io["cos"]), (k.sin[:, :], io["sin"])):
            sp.dma_start(dst, src).then_inc(self.s("loaded"), 16)
        sp.wait_ge(self.s("loaded"), 16 * 9)

    def gpsimd(self, pool):
        k, s = self.k, self.s
        pool.wait_ge(s("rope_loaded"), 16 * 3)
        for half in range(2):
            for a, rows in ((0, P), (1, QL2)):
                pool.tensor_copy(k.aw[0:rows, a, :, KVL + 32 * half:KVL + 32 * half + 32],
                                 k.w_qr[0:rows, a, :].rearrange("p (h f two) -> p h f two", two=2, f=32)[:, :, :, half])\
                    .then_inc(s("rope_cols"), 1)
            pool.tensor_copy(k.w_ck[:, :, KVL + 32 * half:KVL + 32 * half + 32],
                             k.w_kr[:, :, :].rearrange("p a (f two) -> p a f two", two=2)[:, :, :, half])\
                .then_inc(s("rope_cols"), 1)


def prepare_b(nc, ctx, k, io):
    s = Stage(ctx, nc, "pb")
    J = IH * TOPK
    order = ([("x", t) for t in range(NT)] + [("w", h) for h in range(8)] + [("sparse", 1), ("k", 0), ("k", 1), ("cp", 0)]
             + [("sparse", 2), ("cp", 1), ("sparse", 3), ("cp", 2), ("cp", 3), ("sparse", 4), ("a", 0), ("sparse", 5), ("a", 1)]
             + [("sparse", 6)] + [("vo", n) for n in range(4)] + [("sparse", 7), ("w", 8), ("w", 9), ("sparse", 8), ("w", 10)]
             + [("w", 11), ("sparse", 9), ("w", 12), ("w", 13), ("w", 14), ("w", 15), ("sparse", 10), ("c", 0), ("a", 2)]
             + [("a", 3)] + [("vo", n) for n in range(4, 8)])
    jobs = [x for x in order if x[0] != "sparse"]
    at = {j: n for n, j in enumerate(jobs)}
    eye8, mean8, tokens, block_mask = k.small[0:IH, 0:IH], k.small[0:J, 8:16], k.small[:, 16:24], k.small[0:J, 24:24 + J]
    ps6, ps7 = k.ps[:, 6, :], k.ps[:, 7, :]

    with nc.Block() as block:

        @block.sync
        def _(sp):
            for dst, src in ((k.w_gate[:, :, :], io["L0_attn_b_W_gate"].rearrange("(a p) n -> p a n", p=P)),
                             (k.small[:, :], io["small"])):
                sp.dma_start(dst, src).then_inc(s("gate_loaded"), 16)
            for dst, src in ((k.w_idx[:, :, :], io["L0_attn_b_W_idx"].rearrange("(a p) n -> p a n", p=P)),
                             (k.w_s[:, 0, :], io["L0_attn_b_W_sq"]), (k.w_s[:, 1, :], io["L0_attn_b_W_sk"]),
                             (k.w_s[:, 2, :], io["L0_attn_b_W_sv"]), (k.w_s[:, 3, :], io["L0_attn_b_W_iout"][:, 0:DV])):
                sp.dma_start(dst, src).then_inc(s("sparse_loaded"), 16)
            sp.wait_ge(s("job_out"), at[("k", 1)] + 1)
            sp.dma_start(k.kswp[KVL:KVL + 32, :], k.kraw[KVL + 32:P, :]).then_inc(s("swapped"), 16)
            sp.dma_start(k.kswp[KVL + 32:P, :], k.kraw[KVL:KVL + 32, :]).then_inc(s("swapped"), 16)
            sp.wait_ge(s("swapped"), 32)

        @block.tensor
        def _(pe):
            def done(name):
                pe.wait_ge(s("job_out"), at[name] + 1)

            def sparse(n):
                if n == 1:
                    done(("x", NT - 1))
                    pe.wait_ge(s("gate_loaded"), 16 * 2)
                    for half in range(2):
                        for a in range(KO):
                            ins = pe.matmul(k.ps[0:IH, 6 + half, :], k.w_gate[:, a, :], k.xT[:, a, half * BANK:(half + 1) * BANK],
                                            start=(a == 0), stop=(a == KO - 1))
                elif n == 2:
                    pe.wait_ge(s("v_index"), 1)
                    ins = pe.matmul(ps6[:, 0:J], k.ones[0:IH, :], k.bd[:, :, :].rearrange("p a b -> p (a b)"), start=True, stop=True)
                elif n == 3:
                    pe.wait_ge(s("v_onehot"), NT)
                    for a in range(KO):
                        for t in range(NT):
                            ins = pe.matmul(ps7[:, a * J:(a + 1) * J], k.xn[:, t, a * P:(a + 1) * P], k.onehot[:, t, :],
                                            start=(t == 0), stop=(t == NT - 1))
                elif n == 4:
                    pe.wait_ge(s("sparse_loaded"), 16 * 5)
                    pe.wait_ge(s("v_xsel"), 1)
                    for h in range(IH):
                        for a in range(KO):
                            ins = pe.matmul(ps6[:, h * TOPK:(h + 1) * TOPK], k.w_idx[:, a, h * P:(h + 1) * P],
                                            k.xsel[:, a, h * TOPK:(h + 1) * TOPK], start=(a == 0), stop=(a == KO - 1))
                elif n == 5:
                    pe.wait_ge(s("v_sel"), 1)
                    pe.matmul(ps7[:, 0:J], k.w_s[:, 0, :], k.sel[:, :], start=True, stop=True)
                    pe.matmul(ps7[:, J:2 * J], k.w_s[:, 1, :], k.sel[:, :], start=True, stop=True)
                    ins = pe.matmul(ps7[0:J, 2 * J:2 * J + P], k.sel[:, :], k.w_s[:, 2, :], start=True, stop=True)
                elif n == 6:
                    pe.wait_ge(s("v_qkv"), 2)
                    ins = pe.matmul(ps6[0:J, 0:J], k.sqk[:, 0:J], k.sqk[:, J:2 * J], start=True, stop=True)
                elif n == 7:
                    pe.wait_ge(s("v_prob"), 1)
                    ins = pe.matmul(ps7[0:J, 0:IH], k.sprob[:, :], mean8, start=True, stop=True)
                elif n == 8:
                    pe.wait_ge(s("v_pm"), 1)
                    ins = pe.matmul(ps6[:, 0:IH], k.sv[:, :], k.chain[0:J, 0:IH], start=True, stop=True)
                elif n == 9:
                    pe.wait_ge(s("v_m"), 1)
                    ins = pe.matmul(ps7[:, 0:IH], k.w_s[:, 3, :], k.chain[:, 8:8 + IH], start=True, stop=True)
                else:
                    pe.wait_ge(s("v_io"), 1)
                    for h in range(NH):
                        ins = pe.matmul(ps6[0:1, 0:D], k.chain[:, 16 + h // 2:17 + h // 2], k.w_ob[:, h, :],
                                        start=(h == 0), stop=(h == NH - 1))
                ins.then_inc(s("sparse"), 1)

            def job(n, what, i):
                b = k.ps[:, n % 6, :]
                if n >= 6:
                    done(jobs[n - 6])
                if what == "x":
                    for a in range(KO):
                        ins = pe.transpose(b[:, a * P:(a + 1) * P], k.xn[:, i, a * P:(a + 1) * P], k.ident[:, :])
                elif what == "w":
                    cols = slice(i * P, (i + 1) * P)
                    pe.transpose(b[:, 0:P], k.w_qc[:, 0, cols], k.ident[:, :])
                    pe.transpose(b[:, P:QL], k.w_qc[0:QL2, 1, cols], k.ident[0:QL2, 0:QL2])
                    pe.transpose(b[:, QL:QL + KVL], k.w_kc[:, cols], k.ident[0:KVL, 0:KVL])
                    ins = pe.transpose(b[:, QL + KVL:QL + 2 * KVL], k.w_v[:, cols], k.ident[0:KVL, 0:KVL])
                elif what == "k":
                    done(("x", NT - 1))
                    for a in range(KO):
                        ins = pe.matmul(b, k.w_ck[:, a, :], k.xT[:, a, i * BANK:(i + 1) * BANK], start=(a == 0), stop=(a == KO - 1))
                elif what == "cp":
                    for a in range(KO):
                        w = k.w_cp[:, a, 0:P] if i < 2 else k.w_cp[:, a, P:QL]
                        ins = pe.matmul(b if i < 2 else b[0:QL2, :], w, k.xT[:, a, (i % 2) * BANK:(i % 2 + 1) * BANK],
                                        start=(a == 0), stop=(a == KO - 1))
                elif what == "a":
                    done(("w", 4 * i + 3))
                    for h in range(4):
                        for part, rows in ((0, P), (1, QL2)):
                            w = k.wT[:, (4 * i + h) % 8, :]
                            ins = pe.matmul(b[0:rows, part * D + h * KVL:part * D + (h + 1) * KVL],
                                            w[:, part * P:part * P + rows], w[:, QL:QL + KVL], start=True, stop=True)
                elif what == "vo":
                    for j in range(2):
                        ins = pe.matmul(b[KVL * j:KVL * (j + 1), 0:D], k.wT[:, (2 * i + j) % 8, QL + KVL:QL + 2 * KVL],
                                        k.w_ob[:, 2 * i + j, :], start=True, stop=True)
                else:
                    done(("k", 1))
                    for t in range(NT):
                        ins = pe.transpose(b[:, t * KVL:(t + 1) * KVL], k.kraw[0:KVL, t * P:(t + 1) * P], k.ident[0:KVL, 0:KVL])
                ins.then_inc(s("job"), 1)

            for what, i in order:
                if what == "sparse":
                    sparse(i)
                else:
                    job(at[(what, i)], what, i)

        @block.scalar
        def _(act):
            for n, (what, i) in enumerate(jobs):
                b = k.ps[:, n % 6, :]
                half = slice((i % 2) * BANK, (i % 2 + 1) * BANK)
                if what == "x":
                    parts = [(k.xT[:, :, i * P:(i + 1) * P], b[:, 0:D].rearrange("p (a n) -> p a n", a=KO))]
                elif what == "w":
                    parts = [(k.wT[:, i % 8, :], b[:, 0:QL + 2 * KVL])]
                elif what == "k":
                    parts = [(k.kraw[:, half], b)]
                elif what == "cp":
                    parts = [(k.cpT[:, 0, half], b)] if i < 2 else [(k.cpT[0:QL2, 1, half], b[0:QL2, :])]
                elif what == "a":
                    parts = [(k.aw[:, 0, 4 * i:4 * i + 4, 0:KVL], b[:, 0:D].rearrange("p (h n) -> p h n", h=4)),
                             (k.aw[0:QL2, 1, 4 * i:4 * i + 4, 0:KVL], b[0:QL2, D:2 * D].rearrange("p (h n) -> p h n", h=4))]
                elif what == "vo":
                    parts = [(k.w_vo[:, i, :], b[:, 0:D])]
                else:
                    parts = [(k.c_tok[:, :, :].rearrange("p t n -> p (t n)"), b)]
                if (what, i) == ("vo", 0):
                    act.wait_ge(s("v_smax"), 1)
                    act.activation(k.sprob[:, :], k.sprob[:, :], ACT.Exp, bias=k.scol[0:J, 0:1], accum_out=k.scol[0:J, 1:2])\
                        .then_inc(s("exp"), 1)
                if (what, i) == ("w", 8):
                    act.wait_ge(s("key"), 2)
                    act.activation(k.k_hi[:, :], k.key[:, :], ACT.Copy).then_inc(s("khi"), 1)
                act.wait_ge(s("job"), n + 1)
                for o, a in parts:
                    ins = act.activation(o, a, ACT.Copy)
                ins.then_inc(s("job_out"), 1)

        @block.vector
        def _(dve):
            c = Chain(dve, s("dve"))

            def sparse_done(n):
                dve.wait_ge(s("sparse"), n)

            sparse_done(1)
            c.step(dve.tensor_copy(k.gT[:, :], k.ps[0:IH, 6:8, :].rearrange("p a b -> p (a b)")))
            c.step(dve.max(k.top[:, :], k.gT[:, :]))
            c.step(dve.max_index(k.top_at[:, :], k.top[:, :], k.gT[:, :]))
            c.step(dve.tensor_copy(k.top[:, :], k.top_at[:, :]))
            dve.tensor_tensor(k.bd[:, :, :], k.top[:, :].unsqueeze(1).broadcast_to([IH, IH, TOPK]),
                              eye8.unsqueeze(2).broadcast_to([IH, IH, TOPK]), ALU.mult).then_inc(s("v_index"), 1)
            sparse_done(2)
            for t in range(NT):
                dve.tensor_scalar(k.onehot[:, t, :], ps6[:, 0:J], tokens[:, t:t + 1], None, ALU.is_equal).then_inc(s("v_onehot"), 1)
            dve.wait_ge(s("job_out"), at[("k", 1)] + 1)
            dve.tensor_tensor(k.key[:, :], k.kraw[:, :], k.cos[:, :], ALU.mult).then_inc(s("key"), 1)
            sparse_done(3)
            dve.tensor_copy(k.xsel[:, :, :].rearrange("p a b -> p (a b)"), ps7[:, 0:KO * J]).then_inc(s("v_xsel"), 1)
            dve.wait_ge(s("swapped"), 32)
            c.step(dve.tensor_tensor(k.kswp[KVL:P, :], k.kswp[KVL:P, :], k.sin[KVL:P, :], ALU.mult))
            sparse_done(4)
            dve.tensor_copy(k.sel[:, :], ps6[:, 0:J]).then_inc(s("v_sel"), 1)
            dve.wait_ge(s("key"), 1)
            dve.tensor_tensor(k.key[KVL:P, :], k.key[KVL:P, :], k.kswp[KVL:P, :], ALU.add).then_inc(s("key"), 1)
            sparse_done(5)
            dve.tensor_copy(k.sqk[:, :], ps7[:, 0:2 * J]).then_inc(s("v_qkv"), 1)
            dve.tensor_copy(k.sv[:, :], ps7[0:J, 2 * J:2 * J + P]).then_inc(s("v_qkv"), 1)
            sparse_done(6)
            c.step(dve.scalar_tensor_tensor(out=k.sprob[:, :], in0=ps6[0:J, 0:J], scalar=float(P) ** -0.5, in1=block_mask,
                                            op0=ALU.mult, op1=ALU.add))
            dve.tensor_reduce(k.scol[0:J, 0:1], k.sprob[:, :], AX.X, ALU.max, negate=True).then_inc(s("v_smax"), 1)
            dve.wait_ge(s("exp"), 1)
            c.step(dve.reciprocal(k.scol[0:J, 2:3], k.scol[0:J, 1:2]))
            dve.tensor_scalar(k.sprob[:, :], k.sprob[:, :], k.scol[0:J, 2:3], None, ALU.mult).then_inc(s("v_prob"), 1)
            sparse_done(7)
            dve.tensor_copy(k.chain[0:J, 0:IH], ps7[0:J, 0:IH]).then_inc(s("v_pm"), 1)
            sparse_done(8)
            dve.tensor_copy(k.chain[:, 8:8 + IH], ps6[:, 0:IH]).then_inc(s("v_m"), 1)
            sparse_done(9)
            dve.tensor_copy(k.chain[:, 16:16 + IH], ps7[:, 0:IH]).then_inc(s("v_io"), 1)
            dve.wait_ge(s("khi"), 1)
            c.step(dve.tensor_tensor(k.k_lo[:, :], k.key[:, :], k.k_hi[:, :].bitcast(F32), ALU.subtract))
            sparse_done(10)
            c.step(dve.tensor_copy(k.row[:, :], ps6[0:1, 0:D]))


class QueriesB:

    HALF_AT = (0, 3, 6, 9)
    SPLIT_AT = (12, 15)
    PER = 2 * NT

    def __init__(self, k):
        self.k = k

    def bind(self, s, steps, units):
        self.s, self.pairs = s, NH // 2

    def work(self, i):
        p, at = divmod(i, self.PER)
        if p + 1 >= self.pairs:
            return [], []
        return ([4 * (p + 1) + m for m, x in enumerate(self.HALF_AT) if x == at],
                [2 * (p + 1) + m for m, x in enumerate(self.SPLIT_AT) if x == at])

    def product(self, pe, m):
        k, s, (h, half) = self.k, self.s, divmod(m, 2)
        if m >= 1:
            pe.wait_ge(s("q_raw"), m)
            pe.wait_ge(s("q_cos"), m)
        sl = slice(half * BANK, (half + 1) * BANK)
        pe.matmul(k.ps[:, 7, :], k.aw[:, 0, h, :], k.cpT[:, 0, sl], start=True, stop=False)
        pe.matmul(k.ps[:, 7, :], k.aw[0:QL2, 1, h, :], k.cpT[0:QL2, 1, sl], start=False, stop=True).then_inc(s("q_prod"), 1)

    def cosine(self, dve, m):
        k, s, (h, half) = self.k, self.s, divmod(m, 2)
        sl = slice(half * BANK, (half + 1) * BANK)
        dve.wait_ge(s("q_prod"), m + 1)
        if h >= 2:
            dve.wait_ge(s("q_hi"), h - 1)
            dve.wait_ge(s("q_lo"), h - 1)
        dve.wait_ge(s("q_raw"), m + 1)
        dve.tensor_tensor(k.q1[:, h % 2, sl], k.ps[:, 7, :], k.cos[:, sl], ALU.mult).then_inc(s("q_cos"), 1)

    def raw(self, act, m):
        k, s, (h, half) = self.k, self.s, divmod(m, 2)
        act.wait_ge(s("q_prod"), m + 1)
        if h >= 2:
            act.wait_ge(s("q_swap0" if h % 2 == 0 else "q_swap1"), 32 * (h // 2))
        act.activation(k.qraw[KVL:P, h % 2, half * BANK:(half + 1) * BANK], k.ps[KVL:P, 7, :], ACT.Copy).then_inc(s("q_raw"), 1)

    def hi(self, act, h):
        k, s = self.k, self.s
        act.wait_ge(s("q_rope"), h + 1)
        act.wait_ge(s("q_cos"), 2 * h + 2)
        if h >= 4:
            act.wait_ge(s("scores"), self.PER * (h // 2 - 1))
        act.activation(k.q_hl[:, (h // 2) % 2, h % 2, 0, :], k.q1[:, h % 2, :], ACT.Copy).then_inc(s("q_hi"), 1)

    def lo(self, dve, h):
        k, s = self.k, self.s
        dve.wait_ge(s("q_hi"), h + 1)
        dve.wait_ge(s("q_rope"), h + 1)
        if h >= 4:
            dve.wait_ge(s("scores"), self.PER * (h // 2 - 1))
        dve.tensor_tensor(k.q_hl[:, (h // 2) % 2, h % 2, 1, :], k.q1[:, h % 2, :],
                          k.q_hl[:, (h // 2) % 2, h % 2, 0, :].bitcast(F32), ALU.subtract).then_inc(s("q_lo"), 1)

    def pe_first(self, pe):
        for m in range(4):
            self.product(pe, m)

    def dve_first(self, dve):
        for m in range(4):
            self.cosine(dve, m)
        for h in range(2):
            self.lo(dve, h)

    def act_first(self, act):
        for m in range(4):
            self.raw(act, m)
        for h in range(2):
            self.hi(act, h)

    def pe(self, pe, i):
        for m in self.work(i)[0]:
            self.product(pe, m)
        if i % self.PER == 0:
            pe.wait_ge(self.s("q_hi"), 2 * (i // self.PER) + 2)
            pe.wait_ge(self.s("q_lo"), 2 * (i // self.PER) + 2)

    def dve(self, dve, i):
        for m in self.work(i)[0]:
            self.cosine(dve, m)
        for h in self.work(i)[1]:
            self.lo(dve, h)

    def act(self, act, i):
        for m in self.work(i)[0]:
            self.raw(act, m)
        for h in self.work(i)[1]:
            self.hi(act, h)

    def pool(self, pool):
        k, s = self.k, self.s
        for h in range(NH):
            pool.wait_ge(s("q_swap0" if h % 2 == 0 else "q_swap1"), 32 * (h // 2 + 1))
            w = k.swp[KVL:P, h % 2, :]
            pool.tensor_tensor(w, w, k.sin[KVL:P, :], ALU.mult).then_inc(s("q_sin"), 1)
            pool.wait_ge(s("q_sin"), h + 1)
            pool.wait_ge(s("q_cos"), 2 * h + 2)
            q = k.q1[KVL:P, h % 2, :]
            pool.tensor_tensor(q, q, w, ALU.add).then_inc(s("q_rope"), 1)

    def sync(self, sp):
        k, s = self.k, self.s
        for h in range(NH):
            sp.wait_ge(s("q_raw"), 2 * h + 2)
            if h >= 2:
                sp.wait_ge(s("q_rope"), h - 1)
            sem = s("q_swap0" if h % 2 == 0 else "q_swap1")
            sp.dma_start(k.swp[KVL:KVL + 32, h % 2, :], k.qraw[KVL + 32:P, h % 2, :]).then_inc(sem, 16)
            sp.dma_start(k.swp[KVL + 32:P, h % 2, :], k.qraw[KVL:KVL + 32, h % 2, :]).then_inc(sem, 16)


def attend_b(nc, ctx, k):
    def passes(i, u, j, qt):
        q = [k.q_hl[:, (u // NT) % 2, j, part, qt * P:(qt + 1) * P] for part in range(2)]
        return [(q[0], k.k_hi), (q[0], k.k_lo), (q[1], k.k_hi)]

    attention(nc, ctx, k, "ab", 2, passes, lambda b, h: k.c_tok[:, b, :], KVL, 2, extra=QueriesB(k))


def build(nc, io, out):
    with ExitStack() as ctx:
        k = Tensors()

        def sb(name, shape, dt=F32, c=ctx):
            t = c.enter_context(nc.sbuf_tensor(name, shape, dt))
            return t

        k.ps = ctx.enter_context(nc.psum_tensor("banks", [P, 8, BANK], F32))
        k.x = sb("x", [P, NT, D])
        k.xn = sb("xn", [P, NT, D])
        k.t_fc = sb("t_fc", [P, KO, FF], F32R)
        k.t_pr = sb("t_pr", [P, FO, D], F32R)
        k.ident = sb("ident", [P, P])
        k.ident_bf = sb("ident_bf", [P, P], BF16)
        k.mask_bf = sb("mask_bf", [P, P], BF16)
        k.cols = sb("cols", [P, 8])
        k.ones = sb("ones", [P, P])
        k.stats = sb("stats", [P, NT, 12])
        k.mv = sb("mv", [P, NT, 2])
        k.mvh = sb("mvh", [P, NT, 2])
        k.var, k.rstd, k.tmp8, k.sc_fc, k.sc_pr = (sb(n, [P, NT]) for n in ("var", "rstd", "tmp8", "sc_fc", "sc_pr"))
        k.gamma, k.thr, k.nthr, k.wsum = (sb(n, [P, 2]) for n in ("gamma", "thr", "nthr", "wsum"))
        k.big = sb("big", [P, 4])
        k.nmax = sb("nmax", [P, NT, NH])
        k.den = sb("den", [P, NT, NH])
        k.r3 = sb("r3", [P, NT, 96], BF16)
        k.rT = sb("rT", [96, S], BF16)
        k.sel_bf = sb("sel_bf", [96, 12, P], BF16)

        with ExitStack() as a:
            k.w_o = sb("w_o_a", [P, 4, D], F32, a)
            k.v_a = sb("v_a", [P, NT, NH, 32], F32, a)
            k.qhi = sb("qhi", [P, 4, S], F32R, a)
            k.qlo = sb("qlo", [P, 4, S], F32R, a)
            k.khl = sb("khl", [P, 4, S], F32R, a)
            with ExitStack() as w:
                k.mask = sb("mask", [P, P], F32, w)
                k.sel_f = sb("sel_f", [96, 12, P], F32, w)
                k.w_qkv = sb("w_qkv", [P, KO, 3 * D], F32, w)
                k.wq2 = sb("wq2", [P, KO, NH, 2, HD], F32, w)
                k.wk2 = sb("wk2", [P, KO, NH, 2, HD], F32, w)
                k.w_fc = sb("w_fc", [P, FO, D], F32, w)
                k.w_pr = sb("w_pr", [P, KO, FF], F32, w)
                k.tmp2k = sb("tmp2k", [P, 2 * S], F32, w)
                k.tern_in = lambda n, b: (k.w_fc[:, 4 * (n % 2) + b, (n // 2) * P:(n // 2 + 1) * P] if n < 4 else
                                          k.w_pr[:, b % 2, (2 * (n - 4) + b // 2) * P:(2 * (n - 4) + b // 2 + 1) * P])
                k.tern_out = lambda n: (k.t_fc[:, n // 2, BANK * (n % 2):BANK * (n % 2 + 1)] if n < 4 else
                                        k.t_pr[:, 2 * (n - 4):2 * (n - 4) + 2, :].rearrange("p a b -> p (a b)"))
                prepare(nc, ctx, k, io)
                k.xT = k.w_fc[:, :, :].rearrange("p a b -> p (a b)").rearrange("p (a b) -> p a b", a=KO)
                k.khi = sb("khi", [P, 2, BANK], F32R, w)
                k.tmp512 = k.tmp2k[:, 0:BANK]
                project_a(nc, ctx, k)
            k.oT = sb("oT_a", [P, 4, S], F32, a)
            with ExitStack() as w:
                k.qm = sb("qm", [P, 2, 2, 4, P], F32R, w)
                k.prob = sb("prob_a", [P, 3, S], F32, w)
                k.pT = sb("pT_a", [P, 2, 4, S], F32, w)
                attend_a(nc, ctx, k)
            k.w_out = k.w_o
            k.o_hi, k.o_lo = sb("o_hi_a", [P, 4, S], F32R, a), sb("o_lo_a", [P, 4, S], F32R, a)
            k.wo_hi, k.wo_lo = sb("wo_hi_a", [P, 4, D], F32R, a), sb("wo_lo_a", [P, 4, D], F32R, a)
            finish_attention(nc, ctx, k, "fa", 4, k.sel_bf[:, 0:4, :], lambda dve, c: ffn_norm(dve, c, k))

        with ExitStack() as b:
            k.aw = sb("aw", [P, 2, NH, P], F32, b)
            k.w_vo = sb("w_vo", [P, NH // 2, D], F32, b)
            k.cpT = sb("cpT", [P, 2, S], F32, b)
            k.k_hi, k.k_lo = sb("k_hi", [P, S], F32R, b), sb("k_lo", [P, S], F32R, b)
            k.c_tok = sb("c_tok", [P, NT, KVL], F32, b)
            k.cos, k.sin = sb("cos", [P, S], F32, b), sb("sin", [P, S], F32, b)
            k.row = sb("row", [1, D], F32, b)
            with ExitStack() as w:
                k.w_ob = sb("w_ob", [P, NH, D], F32, w)
                k.w_qc = sb("w_qc", [P, 2, NH * DK], F32, w)
                k.w_kc, k.w_v = sb("w_kc", [KVL, NH * DK], F32, w), sb("w_v", [KVL, NH * DV], F32, w)
                k.w_cp = sb("w_cp", [P, KO, QL], F32, w)
                k.w_ck = sb("w_ck", [P, KO, P], F32, w)
                k.w_kr = sb("w_kr", [P, KO, DR], F32, w)
                with ExitStack() as f:
                    k.w_qr = sb("w_qr", [P, 2, NH * DR], F32, f)
                    alloc_ffn(k, lambda n, sh, dt=F32: sb(n + "_1", sh, dt, f))
                    ffn(nc, ctx, k, "f1", beside=LoadB(ctx, nc, k, io))
                J = IH * TOPK
                k.xT = sb("xT_b", [P, KO, S], F32, w)
                k.wT = sb("wT", [P, 8, QL + 2 * KVL], F32, w)
                k.kraw, k.key, k.kswp = (sb(n, [P, S], F32, w) for n in ("kraw", "key", "kswp"))
                k.w_gate, k.w_idx, k.w_s = (sb("w_gate", [P, KO, IH], F32, w), sb("w_idx", [P, KO, IH * P], F32, w),
                                            sb("w_s", [P, 4, P], F32, w))
                k.small = sb("small", [P, 24 + J], F32, w)
                k.gT, k.top, k.top_at = sb("gT", [IH, S], F32, w), sb("top", [IH, 8], F32, w), sb("top_at", [IH, 8], mybir.dt.uint32, w)
                k.bd, k.onehot, k.xsel = sb("bd", [IH, IH, TOPK], F32, w), sb("onehot", [P, NT, J], F32, w), sb("xsel", [P, KO, J], F32, w)
                k.sel, k.sqk, k.sv = sb("sel", [P, J], F32, w), sb("sqk", [P, 2 * J], F32, w), sb("sv", [J, P], F32, w)
                k.sprob, k.scol, k.chain = sb("sprob", [J, J], F32, w), sb("scol", [P, 4], F32, w), sb("chain", [P, 24], F32, w)
                prepare_b(nc, ctx, k, io)
            k.qraw = k.xn[:, :, :].rearrange("p a b -> p (a b)").rearrange("p (a b) -> p a b", a=2)
            k.oT = sb("oT_b", [P, NH // 2, S], F32, b)
            with ExitStack() as w:
                k.swp = sb("swp", [P, 2, S], F32, w)
                k.q1 = sb("q1", [P, 2, S], F32, w)
                k.q_hl = sb("q_hl", [P, 2, 2, 2, S], F32R, w)
                k.prob = sb("prob_b", [P, 3, S], F32, w)
                k.pT = sb("pT_b", [P, 2, 2, S], F32, w)
                attend_b(nc, ctx, k)
            k.w_out = k.w_vo
            k.o_hi, k.o_lo = sb("o_hi_b", [P, 8, S], F32R, b), sb("o_lo_b", [P, 8, S], F32R, b)
            k.wo_hi, k.wo_lo = sb("wo_hi_b", [P, 8, D], F32R, b), sb("wo_lo_b", [P, 8, D], F32R, b)
            finish_attention(nc, ctx, k, "fb", NH // 2, k.sel_bf[:, 4:12, :], lambda dve, c: ffn_norm(dve, c, k), row=k.row[:, :])

        with ExitStack() as f:
            alloc_ffn(k, lambda n, sh, dt=F32: sb(n + "_2", sh, dt, f))
            ffn(nc, ctx, k, "f2", out)


def alloc_ffn(k, sb):
    k.xqT = sb("xqT", [P, 3, 2, KO, P], F32R)
    k.h = sb("h", [P, 2, FF])
    k.hc = sb("hc", [P, 2, FF])
    k.hT = sb("hT", [P, 2, 2, FO, P], F32R)
    k.o_raw = sb("o_raw", [P, NT, D])
    k.nmean = sb("nmean", [P, NT])


def constants():
    c = {"ident": np.eye(P, dtype=np.float32)}
    q, kk = np.arange(P)[:, None], np.arange(P)[None, :]
    c["mask"] = np.where(kk > q, np.float32(-1e30), np.float32(0)).astype(np.float32)
    cols = np.zeros((P, 8), np.float32)
    odd = (np.arange(P) // HD) % 2
    cols[:, 0], cols[:, 1] = odd, 1 - 2 * odd
    for j in range(4):
        cols[32 * j:32 * j + 32, 4 + j] = 1
    c["cols"] = cols
    sel = np.zeros((96, 12, P), np.float32)
    for part in range(3):
        for h in range(NH):
            sel[32 * part + h, h // 4, 32 * (h % 4):32 * (h % 4) + 32] = 1
            sel[32 * part + h, 4 + h // 2, KVL * (h % 2):KVL * (h % 2 + 1)] = 1
    c["sel"] = sel
    inv = 1.0 / 10000.0 ** (np.arange(0, DR, 2)[:DR // 2].astype(np.float32) / DR)
    freqs = np.outer(np.arange(S, dtype=np.float32), inv)
    root = (DK + DR) ** -0.25
    cos, sin = np.cos(freqs).T, np.sin(freqs).T
    c["cos"] = (np.concatenate([np.ones((KVL, S)), cos, cos]) * root).astype(np.float32)
    c["sin"] = (np.concatenate([np.zeros((KVL, S)), -sin, sin]) * root).astype(np.float32)
    J = IH * TOPK
    small = np.zeros((P, 24 + J), np.float32)
    small[:IH, :IH] = np.eye(IH)
    small[:J, 8:16] = np.repeat(np.eye(IH), TOPK, axis=0) / TOPK
    small[:, 16:24] = np.arange(S).reshape(NT, P).T
    head = np.arange(J) // TOPK
    small[:J, 24:] = np.where(head[:, None] == head[None, :], 0, np.float32(-1e30))
    c["small"] = small
    return c


_INS = ["L0_attn_a_x", "L0_attn_a_Wqkv", "L0_attn_a_Wo", "L0_attn_b_W_c", "L0_attn_b_W_cp", "L0_attn_b_W_qc",
        "L0_attn_b_W_qr", "L0_attn_b_W_kc", "L0_attn_b_W_kr", "L0_attn_b_W_v", "L0_attn_b_W_o", "L0_attn_b_W_idx",
        "L0_attn_b_W_gate", "L0_attn_b_W_sq", "L0_attn_b_W_sk", "L0_attn_b_W_sv", "L0_attn_b_W_iout",
        "L0_ffn_w_fc", "L0_ffn_w_proj"]


def kernel(**inputs):
    import numpy as _np
    import concourse.bacc as _bacc
    from concourse import mybir as _mybir
    from concourse.bass_utils import run_bass_kernel_spmd as _run

    nc = _bacc.Bacc("TRN2", target_bir_lowering=False, num_devices=1)
    arrays, io = {}, {}
    for name, a in [(n, _np.ascontiguousarray(inputs[n])) for n in _INS] + list(constants().items()):
        arrays[f"in_{name}"] = a
        io[name] = nc.dram_tensor(f"in_{name}", a.shape, _mybir.dt.from_np(a.dtype), kind="ExternalInput").ap()
    out = nc.dram_tensor("out", (1, S, D), F32, kind="ExternalOutput").ap()
    build(nc, io, out)
    r = _run(nc, [arrays], core_ids=[0])
    return r.results[0]["out"]
```

```python
from contextlib import ExitStack

import concourse.bass as bass
from concourse import mybir
from concourse.alu_op_type import AluOpType as ALU
import numpy as np

ACT = mybir.ActivationFunctionType
AX = mybir.AxisListType
F32 = mybir.dt.float32
F32R = mybir.dt.float32r
BF16 = mybir.dt.bfloat16
I32 = mybir.dt.int32

P = 128
S = 1024
D = 256
NT = S // P
KO = D // P
NH = 16
HD = 16
FF = 4 * D
FO = FF // P
BANK = 512
QL, KVL = 192, 64
QL2 = QL - P
DK, DR, DV = 128, 64, 128
IH, TOPK = 8, 8
RSQRT_SEED = float(0x5F3759DF)


class Tensors:
    pass


class Stage:

    def __init__(self, ctx, nc, name):
        self.ctx, self.nc, self.name, self.made = ctx, nc, name, {}

    def __call__(self, what):
        if what not in self.made:
            self.made[what] = self.ctx.enter_context(self.nc.semaphore(f"{self.name}_{what}"))
        return self.made[what]


class Chain:

    def __init__(self, eng, sem):
        self.eng, self.sem, self.n = eng, sem, 0

    def start(self, ins):
        self.n += 1
        ins.then_inc(self.sem, 1)
        return self.n

    def wait(self, n):
        self.eng.wait_ge(self.sem, n)

    def step(self, ins):
        self.wait(self.start(ins))


def rsqrt(dve, chain, y, t, v):
    chain.step(dve.tensor_scalar(y.bitcast(I32), v.bitcast(I32), -0.5, RSQRT_SEED, ALU.mult, ALU.add))
    for _ in range(3):
        chain.step(dve.tensor_tensor(t, y, y, ALU.mult))
        chain.step(dve.scalar_tensor_tensor(out=t, in0=t, scalar=-0.5, in1=v, op0=ALU.mult, op1=ALU.mult))
        chain.step(dve.scalar_tensor_tensor(out=y, in0=t, scalar=1.5, in1=y, op0=ALU.add, op1=ALU.mult))


def layer_stats(dve, chain, k, x, tiles):
    for t in tiles:
        last = chain.start(dve.bn_stats(k.stats[:, t, 0:6], x[:, t, :]))
    chain.wait(last)
    for t in tiles:
        last = chain.start(dve.bn_aggr(k.mv[:, t, :], k.stats[:, t, 0:6]))
    chain.wait(last)


def project_a(nc, ctx, k, io):
    s = Stage(ctx, nc, "pa")
    jobs = [(what, g, h) for what in ("k", "q") for h in range(2) for g in range(4)]
    weights = (k.w_fc, k.w_pr)
    TERN_AT = (5, 6, 7, 8, 11, 12, 13, 14)

    def turned_x(t):
        return k.ps[:, t, 0:D] if t < 4 else k.ps[:, 4 + (t - 4) // 2, (t % 2) * D:(t % 2 + 1) * D]

    with nc.Block() as block:

        @block.sync
        def _(sp):
            x = io["L0_attn_a_x"].rearrange("a (t p) d -> p (a t) d", p=P)
            sp.dma_start(k.x[:, 0:NT // 2, :], x[:, 0:NT // 2, :]).then_inc(s("x_first"), 16)
            sp.dma_start(k.x[:, NT // 2:NT, :], x[:, NT // 2:NT, :]).then_inc(s("x_second"), 16)
            sp.dma_start(k.w_fc[:, :, :], io["L0_ffn_w_fc"].rearrange("(t p) n -> p t n", p=P)).then_inc(s("w_ffn"), 16)
            sp.dma_start(k.w_pr[:, :, :], io["L0_ffn_w_proj"].rearrange("(t p) n -> p t n", p=P)).then_inc(s("w_ffn"), 16)
            sp.dma_start(k.mask[:, :], io["mask"]).then_inc(s("mask"), 16)
            sp.dma_start(k.sel_f[:, :, :], io["sel"]).then_inc(s("sel"), 16)
            sp.wait_ge(s("wo_zero"), 1)
            for j in range(4):
                src = io["L0_attn_a_Wo"].rearrange("(g j d) n -> j d g n", j=4, d=HD)[j]
                sp.dma_start(k.w_o[32 * j:32 * j + HD, :, :], src).then_inc(s("w_o"), 16)
            sp.wait_ge(s("w_o"), 16 * 4)

        @block.gpsimd
        def _(pool):
            pool.memset(k.w_o[:, :, :], 0.0).then_inc(s("wo_zero"), 1)
            pool.memset(k.ones[:, :], 1.0).then_inc(s("ones"), 1)
            pool.memset(k.v_a[:, :, :, :], 0.0).then_inc(s("v_zero"), 1)
            pool.memset(k.r3[:, :, :], 0.0).then_inc(s("r3_zero"), 1)
            pool.wait_ge(s("sel"), 16)
            pool.tensor_copy(k.sel_bf[:, :, :], k.sel_f[:, :, :]).then_inc(s("sel_out"), 1)

        @block.tensor
        def _(pe):
            def turn_weights(n):
                pe.wait_ge(s("tern"), 1 if n < 4 else 2)
                if n >= 2:
                    pe.wait_ge(s("w_out"), n - 1)
                for b in range(4):
                    ins = pe.transpose(k.ps[:, 6 + n % 2, b * P:(b + 1) * P], k.tern_in(n, b), k.ident[:, :])
                ins.then_inc(s("w_turned"), 1)

            def turn_x(t):
                pe.wait_ge(s("xn"), t + 1)
                for a in range(KO):
                    ins = pe.transpose(turned_x(t)[:, a * P:(a + 1) * P], k.xn[:, t, a * P:(a + 1) * P], k.ident[:, :])
                ins.then_inc(s("turned"), 1)

            pe.wait_ge(s("ident"), 16)
            for t in range(4):
                turn_x(t)
            pe.wait_ge(s("w_dup"), 2)
            for n, (what, g, half) in enumerate(jobs):
                w = k.wk2 if what == "k" else k.wq2
                if n == 4:
                    for t in range(4, NT):
                        turn_x(t)
                    pe.wait_ge(s("xT"), NT)
                if n < 4:
                    pe.wait_ge(s("xT"), 4)
                else:
                    pe.wait_ge(s("hi"), n - 3)
                    pe.wait_ge(s("lo"), n - 3)
                for a in range(KO):
                    ins = pe.matmul(k.ps[:, n % 4, :], w[:, a, 4 * g:4 * g + 4, :, :].rearrange("p h u d -> p (h u d)"),
                                    k.xT[:, a, half * BANK:(half + 1) * BANK], start=(a == 0), stop=(a == KO - 1))
                ins.then_inc(s("proj"), 1)
                if n == 2:
                    pe.wait_ge(s("wsum"), 2)
                    pe.wait_ge(s("ones"), 1)
                    pe.matmul(k.ps[:, 6, 0:2], k.ones[:, :], k.wsum[:, :], start=True, stop=True).then_inc(s("gamma"), 1)
                for m, x in enumerate(TERN_AT):
                    if x == n:
                        turn_weights(m)
            for t in range(NT):
                if t >= 2:
                    pe.wait_ge(s("v"), t - 1)
                for a in range(KO):
                    ins = pe.matmul(k.ps[:, 4 + t % 2, 0:D], k.xT[:, a, t * P:(t + 1) * P], k.w_qkv[:, a, 2 * D:3 * D],
                                    start=(a == 0), stop=(a == KO - 1))
                ins.then_inc(s("vproj"), 1)

        @block.scalar
        def _(act):
            act.dma_start(k.ident[:, :], io["ident"]).then_inc(s("ident"), 16)
            act.dma_start(k.w_qkv[:, :, :], io["L0_attn_a_Wqkv"].rearrange("(a p) n -> p a n", p=P)).then_inc(s("w_qkv"), 16)
            act.dma_start(k.cols[:, :], io["cols"]).then_inc(s("cols"), 16)
            act.wait_ge(s("w_qkv"), 16)
            for n, w in ((1, k.wk2), (0, k.wq2)):
                for dup in range(2):
                    for a in range(KO):
                        ins = act.activation(w[:, a, :, dup, :], k.w_qkv[:, a, n * D:(n + 1) * D].rearrange("p (h d) -> p h d", d=HD),
                                             ACT.Copy)
                ins.then_inc(s("w_dup"), 1)
            def out_x(t):
                act.wait_ge(s("turned"), t + 1 if t < 4 else (t | 1) + 1)
                act.activation(k.xT[:, :, t * P:(t + 1) * P], turned_x(t).rearrange("p (a n) -> p a n", a=KO),
                               ACT.Copy).then_inc(s("xT"), 1)

            for t in range(4):
                out_x(t)
            for n, (what, g, half) in enumerate(jobs):
                if n == 2:
                    for t in range(4, NT):
                        out_x(t)
                act.wait_ge(s("proj"), n + 1)
                sl = slice(half * BANK, (half + 1) * BANK)
                if what == "k":
                    if n >= 2:
                        act.wait_ge(s("lo"), n - 1)
                    act.activation(k.khi[:, n % 2, :], k.ps[:, n % 4, :], ACT.Copy).then_inc(s("hi"), 1)
                else:
                    act.activation(k.qhi[:, g, sl], k.ps[:, n % 4, :], ACT.Copy, scale=float(HD) ** -0.5).then_inc(s("hi"), 1)
                for m, x in enumerate(TERN_AT):
                    if x == n:
                        act.wait_ge(s("w_turned"), m + 1)
                        act.activation(k.tern_out(m), k.ps[:, 6 + m % 2, :], ACT.Copy).then_inc(s("w_out"), 1)
            act.wait_ge(s("v_zero"), 1)
            for t in range(NT):
                act.wait_ge(s("vproj"), t + 1)
                act.activation(k.v_a[:, t, :, 0:HD], k.ps[:, 4 + t % 2, 0:D].rearrange("p (h d) -> p h d", d=HD),
                               ACT.Copy).then_inc(s("v"), 1)

        @block.vector
        def _(dve):
            c = Chain(dve, s("dve"))

            def ternarise(n):
                flat = weights[n][:, :, :].rearrange("p a b -> p (a b)")
                c.step(dve.tensor_scalar(k.tmp2k[:, :], flat, k.nthr[:, n:n + 1], None, ALU.is_lt))
                dve.scalar_tensor_tensor(out=flat, in0=flat, scalar=k.thr[:, n:n + 1], in1=k.tmp2k[:, :],
                                         op0=ALU.is_gt, op1=ALU.subtract).then_inc(s("tern"), 1)
                dve.wait_ge(s("tern"), n + 1)

            for half, loaded in enumerate(("x_first", "x_second")):
                ts = slice(half * NT // 2, (half + 1) * NT // 2)
                dve.wait_ge(s(loaded), 16)
                layer_stats(dve, c, k, k.x, range(ts.start, ts.stop))
                c.step(dve.tensor_scalar(k.var[:, ts], k.mv[:, ts, 1], 1e-5, None, ALU.add))
                rsqrt(dve, c, k.rstd[:, ts], k.tmp8[:, ts], k.var[:, ts])
                for t in range(ts.start, ts.stop):
                    dve.tensor_scalar(k.xn[:, t, :], k.x[:, t, :], k.mv[:, t, 0:1], k.rstd[:, t:t + 1],
                                      ALU.subtract, ALU.mult).then_inc(s("xn"), 1)
            dve.wait_ge(s("cols"), 16)
            dve.wait_ge(s("w_ffn"), 32)
            for n, (what, g, half) in enumerate(jobs):
                if n < 2:
                    dve.tensor_reduce(k.wsum[:, n:n + 1], weights[n][:, :, :].rearrange("p a b -> p (a b)"), AX.X, ALU.add,
                                      apply_absolute_value=True).then_inc(s("wsum"), 1)
                dve.wait_ge(s("proj"), n + 1)
                dve.wait_ge(s("hi"), n + 1)
                sl = slice(half * BANK, (half + 1) * BANK)
                if what == "k":
                    hi = k.khi[:, n % 2, :].bitcast(F32)
                    c.step(dve.tensor_scalar(k.tmp512[:, :], hi, k.cols[:, 1:2], None, ALU.mult))
                    dve.scalar_tensor_tensor(out=k.khl[:, g, sl], in0=k.ps[:, n % 4, :], scalar=k.cols[:, 0:1],
                                             in1=k.tmp512[:, :], op0=ALU.mult, op1=ALU.add).then_inc(s("lo"), 1)
                    dve.wait_ge(s("lo"), n + 1)
                else:
                    dve.scalar_tensor_tensor(out=k.qlo[:, g, sl], in0=k.ps[:, n % 4, :], scalar=float(HD) ** -0.5,
                                             in1=k.qhi[:, g, sl].bitcast(F32), op0=ALU.mult, op1=ALU.subtract).then_inc(s("lo"), 1)
                if n == 1:
                    dve.wait_ge(s("gamma"), 1)
                    c.step(dve.tensor_scalar(k.gamma[:, :], k.ps[:, 6, 0:2], 1.0 / (FF * D), None, ALU.mult))
                    c.step(dve.tensor_scalar(k.thr[:, :], k.gamma[:, :], 1e-6, 0.5, ALU.add, ALU.mult))
                    c.step(dve.tensor_scalar(k.nthr[:, :], k.thr[:, :], -1.0, None, ALU.mult))
                    ternarise(0)
                if n == 7:
                    ternarise(1)
            dve.wait_ge(s("mask"), 16)
            dve.wait_ge(s("ident"), 16)
            c.step(dve.tensor_copy(k.ident_bf[:, :], k.ident[:, :]))
            c.step(dve.tensor_copy(k.mask_bf[:, :], k.mask[:, :]))


def attention(nc, ctx, k, name, hu, passes, value, width, lag_short, pool_unit=None, extra=None):
    s = Stage(ctx, nc, name)
    units = [(g, qt) for g in range(NH // hu) for qt in range(NT)]
    steps = [(u, j) for u in range(len(units)) for j in range(hu)]
    qt_of = [units[u][1] for u, _ in steps]
    n_ch = [1 if q < 4 else 2 for q in qt_of]
    first_ch = [sum(n_ch[:i]) for i in range(len(steps) + 1)]
    NS = len(steps)
    turn_steps, n = [], 0
    while n < NS:
        i = len(turn_steps)
        m = max(n, min(NS, i + 1 - (lag_short if i < NS and n_ch[i] == 1 else 2)))
        turn_steps.append(range(n, m))
        n = m
    turned_at = {i2: i for i, r in enumerate(turn_steps) for i2 in r}
    pv_round = [turned_at[hu * u + hu - 1] + 2 for u in range(len(units))]
    for u in reversed(range(len(units) - 2)):
        pv_round[u] = min(pv_round[u], turned_at[hu * (u + 2)] - 1, pv_round[u + 1] - 1)
    pv_at = {r: u for u, r in enumerate(pv_round)}
    rounds = max(pv_at) + 2

    def turns(i):
        return turn_steps[i] if i < len(turn_steps) else ()

    def scores_of(i):
        return k.ps[:, first_ch[i] % 4:first_ch[i] % 4 + n_ch[i], :].rearrange("p a b -> p (a b)")[:, 0:(qt_of[i] + 1) * P]

    def probs_of(i, c0, c1):
        at = (first_ch[i] % 6) * BANK
        return k.prob[:, :, :].rearrange("p a b -> p (a b)")[:, at + c0:at + c1]

    if extra is not None:
        extra.bind(s, steps, units)

    def even(n):
        return (n + 1) // 2

    def odd(n):
        return n // 2

    with nc.Block() as block:

        @block.tensor
        def _(pe):
            if extra is not None:
                extra.pe_first(pe)
            for i in range(rounds):
                if i < NS:
                    u, j = steps[i]
                    qt = qt_of[i]
                    if extra is not None:
                        extra.pe(pe, i)
                    if pool_unit is not None:
                        pe.wait_ge(s("q_masked"), 2 * (u + 1))
                    before = sum(1 for m in range(i) if first_ch[m] < first_ch[i + 1] - 4)
                    if before:
                        pe.wait_ge(s("exp"), before)
                    nk = (qt + 1) * P
                    for c0 in range(0, nk, BANK):
                        n = min(BANK, nk - c0)
                        out = k.ps[:, first_ch[i] % 4 + c0 // BANK, 0:n]
                        last = c0 + n == nk
                        ps = passes(i, u, j, qt)
                        for m, (q, kk) in enumerate(ps):
                            ins = pe.matmul(out, q, kk[:, c0:c0 + n], start=(m == 0), stop=(m == len(ps) - 1 and not last))
                        if last:
                            ins = pe.matmul(out[:, n - P:n], k.ident_bf[:, :], k.mask_bf[:, :], start=False, stop=True)
                    ins.then_inc(s("scores"), 1)
                for i2 in turns(i):
                    pe.wait_ge(s("exp"), i2 + 1)
                    for ch in range(n_ch[i2]):
                        n = first_ch[i2] + ch
                        if n >= 2:
                            pe.wait_ge(s("out_even" if n % 2 == 0 else "out_odd"), n // 2)
                        for b in range(4 * ch, min(4 * ch + 4, qt_of[i2] + 1)):
                            ins = pe.transpose(k.ps[:, 4 + n % 2, (b % 4) * P:(b % 4 + 1) * P],
                                               probs_of(i2, b * P, (b + 1) * P), k.ident[:, :])
                        ins.then_inc(s("turned"), 1)
                if i in pv_at:
                    u = pv_at[i]
                    g, qt = units[u]
                    n = first_ch[hu * u + hu]
                    pe.wait_ge(s("out_even"), even(n))
                    pe.wait_ge(s("out_odd"), odd(n))
                    if u >= 1:
                        pe.wait_ge(s("o_out"), u)
                    for b in range(qt + 1):
                        for jj in range(hu):
                            ins = pe.matmul(k.ps[width * jj:width * (jj + 1), 6, 0:P], value(b, g * hu + jj),
                                            k.pT[:, u % 2, jj, b * P:(b + 1) * P], start=(b == 0), stop=(b == qt))
                    ins.then_inc(s("pv"), 1)

        def take_out(eng, i2, parity, copy):
            u, j = steps[i2]
            for ch in range(n_ch[i2]):
                n = first_ch[i2] + ch
                if n % 2 != parity:
                    continue
                eng.wait_ge(s("turned"), n + 1)
                if u >= 2:
                    eng.wait_ge(s("pv"), u - 1)
                w = (min(4 * ch + 4, qt_of[i2] + 1) - 4 * ch) * P
                copy(k.pT[:, u % 2, j, ch * BANK:ch * BANK + w], k.ps[:, 4 + parity, 0:w])

        @block.vector
        def _(dve):
            if extra is not None:
                extra.dve_first(dve)
            for i in range(rounds):
                if i < NS:
                    dve.wait_ge(s("scores"), i + 1)
                    u, j = steps[i]
                    dve.tensor_reduce(k.nmax[:, qt_of[i], units[u][0] * hu + j:units[u][0] * hu + j + 1], scores_of(i), AX.X, ALU.max,
                                      negate=True).then_inc(s("max"), 1)
                for i2 in turns(i):
                    take_out(dve, i2, 1, lambda o, a: dve.tensor_copy(o, a).then_inc(s("out_odd"), 1))
                if i - 1 in pv_at:
                    u = pv_at[i - 1]
                    g, qt = units[u]
                    dve.wait_ge(s("pv"), u + 1)
                    dve.tensor_copy(k.oT[:, g, qt * P:(qt + 1) * P], k.ps[:, 6, 0:P]).then_inc(s("o_out"), 1)
                if extra is not None and i < NS:
                    extra.dve(dve, i)

        @block.scalar
        def _(act):
            if extra is not None:
                extra.act_first(act)
            for i in range(rounds):
                for i2 in turns(i):
                    take_out(act, i2, 0, lambda o, a: act.activation(o, a, ACT.Copy).then_inc(s("out_even"), 1))
                if i < NS:
                    nk = (qt_of[i] + 1) * P
                    u, j = steps[i]
                    h = units[u][0] * hu + j
                    act.wait_ge(s("max"), i + 1)
                    if first_ch[i + 1] > 6:
                        act.wait_ge(s("turned"), first_ch[i + 1] - 6)
                    act.activation(probs_of(i, 0, nk), scores_of(i), ACT.Exp, bias=k.nmax[:, qt_of[i], h:h + 1],
                                   accum_out=k.den[:, qt_of[i], h:h + 1]).then_inc(s("exp"), 1)
                if extra is not None and i < NS:
                    extra.act(act, i)

        if pool_unit is not None:
            @block.gpsimd
            def _(pool):
                for u, (g, qt) in enumerate(units):
                    if u >= 2:
                        pool.wait_ge(s("scores"), hu * (u - 1))
                    pool_unit(pool, s, u, g, qt)
        if extra is not None:
            @block.gpsimd
            def _(pool):
                extra.pool(pool)

            @block.sync
            def _(sp):
                extra.sync(sp)


def attend_a(nc, ctx, k):
    def masked(pool, s, u, g, qt):
        for part, q in enumerate((k.qhi, k.qlo)):
            src = q[:, g, qt * P:(qt + 1) * P].bitcast(F32).unsqueeze(1).broadcast_to([P, 4, P])
            row = k.cols[:, 4:8].unsqueeze(2).broadcast_to([P, 4, P])
            pool.tensor_tensor(k.qm[:, u % 2, part, :, :], src, row, ALU.mult).then_inc(s("q_masked"), 1)

    def passes(i, u, j, qt):
        g = u // NT
        return [(k.qm[:, u % 2, part, j, :], k.khl[:, g, :]) for part in range(2)]

    attention(nc, ctx, k, "aa", 4, passes, lambda b, h: k.v_a[:, b, h, :], 32, 3, pool_unit=masked)


def finish_attention(nc, ctx, k, name, ng, sel, row=None):
    s = Stage(ctx, nc, name)
    parts = [(half, g) for half in range(2) for g in range(ng)]

    def of(n):
        half, g = parts[n]
        return g, slice(half * BANK, (half + 1) * BANK)

    def parts_before(t):
        return range(ng + 2 * t, ng + 2 * t + 2) if 2 * t < ng else ()
    def lo(eng, n, sem):
        g, sl = of(n)
        eng.wait_ge(s("o_hi"), n + 1)
        eng.tensor_tensor(k.o_lo[:, g, sl], k.oT[:, g, sl], k.o_hi[:, g, sl].bitcast(F32), ALU.subtract).then_inc(s(sem), 1)

    with nc.Block() as block:

        @block.tensor
        def _(pe):
            def spread_product(n):
                g, sl = of(n)
                if n >= 4:
                    pe.wait_ge(s("o_norm"), n - 3)
                pe.matmul(k.ps[:, n % 4, :], sel[:, g, :], k.rT[:, sl], start=True, stop=True).then_inc(s("spread"), 1)

            def project(t):
                done = ng if t < 4 else 2 * ng
                pe.wait_ge(s("o_hi"), done)
                pe.wait_ge(s("o_lo_even"), done // 2)
                pe.wait_ge(s("o_lo_odd"), done // 2)
                if t >= 2:
                    pe.wait_ge(s("x_new"), t - 1)
                for g in range(ng):
                    for m, (o, w) in enumerate(((k.o_hi, k.wo_hi), (k.o_lo, k.wo_hi), (k.o_hi, k.wo_lo))):
                        ins = pe.matmul(k.ps[:, 4 + t % 2, 0:D], o[:, g, t * P:(t + 1) * P], w[:, g, :],
                                        start=(g == 0 and m == 0), stop=(g == ng - 1 and m == 2))
                ins.then_inc(s("proj"), 1)

            if row is not None:
                pe.matmul(k.ps[:, 7, 0:D], k.ones[:, :], row, start=True, stop=True).then_inc(s("row"), 1)
            pe.wait_ge(s("parts"), 1)
            turned = k.ps[0:96, 6, :].bitcast(BF16)
            for t in range(NT):
                ins = pe.transpose(turned[:, t * P:(t + 1) * P], k.r3[:, t, :], k.ident_bf[:, :])
            ins.then_inc(s("rT"), 1)
            pe.wait_ge(s("rT_out"), 1)
            for n in range(ng):
                spread_product(n)
            pe.wait_ge(s("w_hi"), 1)
            pe.wait_ge(s("w_lo"), 1)
            for t in range(NT):
                for n in parts_before(t):
                    spread_product(n)
                project(t)

        @block.scalar
        def _(act):
            act.activation(k.wo_hi[:, :, :], k.w_out[:, :, :], ACT.Copy).then_inc(s("w_hi"), 1)
            if row is not None:
                act.wait_ge(s("row"), 1)
                act.activation(k.row_all[:, :], k.ps[:, 7, 0:D], ACT.Copy).then_inc(s("row_out"), 1)
            act.wait_ge(s("rT"), 1)
            act.activation(k.rT[:, :], k.ps[0:96, 6, :].bitcast(BF16), ACT.Copy).then_inc(s("rT_out"), 1)
            for n in range(len(parts)):
                g, sl = of(n)
                act.wait_ge(s("o_norm"), n + 1)
                act.activation(k.o_hi[:, g, sl], k.oT[:, g, sl], ACT.Copy).then_inc(s("o_hi"), 1)

        @block.gpsimd
        def _(pool):
            if row is not None:
                pool.wait_ge(s("row_out"), 1)
                pool.tensor_tensor(k.x[:, :, :], k.x[:, :, :], k.row_all[:, :].unsqueeze(1).broadcast_to([P, NT, D]),
                                   ALU.add).then_inc(s("x_row"), 1)
            for n in range(0, len(parts), 2):
                lo(pool, n, "o_lo_even")

        @block.vector
        def _(dve):
            c = Chain(dve, s("dve"))

            def normalise(n):
                g, sl = of(n)
                o = k.oT[:, g, sl]
                dve.wait_ge(s("spread"), n + 1)
                dve.tensor_tensor(o, k.ps[:, n % 4, :], o, ALU.mult).then_inc(s("o_norm"), 1)
                if n >= 2 and n % 2 == 0:
                    lo(dve, n - 1, "o_lo_odd")
                if n == len(parts) - 1:
                    lo(dve, n, "o_lo_odd")

            def add(t):
                dve.wait_ge(s("proj"), t + 1)
                dve.tensor_tensor(k.x[:, t, :], k.ps[:, 4 + t % 2, 0:D], k.x[:, t, :], ALU.add).then_inc(s("x_new"), 1)
                dve.wait_ge(s("x_new"), t + 1)
                c.step(dve.bn_stats(k.stats[:, t, 0:6], k.x[:, t, :]))
                c.step(dve.bn_aggr(k.mv[:, t, :], k.stats[:, t, 0:6]))

            c.step(dve.reciprocal(k.den[:, :, :], k.den[:, :, :]))
            for part in range(3):
                r = k.r3[:, :, 32 * part:32 * part + NH]
                if part == 2:
                    dve.tensor_copy(r, k.den[:, :, :]).then_inc(s("parts"), 1)
                else:
                    c.step(dve.tensor_copy(r, k.den[:, :, :]))
                    c.step(dve.tensor_tensor(k.den[:, :, :], k.den[:, :, :], r, ALU.subtract))
            dve.wait_ge(s("w_hi"), 1)
            dve.tensor_tensor(k.wo_lo[:, :, :], k.w_out[:, :, :], k.wo_hi[:, :, :].bitcast(F32), ALU.subtract).then_inc(s("w_lo"), 1)
            for n in range(ng):
                normalise(n)
            if row is not None:
                dve.wait_ge(s("x_row"), 1)
            for t in range(NT):
                for n in parts_before(t):
                    normalise(n)
                add(t)


def ffn_norm(dve, c, k):
    e1, e2 = 1e-5, 1e-6
    c.step(dve.tensor_scalar(k.var[:, :], k.mv[:, :, 1], 1.0 + e2, e1 * e2, ALU.mult, ALU.add))
    rsqrt(dve, c, k.rstd[:, :], k.tmp8[:, :], k.var[:, :])
    return dve.tensor_scalar(k.sc_fc[:, :], k.rstd[:, :], k.gamma[:, 0:1], None, ALU.mult)


def ffn(nc, ctx, k, name, out=None, beside=None):
    s = Stage(ctx, nc, name)

    def x_turn(t):
        return t + 2 * max(0, t - 2)

    def hidden_turn(t):
        return min(t + 3, NT) + 2 * t

    def dst(buf, part, w, b0):
        return buf[:, part, b0:b0 + w, :].rearrange("p a b -> p (a b)")

    def chunks(t):
        return [(hidden_turn(t) + c, k.hT[:, t % 2], 4 * c) for c in range(2)]

    with nc.Block() as block:

        @block.tensor
        def _(pe):
            def turn(n, src, w):
                if n >= 3:
                    pe.wait_ge(s("hi"), n - 2)
                    pe.wait_ge(s("lo"), n - 2)
                for b in range(w):
                    ins = pe.transpose(k.ps[:, 4 + n % 3, b * P:(b + 1) * P], src[:, b * P:(b + 1) * P], k.ident[:, :])
                ins.then_inc(s("turned"), 1)

            def fc(t):
                pe.wait_ge(s("hi"), x_turn(t) + 1)
                pe.wait_ge(s("lo"), x_turn(t) + 1)
                if t >= 2:
                    pe.wait_ge(s("gelu"), t - 1)
                for n in range(2):
                    for m, (part, a) in enumerate([(part, a) for part in range(2) for a in range(KO)]):
                        ins = pe.matmul(k.ps[:, 2 * (t % 2) + n, :], k.xqT[:, t % 3, part, a, :],
                                        k.t_fc[:, a, n * BANK:(n + 1) * BANK], start=(m == 0), stop=(m == 2 * KO - 1))
                ins.then_inc(s("fc"), 1)

            def proj(t):
                pe.wait_ge(s("hi"), hidden_turn(t) + 2)
                pe.wait_ge(s("lo"), hidden_turn(t) + 2)
                if t >= 1:
                    pe.wait_ge(s("o_raw"), t)
                for f in range(FO):
                    for part in range(2):
                        ins = pe.matmul(k.ps[:, 7, 0:D], k.hT[:, t % 2, part, f, :], k.t_pr[:, f, :],
                                        start=(f == 0 and part == 0), stop=(f == FO - 1 and part == 1))
                ins.then_inc(s("proj"), 1)

            for t in range(NT + 3):
                if 1 <= t < NT + 1:
                    fc(t - 1)
                if t < NT:
                    if t < 2:
                        pe.wait_ge(s("x_clip_dve"), t + 1)
                    else:
                        pe.wait_ge(s("x_clip"), t - 1)
                    turn(x_turn(t), k.xn[:, t, :], KO)
                if 2 <= t < NT + 2:
                    pe.wait_ge(s("h_clip"), t - 1)
                    for c in range(2):
                        turn(hidden_turn(t - 2) + c, k.hc[:, (t - 2) % 2, c * BANK:(c + 1) * BANK], 4)
                if t >= 3:
                    proj(t - 3)

        @block.scalar
        def _(act):
            act.activation(k.warm[:, :], k.ones[:, 0:1], ACT.Gelu)

            def hi(n, buf, w, b0):
                act.wait_ge(s("turned"), n + 1)
                act.activation(dst(buf, 0, w, b0), k.ps[:, 4 + n % 3, 0:w * P], ACT.Copy).then_inc(s("hi"), 1)

            for t in range(NT + 4):
                if t >= 4:
                    act.wait_ge(s("proj"), t - 3)
                    act.activation(k.o_raw[:, t - 4, :], k.ps[:, 7, 0:D], ACT.Copy).then_inc(s("o_raw"), 1)
                if t < NT:
                    if t >= 3:
                        act.wait_ge(s("fc"), t - 2)
                    hi(x_turn(t), k.xqT[:, t % 3], KO, 0)
                if 1 <= t < NT + 1:
                    h = t - 1
                    if h == 0:
                        act.wait_ge(s("scale"), 1)
                    act.wait_ge(s("fc"), h + 1)
                    if h >= 2:
                        act.wait_ge(s("squared"), h - 1)
                    act.activation(k.h[:, h % 2, :], k.ps[:, 2 * (h % 2):2 * (h % 2) + 2, :].rearrange("p a b -> p (a b)"),
                                   ACT.Gelu, scale=k.sc_fc[:, h:h + 1], accum_out=k.hsum[:, h:h + 1]).then_inc(s("gelu"), 1)
                    act.wait_ge(s("gelu"), h + 1)
                    act.activation(k.nmean[:, h:h + 1], k.hsum[:, h:h + 1], ACT.Copy, scale=-1.0 / FF).then_inc(s("mean"), 1)
                    act.wait_ge(s("mean"), h + 1)
                    if h >= 2:
                        act.wait_ge(s("turned"), hidden_turn(h - 2) + 2)
                    act.activation(k.hc[:, h % 2, :], k.h[:, h % 2, :], ACT.Identity,
                                   bias=k.nmean[:, h:h + 1]).then_inc(s("centred"), 1)
                if 2 <= t < NT + 2:
                    if t >= 4:
                        act.wait_ge(s("proj"), t - 3)
                    for n, buf, b0 in chunks(t - 2):
                        hi(n, buf, 4, b0)
                if 1 <= t < NT + 1:
                    h = t - 1
                    act.wait_ge(s("centred"), h + 1)
                    act.activation(k.h[:, h % 2, :], k.h[:, h % 2, :], ACT.Square, bias=k.nmean[:, h:h + 1],
                                   accum_out=k.hsq[:, h:h + 1]).then_inc(s("squared"), 1)

        @block.gpsimd
        def _(pool):
            for t in range(2, NT + 1):
                if t < NT:
                    pool.tensor_scalar(k.xn[:, t, :], k.x[:, t, :], k.mv[:, t, 0:1], None, ALU.subtract).then_inc(s("x_centred"), 1)
                if t >= 3:
                    pool.wait_ge(s("x_max"), t - 2)
                    pool.tensor_scalar(k.xn[:, t - 1, :], k.xn[:, t - 1, :], k.xbig[:, t - 1, 0:1], k.xbig[:, t - 1, 1:2],
                                       ALU.min, ALU.max).then_inc(s("x_clip"), 1)
            if beside is not None:
                beside.gpsimd(pool)

        @block.vector
        def _(dve):
            c = Chain(dve, s("dve"))

            def x_all(t):
                xc = k.xn[:, t, :]
                c.step(dve.tensor_scalar(xc, k.x[:, t, :], k.mv[:, t, 0:1], None, ALU.subtract))
                c.step(dve.tensor_reduce(k.xbig[:, t, 0:1], xc, AX.X, ALU.max, apply_absolute_value=True))
                c.step(dve.tensor_scalar(k.xbig[:, t, 1:2], k.xbig[:, t, 0:1], -1.0, None, ALU.mult))
                dve.tensor_scalar(xc, xc, k.xbig[:, t, 0:1], k.xbig[:, t, 1:2], ALU.min, ALU.max).then_inc(s("x_clip_dve"), 1)

            def x_max(t):
                dve.wait_ge(s("x_centred"), t - 1)
                c.step(dve.tensor_reduce(k.xbig[:, t, 0:1], k.xn[:, t, :], AX.X, ALU.max, apply_absolute_value=True))
                dve.tensor_scalar(k.xbig[:, t, 1:2], k.xbig[:, t, 0:1], -1.0, None, ALU.mult).then_inc(s("x_max"), 1)

            def hidden_clip(t):
                hc = k.hc[:, t % 2, :]
                dve.wait_ge(s("centred"), t + 1)
                c.step(dve.tensor_reduce(k.big[:, 2:3], hc, AX.X, ALU.max, apply_absolute_value=True))
                c.step(dve.tensor_scalar(k.big[:, 3:4], k.big[:, 2:3], -1.0, None, ALU.mult))
                dve.tensor_scalar(hc, hc, k.big[:, 2:3], k.big[:, 3:4], ALU.min, ALU.max).then_inc(s("h_clip"), 1)
                dve.wait_ge(s("h_clip"), t + 1)

            def lo(n, buf, w, b0):
                dve.wait_ge(s("hi"), n + 1)
                dve.tensor_tensor(dst(buf, 1, w, b0), k.ps[:, 4 + n % 3, 0:w * P], dst(buf, 0, w, b0).bitcast(F32),
                                  ALU.subtract).then_inc(s("lo"), 1)

            x_all(0)
            x_all(1)
            for t in range(NT + 2):
                if t < NT:
                    lo(x_turn(t), k.xqT[:, t % 3], KO, 0)
                if t == 0:
                    ffn_norm(dve, c, k).then_inc(s("scale"), 1)
                    x_max(2)
                if t + 3 < NT:
                    x_max(t + 3)
                if 1 <= t < NT + 1:
                    hidden_clip(t - 1)
                if t >= 2:
                    for n, buf, b0 in chunks(t - 2):
                        lo(n, buf, 4, b0)
            dve.wait_ge(s("scale"), 1)
            dve.wait_ge(s("squared"), NT)
            c.step(dve.tensor_scalar(k.var[:, :], k.hsq[:, :], 1.0 / FF, 1e-6, ALU.mult, ALU.add))
            rsqrt(dve, c, k.rstd[:, :], k.tmp8[:, :], k.var[:, :])
            c.step(dve.tensor_scalar(k.sc_pr[:, :], k.rstd[:, :], k.gamma[:, 1:2], None, ALU.mult))
            for t in range(NT):
                dve.wait_ge(s("o_raw"), t + 1)
                dve.scalar_tensor_tensor(out=k.x[:, t, :], in0=k.o_raw[:, t, :], scalar=k.sc_pr[:, t:t + 1],
                                         in1=k.x[:, t, :], op0=ALU.mult, op1=ALU.add).then_inc(s("x_new"), 1)

        if beside is not None:
            @block.sync
            def _(sp):
                beside.sync(sp)

        if out is not None:
            @block.sync
            def _(sp):
                for t in range(NT):
                    sp.wait_ge(s("x_new"), t + 1)
                    sp.dma_start(out[0, t * P:(t + 1) * P, :], k.x[:, t, :]).then_inc(s("stored"), 16)
                sp.wait_ge(s("stored"), 16 * NT)


class LoadB:

    def __init__(self, ctx, nc, k, io):
        self.s, self.k, self.io = Stage(ctx, nc, "lb"), k, io

    def sync(self, sp):
        k, io = self.k, self.io
        for dst, src in ((k.w_qr[:, 0, :], io["L0_attn_b_W_qr"][0:P]), (k.w_qr[0:QL2, 1, :], io["L0_attn_b_W_qr"][P:QL]),
                         (k.w_qr[QL2:P, 1, :], io["L0_attn_b_W_qr"][P:QL]),
                         (k.w_kr[:, :, :], io["L0_attn_b_W_kr"].rearrange("(a p) n -> p a n", p=P))):
            sp.dma_start(dst, src).then_inc(self.s("rope_loaded"), 16)
        for dst, src in ((k.w_qc[:, 0, :], io["L0_attn_b_W_qc"][0:P]), (k.w_qc[0:QL2, 1, :], io["L0_attn_b_W_qc"][P:QL]),
                         (k.w_kc[:, :], io["L0_attn_b_W_kc"]), (k.w_v[:, :], io["L0_attn_b_W_v"]),
                         (k.w_ob[:, :, :], io["L0_attn_b_W_o"].rearrange("(h p) n -> p h n", p=P)),
                         (k.w_cp[:, :, 0:QL], io["L0_attn_b_W_cp"].rearrange("(a p) n -> p a n", p=P)),
                         (k.w_cp[:, :, QL:QL + QL2], io["L0_attn_b_W_cp"].rearrange("(a p) n -> p a n", p=P)[:, :, P:QL]),
                         (k.w_ck[:, :, 0:KVL], io["L0_attn_b_W_c"].rearrange("(a p) n -> p a n", p=P)),
                         (k.cos[:, :], io["cos"]), (k.sin[:, :], io["sin"])):
            sp.dma_start(dst, src).then_inc(self.s("loaded"), 16)
        sp.wait_ge(self.s("loaded"), 16 * 10)

    def gpsimd(self, pool):
        k, s = self.k, self.s
        pool.wait_ge(s("rope_loaded"), 16 * 4)
        for half in range(2):
            cols = slice(KVL + 32 * half, KVL + 32 * half + 32)
            w = [k.w_qr[:, a, :].rearrange("p (h f two) -> p h f two", two=2, f=32)[:, :, :, half] for a in range(2)]
            pool.tensor_copy(k.aw0[:, :, cols], w[0]).then_inc(s("rope_cols"), 1)
            pool.tensor_copy(k.aw1[:, :, cols], w[1]).then_inc(s("rope_hi"), 1)
            pool.wait_ge(s("rope_hi"), half + 1)
            pool.tensor_tensor(k.aw1[QL2:P, :, cols], w[1][QL2:P], k.aw1[QL2:P, :, cols].bitcast(F32), ALU.subtract)\
                .then_inc(s("rope_lo"), 1)
            pool.wait_ge(s("rope_lo"), half + 1)
            pool.tensor_copy(k.w_ck[:, :, KVL + 32 * half:KVL + 32 * half + 32],
                             k.w_kr[:, :, :].rearrange("p a (f two) -> p a f two", two=2)[:, :, :, half])\
                .then_inc(s("rope_cols"), 1)


def prepare_b(nc, ctx, k, io):
    s = Stage(ctx, nc, "pb")
    J = IH * TOPK
    order = ([("w", h) for h in range(8)] + [("a", 0), ("a", 1)] + [("x", t) for t in range(NT)]
             + [("sparse", 1), ("k", 0), ("k", 1), ("cp", 0), ("sparse", 2), ("cp", 1), ("sparse", 3), ("cp", 2)]
             + [("sparse", 4), ("cp", 3), ("sparse", 5), ("vo", 0), ("sparse", 6)]
             + [("vo", n) for n in range(1, 4)] + [("sparse", 7), ("w", 8), ("w", 9), ("sparse", 8), ("w", 10)]
             + [("w", 11), ("sparse", 9), ("w", 12), ("w", 13), ("w", 14), ("w", 15), ("sparse", 10), ("c", 0), ("a", 2)]
             + [("a", 3)] + [("vo", n) for n in range(4, 8)])
    jobs = [x for x in order if x[0] != "sparse"]
    at = {j: n for n, j in enumerate(jobs)}
    lo_jobs = [x for x in jobs if x[0] == "a" or x in (("cp", 2), ("cp", 3))]
    KC = QL + QL2
    WV = KC + KVL
    eye8, mean8, tokens, block_mask = k.small[0:IH, 0:IH], k.small[0:J, 8:16], k.small[:, 16:24], k.small[0:J, 24:24 + J]
    ps6, ps7 = k.ps[:, 6, :], k.ps[:, 7, :]

    with nc.Block() as block:

        @block.sync
        def _(sp):
            for dst, src in ((k.w_gate[:, :, :], io["L0_attn_b_W_gate"].rearrange("(a p) n -> p a n", p=P)),
                             (k.small[:, :], io["small"])):
                sp.dma_start(dst, src).then_inc(s("gate_loaded"), 16)
            for dst, src in ((k.w_idx[:, :, :], io["L0_attn_b_W_idx"].rearrange("(a p) n -> p a n", p=P)),
                             (k.w_s[:, 0, :], io["L0_attn_b_W_sq"]), (k.w_s[:, 1, :], io["L0_attn_b_W_sk"]),
                             (k.w_s[:, 2, :], io["L0_attn_b_W_sv"]), (k.w_s[:, 3, :], io["L0_attn_b_W_iout"][:, 0:DV])):
                sp.dma_start(dst, src).then_inc(s("sparse_loaded"), 16)
            sp.wait_ge(s("job_out"), at[("k", 1)] + 1)
            sp.dma_start(k.kswp[KVL:KVL + 32, :], k.kraw[KVL + 32:P, :]).then_inc(s("swapped"), 16)
            sp.dma_start(k.kswp[KVL + 32:P, :], k.kraw[KVL:KVL + 32, :]).then_inc(s("swapped"), 16)
            sp.wait_ge(s("swapped"), 32)

        @block.gpsimd
        def _(pool):
            pool.memset(k.row[:, :], 0.0).then_inc(s("row_zero"), 1)

        @block.tensor
        def _(pe):
            def done(name):
                pe.wait_ge(s("job_out"), at[name] + 1)

            def sparse(n):
                if n == 1:
                    done(("x", NT - 1))
                    pe.wait_ge(s("gate_loaded"), 16 * 2)
                    for half in range(2):
                        for a in range(KO):
                            ins = pe.matmul(k.ps[0:IH, 6 + half, :], k.w_gate[:, a, :], k.xT[:, a, half * BANK:(half + 1) * BANK],
                                            start=(a == 0), stop=(a == KO - 1))
                elif n == 2:
                    pe.wait_ge(s("v_index"), 1)
                    ins = pe.matmul(ps6[:, 0:J], k.ones[0:IH, :], k.bd[:, :, :].rearrange("p a b -> p (a b)"), start=True, stop=True)
                elif n == 3:
                    pe.wait_ge(s("v_onehot"), NT)
                    for a in range(KO):
                        for t in range(NT):
                            ins = pe.matmul(ps7[:, a * J:(a + 1) * J], k.xn[:, t, a * P:(a + 1) * P], k.onehot[:, t, :],
                                            start=(t == 0), stop=(t == NT - 1))
                elif n == 4:
                    pe.wait_ge(s("sparse_loaded"), 16 * 5)
                    pe.wait_ge(s("v_xsel"), 1)
                    for h in range(IH):
                        for a in range(KO):
                            ins = pe.matmul(ps6[:, h * TOPK:(h + 1) * TOPK], k.w_idx[:, a, h * P:(h + 1) * P],
                                            k.xsel[:, a, h * TOPK:(h + 1) * TOPK], start=(a == 0), stop=(a == KO - 1))
                elif n == 5:
                    pe.wait_ge(s("v_sel"), 1)
                    pe.matmul(ps7[:, 0:J], k.w_s[:, 0, :], k.sel[:, :], start=True, stop=True)
                    pe.matmul(ps7[:, J:2 * J], k.w_s[:, 1, :], k.sel[:, :], start=True, stop=True)
                    ins = pe.matmul(ps7[0:J, 2 * J:2 * J + P], k.sel[:, :], k.w_s[:, 2, :], start=True, stop=True)
                elif n == 6:
                    pe.wait_ge(s("v_qkv"), 2)
                    ins = pe.matmul(ps6[0:J, 0:J], k.sqk[:, 0:J], k.sqk[:, J:2 * J], start=True, stop=True)
                elif n == 7:
                    pe.wait_ge(s("v_prob"), 1)
                    ins = pe.matmul(ps7[0:J, 0:IH], k.sprob[:, :], mean8, start=True, stop=True)
                elif n == 8:
                    pe.wait_ge(s("v_pm"), 1)
                    ins = pe.matmul(ps6[:, 0:IH], k.sv[:, :], k.chain[0:J, 0:IH], start=True, stop=True)
                elif n == 9:
                    pe.wait_ge(s("v_m"), 1)
                    ins = pe.matmul(ps7[:, 0:IH], k.w_s[:, 3, :], k.chain[:, 8:8 + IH], start=True, stop=True)
                else:
                    pe.wait_ge(s("v_io"), 1)
                    for h in range(NH):
                        ins = pe.matmul(ps6[32 * (h % 4):32 * (h % 4) + 1, 0:D], k.chain[:, 16 + h // 2:17 + h // 2], k.w_ob[:, h, :],
                                        start=(h < 4), stop=(h >= NH - 4))
                ins.then_inc(s("sparse"), 1)

            def job(n, what, i):
                b = k.ps[:, n % 6, :]
                if n >= 6:
                    done(jobs[n - 6])
                    if jobs[n - 6] in lo_jobs:
                        pe.wait_ge(s("lo"), lo_jobs.index(jobs[n - 6]) + 1)
                if what == "x":
                    pe.wait_ge(s("xn"), i + 1)
                    for a in range(KO):
                        ins = pe.transpose(b[:, a * P:(a + 1) * P], k.xn[:, i, a * P:(a + 1) * P], k.ident[:, :])
                elif what == "w":
                    cols = slice(i * P, (i + 1) * P)
                    pe.transpose(b[:, 0:P], k.w_qc[:, 0, cols], k.ident[:, :])
                    pe.transpose(b[:, P:QL], k.w_qc[0:QL2, 1, cols], k.ident[0:QL2, 0:QL2])
                    pe.transpose(b[:, QL:KC], k.w_qc[0:QL2, 1, cols], k.ident[0:QL2, 0:QL2])
                    pe.transpose(b[:, KC:WV], k.w_kc[:, cols], k.ident[0:KVL, 0:KVL])
                    ins = pe.transpose(b[:, WV:WV + KVL], k.w_v[:, cols], k.ident[0:KVL, 0:KVL])
                elif what == "k":
                    done(("x", NT - 1))
                    for a in range(KO):
                        ins = pe.matmul(b, k.w_ck[:, a, :], k.xT[:, a, i * BANK:(i + 1) * BANK], start=(a == 0), stop=(a == KO - 1))
                elif what == "cp":
                    for a in range(KO):
                        w = k.w_cp[:, a, 0:P] if i < 2 else k.w_cp[:, a, P:QL + QL2]
                        ins = pe.matmul(b, w, k.xT[:, a, (i % 2) * BANK:(i % 2 + 1) * BANK],
                                        start=(a == 0), stop=(a == KO - 1))
                elif what == "a":
                    done(("w", 4 * i + 3))
                    for h in range(4):
                        for part in range(2):
                            w = k.wT[:, (4 * i + h) % 8, :]
                            ins = pe.matmul(b[:, part * D + h * KVL:part * D + (h + 1) * KVL],
                                            w[:, part * P:(part + 1) * P], w[:, KC:WV], start=True, stop=True)
                elif what == "vo":
                    for j in range(2):
                        ins = pe.matmul(b[KVL * j:KVL * (j + 1), 0:D], k.wT[:, (2 * i + j) % 8, WV:WV + KVL],
                                        k.w_ob[:, 2 * i + j, :], start=True, stop=True)
                else:
                    done(("k", 1))
                    for t in range(NT):
                        ins = pe.transpose(b[:, t * KVL:(t + 1) * KVL], k.kraw[0:KVL, t * P:(t + 1) * P], k.ident[0:KVL, 0:KVL])
                ins.then_inc(s("job"), 1)

            for what, i in order:
                if what == "sparse":
                    sparse(i)
                else:
                    job(at[(what, i)], what, i)

        @block.scalar
        def _(act):
            for n, (what, i) in enumerate(jobs):
                b = k.ps[:, n % 6, :]
                half = slice((i % 2) * BANK, (i % 2 + 1) * BANK)
                if what == "x":
                    parts = [(k.xT[:, :, i * P:(i + 1) * P], b[:, 0:D].rearrange("p (a n) -> p a n", a=KO))]
                elif what == "w":
                    parts = [(k.wT[:, i % 8, :], b[:, 0:WV + KVL])]
                elif what == "k":
                    parts = [(k.kraw[:, half], b)]
                elif what == "cp":
                    parts = [(k.cp0[:, half] if i < 2 else k.cp1[:, half], b)]
                elif what == "a":
                    parts = [(w[:, 4 * i:4 * i + 4, 0:KVL], b[:, part * D:(part + 1) * D].rearrange("p (h n) -> p h n", h=4))
                             for part, w in enumerate((k.aw0, k.aw1))]
                elif what == "vo":
                    parts = [(k.w_vo[:, i, :], b[:, 0:D])]
                else:
                    parts = [(k.c_tok[:, :, :].rearrange("p t n -> p (t n)"), b)]
                if (what, i) == ("vo", 1):
                    act.wait_ge(s("v_smax"), 1)
                    act.activation(k.sprob[:, :], k.sprob[:, :], ACT.Exp, bias=k.scol[0:J, 0:1], accum_out=k.scol[0:J, 1:2])\
                        .then_inc(s("exp"), 1)
                if (what, i) == ("w", 8):
                    act.wait_ge(s("key"), 2)
                    act.activation(k.k_hi[:, :], k.key[:, :], ACT.Copy).then_inc(s("khi"), 1)
                act.wait_ge(s("job"), n + 1)
                for o, a in parts:
                    ins = act.activation(o, a, ACT.Copy)
                ins.then_inc(s("job_out"), 1)

        @block.vector
        def _(dve):
            c = Chain(dve, s("dve"))

            def sparse_done(n):
                dve.wait_ge(s("sparse"), n)

            def lo(name):
                what, i = name
                b = k.ps[:, at[name] % 6, :]
                dve.wait_ge(s("job_out"), at[name] + 1)
                if what == "cp":
                    half = slice((i - 2) * BANK, (i - 1) * BANK)
                    ins = dve.tensor_tensor(k.cp1_lo[0:QL2, half], b[0:QL2, :], k.cp1[0:QL2, half].bitcast(F32), ALU.subtract)
                else:
                    w = k.aw1[QL2:P, 4 * i:4 * i + 4, 0:KVL]
                    ins = dve.tensor_tensor(w, b[QL2:P, D:2 * D].rearrange("p (h n) -> p h n", h=4), w.bitcast(F32), ALU.subtract)
                ins.then_inc(s("lo"), 1)

            layer_stats(dve, c, k, k.x, range(NT))
            c.step(dve.tensor_scalar(k.var[:, :], k.mv[:, :, 1], 1e-5, None, ALU.add))
            rsqrt(dve, c, k.rstd[:, :], k.tmp8[:, :], k.var[:, :])
            for t in range(NT):
                dve.tensor_scalar(k.xn[:, t, :], k.x[:, t, :], k.mv[:, t, 0:1], k.rstd[:, t:t + 1],
                                  ALU.subtract, ALU.mult).then_inc(s("xn"), 1)
            lo(("a", 0))
            lo(("a", 1))
            sparse_done(1)
            c.step(dve.tensor_copy(k.gT[:, :], k.ps[0:IH, 6:8, :].rearrange("p a b -> p (a b)")))
            c.step(dve.max(k.top[:, :], k.gT[:, :]))
            c.step(dve.max_index(k.top_at[:, :], k.top[:, :], k.gT[:, :]))
            c.step(dve.tensor_copy(k.top[:, :], k.top_at[:, :]))
            dve.tensor_tensor(k.bd[:, :, :], k.top[:, :].unsqueeze(1).broadcast_to([IH, IH, TOPK]),
                              eye8.unsqueeze(2).broadcast_to([IH, IH, TOPK]), ALU.mult).then_inc(s("v_index"), 1)
            sparse_done(2)
            for t in range(NT):
                dve.tensor_scalar(k.onehot[:, t, :], ps6[:, 0:J], tokens[:, t:t + 1], None, ALU.is_equal).then_inc(s("v_onehot"), 1)
            dve.wait_ge(s("job_out"), at[("k", 1)] + 1)
            dve.tensor_tensor(k.key[:, :], k.kraw[:, :], k.cos[:, :], ALU.mult).then_inc(s("key"), 1)
            sparse_done(3)
            dve.tensor_copy(k.xsel[:, :, :].rearrange("p a b -> p (a b)"), ps7[:, 0:KO * J]).then_inc(s("v_xsel"), 1)
            dve.wait_ge(s("swapped"), 32)
            c.step(dve.tensor_tensor(k.kswp[KVL:P, :], k.kswp[KVL:P, :], k.sin[KVL:P, :], ALU.mult))
            sparse_done(4)
            dve.tensor_copy(k.sel[:, :], ps6[:, 0:J]).then_inc(s("v_sel"), 1)
            dve.wait_ge(s("key"), 1)
            dve.tensor_tensor(k.key[KVL:P, :], k.key[KVL:P, :], k.kswp[KVL:P, :], ALU.add).then_inc(s("key"), 1)
            sparse_done(5)
            dve.tensor_copy(k.sqk[:, :], ps7[:, 0:2 * J]).then_inc(s("v_qkv"), 1)
            dve.tensor_copy(k.sv[:, :], ps7[0:J, 2 * J:2 * J + P]).then_inc(s("v_qkv"), 1)
            lo(("cp", 2))
            lo(("cp", 3))
            sparse_done(6)
            c.step(dve.scalar_tensor_tensor(out=k.sprob[:, :], in0=ps6[0:J, 0:J], scalar=float(P) ** -0.5, in1=block_mask,
                                            op0=ALU.mult, op1=ALU.add))
            dve.tensor_reduce(k.scol[0:J, 0:1], k.sprob[:, :], AX.X, ALU.max, negate=True).then_inc(s("v_smax"), 1)
            dve.wait_ge(s("exp"), 1)
            c.step(dve.reciprocal(k.scol[0:J, 2:3], k.scol[0:J, 1:2]))
            dve.tensor_scalar(k.sprob[:, :], k.sprob[:, :], k.scol[0:J, 2:3], None, ALU.mult).then_inc(s("v_prob"), 1)
            sparse_done(7)
            dve.tensor_copy(k.chain[0:J, 0:IH], ps7[0:J, 0:IH]).then_inc(s("v_pm"), 1)
            sparse_done(8)
            dve.tensor_copy(k.chain[:, 8:8 + IH], ps6[:, 0:IH]).then_inc(s("v_m"), 1)
            sparse_done(9)
            dve.tensor_copy(k.chain[:, 16:16 + IH], ps7[:, 0:IH]).then_inc(s("v_io"), 1)
            dve.wait_ge(s("khi"), 1)
            c.step(dve.tensor_tensor(k.k_lo[:, :], k.key[:, :], k.k_hi[:, :].bitcast(F32), ALU.subtract))
            sparse_done(10)
            dve.wait_ge(s("row_zero"), 1)
            for j in range(4):
                last = c.start(dve.tensor_copy(k.row[32 * j:32 * j + 1, :], ps6[32 * j:32 * j + 1, 0:D]))
            c.wait(last)
            lo(("a", 2))
            lo(("a", 3))


class QueriesB:

    HALF_AT = (0, 3, 6, 9)
    HALF_AT_0 = (3, 5, 7, 9)
    SPLIT_AT = (12, 15)
    PER = 2 * NT
    FIRST = ((0, 0), (1, 0), (0, 1), (1, 1))

    def __init__(self, k):
        self.k = k

    def bind(self, s, steps, units):
        self.s, self.pairs = s, NH // 2

    def work(self, i):
        p, at = divmod(i, self.PER)
        if p + 1 >= self.pairs:
            return [], []
        return ([4 * (p + 1) + m for m, x in enumerate(self.HALF_AT if p else self.HALF_AT_0) if x == at],
                [2 * (p + 1) + m for m, x in enumerate(self.SPLIT_AT) if x == at])

    def bank(self, m):
        return self.k.ps[:, m if m < 4 else 7, :]

    def part(self, m):
        return self.FIRST[m] if m < 4 else divmod(m, 2)

    def product(self, pe, m):
        k, s, (h, half) = self.k, self.s, self.part(m)
        if m >= 5:
            pe.wait_ge(s("q_raw"), m)
            pe.wait_ge(s("q_cos"), m)
        sl = slice(half * BANK, (half + 1) * BANK)
        pe.matmul(self.bank(m), k.aw0[:, h, :], k.cp0[:, sl], start=True, stop=False)
        pe.matmul(self.bank(m), k.aw1[:, h, :], k.cp1[:, sl], start=False, stop=False)
        pe.matmul(self.bank(m), k.aw1[0:QL2, h, :], k.cp1_lo[0:QL2, sl], start=False, stop=True).then_inc(s("q_prod"), 1)

    def cosine(self, dve, m):
        k, s, (h, half) = self.k, self.s, self.part(m)
        sl = slice(half * BANK, (half + 1) * BANK)
        dve.wait_ge(s("q_prod"), m + 1)
        if h >= 2:
            dve.wait_ge(s("q_hi"), h - 1)
            dve.wait_ge(s("q_lo"), h - 1)
        dve.wait_ge(s("q_raw"), m + 1)
        dve.tensor_tensor(k.q1[:, h % 2, sl], self.bank(m), k.cos[:, sl], ALU.mult).then_inc(s("q_cos"), 1)

    def raw(self, act, m):
        k, s, (h, half) = self.k, self.s, self.part(m)
        act.wait_ge(s("q_prod"), m + 1)
        if h >= 2:
            act.wait_ge(s("q_swap0" if h % 2 == 0 else "q_swap1"), 32 * (h // 2))
        act.activation(k.qraw[KVL:P, h % 2, half * BANK:(half + 1) * BANK], self.bank(m)[KVL:P, :], ACT.Copy).then_inc(s("q_raw"), 1)

    def rope_first(self, dve, m):
        k, s, (h, half) = self.k, self.s, self.FIRST[m]
        sl = slice(half * BANK, (half + 1) * BANK)
        if half == 0:
            dve.wait_ge(s(f"q_swap_first{h}"), 32)
        else:
            dve.wait_ge(s(f"q_swap{h}"), 32)
        w = k.swp[KVL:P, h, sl]
        dve.tensor_tensor(w, w, k.sin[KVL:P, sl], ALU.mult).then_inc(s("q_sin_dve"), 1)
        dve.wait_ge(s("q_sin_dve"), m + 1)
        dve.wait_ge(s("q_cos"), m + 1)
        q = k.q1[KVL:P, h, sl]
        dve.tensor_tensor(q, q, w, ALU.add).then_inc(s("q_rope_first" if half == 0 else "q_rope_dve"), 1)

    def hi_first(self, act, m):
        k, s, (h, half) = self.k, self.s, self.FIRST[m]
        sl = slice(half * BANK, (half + 1) * BANK)
        act.wait_ge(s("q_rope_first" if half == 0 else "q_rope_dve"), h + 1)
        act.wait_ge(s("q_cos"), m + 1)
        act.activation(k.q_hl[:, 0, h, 0, sl], k.q1[:, h, sl], ACT.Copy).then_inc(s("q_hi_first" if half == 0 else "q_hi"), 1)

    def lo_first(self, dve, m):
        k, s, (h, half) = self.k, self.s, self.FIRST[m]
        sl = slice(half * BANK, (half + 1) * BANK)
        dve.wait_ge(s("q_hi_first" if half == 0 else "q_hi"), h + 1)
        dve.wait_ge(s("q_rope_first" if half == 0 else "q_rope_dve"), h + 1)
        dve.tensor_tensor(k.q_hl[:, 0, h, 1, sl], k.q1[:, h, sl], k.q_hl[:, 0, h, 0, sl].bitcast(F32), ALU.subtract)\
            .then_inc(s("q_lo_first" if half == 0 else "q_lo"), 1)

    def rope(self, pool, h):
        k, s = self.k, self.s
        pool.wait_ge(s("q_swap0" if h % 2 == 0 else "q_swap1"), 32 * (h // 2 + 1))
        w = k.swp[KVL:P, h % 2, :]
        pool.tensor_tensor(w, w, k.sin[KVL:P, :], ALU.mult).then_inc(s("q_sin"), 1)
        pool.wait_ge(s("q_sin"), h - 1)
        pool.wait_ge(s("q_cos"), 2 * h + 2)
        q = k.q1[KVL:P, h % 2, :]
        pool.tensor_tensor(q, q, w, ALU.add).then_inc(s("q_rope"), 1)

    def roped(self, eng, h):
        if h < 2:
            eng.wait_ge(self.s("q_rope_dve"), h + 1)
        else:
            eng.wait_ge(self.s("q_rope"), h - 1)

    def hi(self, act, h):
        k, s = self.k, self.s
        self.roped(act, h)
        act.wait_ge(s("q_cos"), 2 * h + 2)
        if h >= 4:
            act.wait_ge(s("scores"), self.PER * (h // 2 - 1))
        act.activation(k.q_hl[:, (h // 2) % 2, h % 2, 0, :], k.q1[:, h % 2, :], ACT.Copy).then_inc(s("q_hi"), 1)

    def lo(self, dve, h):
        k, s = self.k, self.s
        dve.wait_ge(s("q_hi"), h + 1)
        self.roped(dve, h)
        if h >= 4:
            dve.wait_ge(s("scores"), self.PER * (h // 2 - 1))
        dve.tensor_tensor(k.q_hl[:, (h // 2) % 2, h % 2, 1, :], k.q1[:, h % 2, :],
                          k.q_hl[:, (h // 2) % 2, h % 2, 0, :].bitcast(F32), ALU.subtract).then_inc(s("q_lo"), 1)

    def pe_first(self, pe):
        for m in range(4):
            self.product(pe, m)

    def dve_first(self, dve):
        for m in range(4):
            self.cosine(dve, m)
            if m >= 2:
                self.rope_first(dve, m - 2)
        for m in range(2):
            self.lo_first(dve, m)

    def act_first(self, act):
        for m in range(4):
            self.raw(act, m)
        for m in range(2):
            self.hi_first(act, m)

    def pe(self, pe, i):
        for m in self.work(i)[0]:
            self.product(pe, m)
        p, at = divmod(i, self.PER)
        if i < 2:
            pe.wait_ge(self.s("q_hi_first"), i + 1)
            pe.wait_ge(self.s("q_lo_first"), i + 1)
        if i in (NT, NT + 1):
            pe.wait_ge(self.s("q_hi"), i - NT + 1)
            pe.wait_ge(self.s("q_lo"), i - NT + 1)
        if p > 0 and at < 2:
            pe.wait_ge(self.s("q_hi"), 2 * p + at + 1)
            pe.wait_ge(self.s("q_lo"), 2 * p + at + 1)

    def dve(self, dve, i):
        if i in (0, 1):
            self.rope_first(dve, i + 2)
        if i in (2, 3):
            self.lo_first(dve, i)
        for m in self.work(i)[0]:
            self.cosine(dve, m)
        for h in self.work(i)[1]:
            self.lo(dve, h)

    def act(self, act, i):
        if i in (1, 2):
            self.hi_first(act, i + 1)
        for m in self.work(i)[0]:
            self.raw(act, m)
        for h in self.work(i)[1]:
            self.hi(act, h)

    def pool(self, pool):
        for h in range(2, NH):
            self.rope(pool, h)

    def sync(self, sp):
        k, s = self.k, self.s
        for m, (h, half) in enumerate(self.FIRST):
            sl = slice(half * BANK, (half + 1) * BANK)
            sp.wait_ge(s("q_raw"), m + 1)
            sem = s(f"q_swap_first{h}" if half == 0 else f"q_swap{h}")
            sp.dma_start(k.swp[KVL:KVL + 32, h, sl], k.qraw[KVL + 32:P, h, sl]).then_inc(sem, 16)
            sp.dma_start(k.swp[KVL + 32:P, h, sl], k.qraw[KVL:KVL + 32, h, sl]).then_inc(sem, 16)
        for h in range(2, NH):
            sp.wait_ge(s("q_raw"), 2 * h + 2)
            self.roped(sp, h - 2)
            sem = s("q_swap0" if h % 2 == 0 else "q_swap1")
            sp.dma_start(k.swp[KVL:KVL + 32, h % 2, :], k.qraw[KVL + 32:P, h % 2, :]).then_inc(sem, 16)
            sp.dma_start(k.swp[KVL + 32:P, h % 2, :], k.qraw[KVL:KVL + 32, h % 2, :]).then_inc(sem, 16)


def attend_b(nc, ctx, k):
    def passes(i, u, j, qt):
        q = [k.q_hl[:, (u // NT) % 2, j, part, qt * P:(qt + 1) * P] for part in range(2)]
        return [(q[0], k.k_hi), (q[0], k.k_lo), (q[1], k.k_hi)]

    attention(nc, ctx, k, "ab", 2, passes, lambda b, h: k.c_tok[:, b, :], KVL, 2, extra=QueriesB(k))


def build(nc, io, out):
    with ExitStack() as ctx:
        k = Tensors()

        def sb(name, shape, dt=F32, c=ctx):
            t = c.enter_context(nc.sbuf_tensor(name, shape, dt))
            return t

        k.ps = ctx.enter_context(nc.psum_tensor("banks", [P, 8, BANK], F32))
        k.x = sb("x", [P, NT, D])
        k.xn = sb("xn", [P, NT, D])
        k.t_fc = sb("t_fc", [P, KO, FF], F32R)
        k.t_pr = sb("t_pr", [P, FO, D], F32R)
        k.ident = sb("ident", [P, P])
        k.ident_bf = sb("ident_bf", [P, P], BF16)
        k.mask_bf = sb("mask_bf", [P, P], BF16)
        k.cols = sb("cols", [P, 8])
        k.ones = sb("ones", [P, P])
        k.stats = sb("stats", [P, NT, 6])
        k.mv = sb("mv", [P, NT, 2])
        k.var, k.rstd, k.tmp8, k.sc_fc, k.sc_pr = (sb(n, [P, NT]) for n in ("var", "rstd", "tmp8", "sc_fc", "sc_pr"))
        k.gamma, k.thr, k.nthr, k.wsum = (sb(n, [P, 2]) for n in ("gamma", "thr", "nthr", "wsum"))
        k.big = sb("big", [P, 4])
        k.nmax = sb("nmax", [P, NT, NH])
        k.den = sb("den", [P, NT, NH])
        k.r3 = sb("r3", [P, NT, 96], BF16)
        k.rT = sb("rT", [96, S], BF16)
        k.sel_bf = sb("sel_bf", [96, 12, P], BF16)

        with ExitStack() as a:
            k.w_o = sb("w_o_a", [P, 4, D], F32, a)
            k.v_a = sb("v_a", [P, NT, NH, 32], F32, a)
            k.qhi = sb("qhi", [P, 4, S], F32R, a)
            k.qlo = sb("qlo", [P, 4, S], F32R, a)
            k.khl = sb("khl", [P, 4, S], F32R, a)
            with ExitStack() as w:
                k.mask = sb("mask", [P, P], F32, w)
                k.sel_f = sb("sel_f", [96, 12, P], F32, w)
                k.w_qkv = sb("w_qkv", [P, KO, 3 * D], F32, w)
                k.wq2 = sb("wq2", [P, KO, NH, 2, HD], F32, w)
                k.wk2 = sb("wk2", [P, KO, NH, 2, HD], F32, w)
                k.w_fc = sb("w_fc", [P, FO, D], F32, w)
                k.w_pr = sb("w_pr", [P, KO, FF], F32, w)
                k.tmp2k = sb("tmp2k", [P, 2 * S], F32, w)
                k.tern_in = lambda n, b: (k.w_fc[:, 4 * (n % 2) + b, (n // 2) * P:(n // 2 + 1) * P] if n < 4 else
                                          k.w_pr[:, b % 2, (2 * (n - 4) + b // 2) * P:(2 * (n - 4) + b // 2 + 1) * P])
                k.tern_out = lambda n: (k.t_fc[:, n // 2, BANK * (n % 2):BANK * (n % 2 + 1)] if n < 4 else
                                        k.t_pr[:, 2 * (n - 4):2 * (n - 4) + 2, :].rearrange("p a b -> p (a b)"))
                k.xT = sb("xT_a", [P, KO, S], F32, w)
                k.khi = sb("khi", [P, 2, BANK], F32R, w)
                k.tmp512 = sb("tmp512", [P, BANK], F32, w)
                project_a(nc, ctx, k, io)
            k.oT = sb("oT_a", [P, 4, S], F32, a)
            with ExitStack() as w:
                k.qm = sb("qm", [P, 2, 2, 4, P], F32R, w)
                k.prob = sb("prob_a", [P, 3, S], F32, w)
                k.pT = sb("pT_a", [P, 2, 4, S], F32, w)
                attend_a(nc, ctx, k)
            k.w_out = k.w_o
            k.o_hi, k.o_lo = sb("o_hi_a", [P, 4, S], F32R, a), sb("o_lo_a", [P, 4, S], F32R, a)
            k.wo_hi, k.wo_lo = sb("wo_hi_a", [P, 4, D], F32R, a), sb("wo_lo_a", [P, 4, D], F32R, a)
            finish_attention(nc, ctx, k, "fa", 4, k.sel_bf[:, 0:4, :])

        with ExitStack() as b:
            k.aw0, k.aw1 = sb("aw0", [P, NH, P], F32, b), sb("aw1", [P, NH, P], F32R, b)
            k.w_vo = sb("w_vo", [P, NH // 2, D], F32, b)
            k.cp0, k.cp1, k.cp1_lo = sb("cp0", [P, S], F32, b), sb("cp1", [P, S], F32R, b), sb("cp1_lo", [P, S], F32R, b)
            k.k_hl = sb("k_hl", [P, 2, S], F32R, b)
            k.k_hi, k.k_lo = k.k_hl[:, 0, :], k.k_hl[:, 1, :]
            k.c_tok = sb("c_tok", [P, NT, KVL], F32, b)
            k.cos, k.sin = sb("cos", [P, S], F32, b), sb("sin", [P, S], F32, b)
            k.row = sb("row", [P, D], F32, b)
            with ExitStack() as w:
                k.w_ob = sb("w_ob", [P, NH, D], F32, w)
                k.w_qc = sb("w_qc", [P, 2, NH * DK], F32, w)
                k.w_kc, k.w_v = sb("w_kc", [KVL, NH * DK], F32, w), sb("w_v", [KVL, NH * DV], F32, w)
                k.w_cp = sb("w_cp", [P, KO, QL + QL2], F32, w)
                k.w_ck = sb("w_ck", [P, KO, P], F32, w)
                k.w_kr = sb("w_kr", [P, KO, DR], F32, w)
                with ExitStack() as f:
                    k.w_qr = sb("w_qr", [P, 2, NH * DR], F32, f)
                    alloc_ffn(k, lambda n, sh, dt=F32: sb(n + "_1", sh, dt, f))
                    ffn(nc, ctx, k, "f1", beside=LoadB(ctx, nc, k, io))
                J = IH * TOPK
                k.xT = sb("xT_b", [P, KO, S], F32, w)
                k.wT = sb("wT", [P, 8, QL + QL2 + 2 * KVL], F32, w)
                k.kraw, k.key, k.kswp = (sb(n, [P, S], F32, w) for n in ("kraw", "key", "kswp"))
                k.w_gate, k.w_idx, k.w_s = (sb("w_gate", [P, KO, IH], F32, w), sb("w_idx", [P, KO, IH * P], F32, w),
                                            sb("w_s", [P, 4, P], F32, w))
                k.small = sb("small", [P, 24 + J], F32, w)
                k.gT, k.top, k.top_at = sb("gT", [IH, S], F32, w), sb("top", [IH, 8], F32, w), sb("top_at", [IH, 8], mybir.dt.uint32, w)
                k.bd, k.onehot, k.xsel = sb("bd", [IH, IH, TOPK], F32, w), sb("onehot", [P, NT, J], F32, w), sb("xsel", [P, KO, J], F32, w)
                k.sel, k.sqk, k.sv = sb("sel", [P, J], F32, w), sb("sqk", [P, 2 * J], F32, w), sb("sv", [J, P], F32, w)
                k.sprob, k.scol, k.chain = sb("sprob", [J, J], F32, w), sb("scol", [P, 4], F32, w), sb("chain", [P, 24], F32, w)
                prepare_b(nc, ctx, k, io)
            k.qraw = k.xn[:, :, :].rearrange("p a b -> p (a b)").rearrange("p (a b) -> p a b", a=2)
            k.oT = sb("oT_b", [P, NH // 2, S], F32, b)
            with ExitStack() as w:
                k.swp = sb("swp", [P, 2, S], F32, w)
                k.q1 = sb("q1", [P, 2, S], F32, w)
                k.q_hl = sb("q_hl", [P, 2, 2, 2, S], F32R, w)
                k.prob = sb("prob_b", [P, 3, S], F32, w)
                k.pT = sb("pT_b", [P, 2, 2, S], F32, w)
                attend_b(nc, ctx, k)
            k.w_out = k.w_vo
            k.o_hi, k.o_lo = sb("o_hi_b", [P, 8, S], F32R, b), sb("o_lo_b", [P, 8, S], F32R, b)
            k.row_all = sb("row_all", [P, D], F32, b)
            k.wo_hi = sb("wo_hi_b", [P, 8, D], F32R, b)
            k.wo_lo = k.k_hl[:, :, :].rearrange("p a b -> p (a b)").rearrange("p (a b) -> p a b", a=8)
            finish_attention(nc, ctx, k, "fb", NH // 2, k.sel_bf[:, 4:12, :], row=k.row[:, :])

        with ExitStack() as f:
            alloc_ffn(k, lambda n, sh, dt=F32: sb(n + "_2", sh, dt, f))
            ffn(nc, ctx, k, "f2", out)


def alloc_ffn(k, sb):
    k.xqT = sb("xqT", [P, 3, 2, KO, P], F32R)
    k.h = sb("h", [P, 2, FF])
    k.hc = sb("hc", [P, 2, FF])
    k.hT = sb("hT", [P, 2, 2, FO, P], F32R)
    k.o_raw = sb("o_raw", [P, NT, D])
    k.nmean, k.hsum, k.hsq = (sb(n, [P, NT]) for n in ("nmean", "hsum", "hsq"))
    k.xbig, k.warm = sb("xbig", [P, NT, 2]), sb("warm", [P, 1])


def constants():
    c = {"ident": np.eye(P, dtype=np.float32)}
    q, kk = np.arange(P)[:, None], np.arange(P)[None, :]
    c["mask"] = np.where(kk > q, np.float32(-1e30), np.float32(0)).astype(np.float32)
    cols = np.zeros((P, 8), np.float32)
    odd = (np.arange(P) // HD) % 2
    cols[:, 0], cols[:, 1] = odd, 1 - 2 * odd
    for j in range(4):
        cols[32 * j:32 * j + 32, 4 + j] = 1
    c["cols"] = cols
    sel = np.zeros((96, 12, P), np.float32)
    for part in range(3):
        for h in range(NH):
            sel[32 * part + h, h // 4, 32 * (h % 4):32 * (h % 4) + 32] = 1
            sel[32 * part + h, 4 + h // 2, KVL * (h % 2):KVL * (h % 2 + 1)] = 1
    c["sel"] = sel
    inv = 1.0 / 10000.0 ** (np.arange(0, DR, 2)[:DR // 2].astype(np.float32) / DR)
    freqs = np.outer(np.arange(S, dtype=np.float32), inv)
    root = (DK + DR) ** -0.25
    cos, sin = np.cos(freqs).T, np.sin(freqs).T
    c["cos"] = (np.concatenate([np.ones((KVL, S)), cos, cos]) * root).astype(np.float32)
    c["sin"] = (np.concatenate([np.zeros((KVL, S)), -sin, sin]) * root).astype(np.float32)
    J = IH * TOPK
    small = np.zeros((P, 24 + J), np.float32)
    small[:IH, :IH] = np.eye(IH)
    small[:J, 8:16] = np.repeat(np.eye(IH), TOPK, axis=0) / TOPK
    small[:, 16:24] = np.arange(S).reshape(NT, P).T
    head = np.arange(J) // TOPK
    small[:J, 24:] = np.where(head[:, None] == head[None, :], 0, np.float32(-1e30))
    c["small"] = small
    return c


_INS = ["L0_attn_a_x", "L0_attn_a_Wqkv", "L0_attn_a_Wo", "L0_attn_b_W_c", "L0_attn_b_W_cp", "L0_attn_b_W_qc",
        "L0_attn_b_W_qr", "L0_attn_b_W_kc", "L0_attn_b_W_kr", "L0_attn_b_W_v", "L0_attn_b_W_o", "L0_attn_b_W_idx",
        "L0_attn_b_W_gate", "L0_attn_b_W_sq", "L0_attn_b_W_sk", "L0_attn_b_W_sv", "L0_attn_b_W_iout",
        "L0_ffn_w_fc", "L0_ffn_w_proj"]


def kernel(**inputs):
    import numpy as _np
    import concourse.bacc as _bacc
    from concourse import mybir as _mybir
    from concourse.bass_utils import run_bass_kernel_spmd as _run

    nc = _bacc.Bacc("TRN2", target_bir_lowering=False, num_devices=1)
    arrays, io = {}, {}
    for name, a in [(n, _np.ascontiguousarray(inputs[n])) for n in _INS] + list(constants().items()):
        arrays[f"in_{name}"] = a
        io[name] = nc.dram_tensor(f"in_{name}", a.shape, _mybir.dt.from_np(a.dtype), kind="ExternalInput").ap()
    out = nc.dram_tensor("out", (1, S, D), F32, kind="ExternalOutput").ap()
    build(nc, io, out)
    r = _run(nc, [arrays], core_ids=[0])
    return r.results[0]["out"]
```
